# Optimizing a Trainium2 kernel written in Bass

```python
import numpy as np
import jax
import jax.numpy as jnp

def _softmax(x, axis=-1):
    return jax.nn.softmax(x, axis=axis)

def _gelu(x):
    return jax.nn.gelu(x, approximate=True)

def _silu(x):
    return jax.nn.silu(x)

def _sigmoid(x):
    return jax.nn.sigmoid(x)

def _layernorm(x, axis=-1, eps=1e-05):
    m = jnp.mean(x, axis=axis, keepdims=True)
    v = jnp.var(x, axis=axis, keepdims=True)
    return (x - m) / jnp.sqrt(v + eps)

def _scatter_add(tgt, idx, src, axis=0):
    return tgt.at[idx].add(src)

def _segment_sum(src, seg, n):
    return jax.ops.segment_sum(src, seg, n)
kernel_name = 'mk_audio_tower_d1_tok_audfeat512_r4_856cc3'

def setup_inputs(seed: int=0):
    np.random.seed(seed)
    _w = jnp.asarray

    def _rec_inputs():
        import jax
        import jax.numpy as jnp
        _rk = jax.random.key(seed)
        x = -7.10856e-05 + 0.999911 * jax.random.normal(jax.random.fold_in(_rk, 1), (16, 750, 128), jnp.float32)
        return x
    x = _rec_inputs()

    def _L0_tok_setup():
        import jax, jax.numpy as jnp
        import numpy as np
        P = 2
        key = jax.random.key(seed)
        k1, k2 = jax.random.split(key)
        B, N, D = (32, 1024, 128)
        x = jax.random.normal(k1, (B, N, D), dtype=jnp.float32)
        stdv = 1.0 / np.sqrt(D)
        weight1 = jax.random.uniform(k2, (P, D), minval=-stdv, maxval=stdv, dtype=jnp.float32)
        return {'x': x, 'weight1': weight1}
    _L0_tok_all = _L0_tok_setup()
    _L0_tok_in = {k: v for k, v in _L0_tok_all.items() if k in ('weight1',)}
    del _L0_tok_all

    def _L0_attn_setup():
        import jax, jax.numpy as jnp
        import numpy as np
        GROUPS = 8
        EPS = 0.001

        def group_norm(x, gamma, beta):
            B, L, C = x.shape
            xg = x.reshape(B, L, GROUPS, C // GROUPS)
            mean = jnp.mean(xg, axis=(1, 3), keepdims=True)
            var = jnp.var(xg, axis=(1, 3), keepdims=True)
            xn = ((xg - mean) * jax.lax.rsqrt(var + EPS)).reshape(B, L, C)
            return xn * gamma + beta
        key = jax.random.key(seed)
        ks = jax.random.split(key, 6)
        B, L, C = (8, 512, 128)
        x = jax.random.normal(ks[0], (B, L, C), dtype=jnp.float32)
        s = 0.02
        return {'x': x, 'gamma': jnp.ones((C,), jnp.float32), 'beta': jnp.zeros((C,), jnp.float32), 'wq': jax.random.normal(ks[1], (C, C), jnp.float32) * s, 'bq': jnp.zeros((C,), jnp.float32), 'wk': jax.random.normal(ks[2], (C, C), jnp.float32) * s, 'bk': jnp.zeros((C,), jnp.float32), 'wv': jax.random.normal(ks[3], (C, C), jnp.float32) * s, 'bv': jnp.zeros((C,), jnp.float32), 'wp': jax.random.normal(ks[4], (C, C), jnp.float32) * s, 'bp': jnp.zeros((C,), jnp.float32)}
    _L0_attn_all = _L0_attn_setup()
    _L0_attn_in = {k: v for k, v in _L0_attn_all.items() if k in ('gamma', 'beta', 'wq', 'bq', 'wk', 'bk', 'wv', 'bv', 'wp', 'bp')}
    del _L0_attn_all

    def _L0_ffn_setup():
        import jax, jax.numpy as jnp
        import numpy as np
        B, S, D = (4, 512, 128)
        I = 96
        E = 16
        K = 2

        def _inv_softplus(v):
            return float(np.log(np.expm1(v)))

        def swiglu5(h, alpha, gate_scale, up_shift, gate_clamp_raw, up_clamp_raw):
            gate_clamp = jax.nn.softplus(gate_clamp_raw)
            up_clamp = jax.nn.softplus(up_clamp_raw)
            g = jnp.clip(h[..., ::2], -gate_clamp, gate_clamp)
            u = jnp.clip(h[..., 1::2], -up_clamp, up_clamp)
            return g * jax.nn.sigmoid(g * alpha) * gate_scale * (u + up_shift)
        key = jax.random.key(seed)
        ks = jax.random.split(key, 10)
        std = 0.02
        raw = _inv_softplus(7.0)
        act = jnp.array([1.702, 1.0, 1.0, raw, raw], dtype=jnp.float32)
        return {'x': jax.random.normal(ks[0], (B, S, D), dtype=jnp.float32), 'gate_w': jax.random.normal(ks[1], (D, E), dtype=jnp.float32) * 0.01, 'gate_b': jnp.zeros((E,), dtype=jnp.float32), 'shared_w1': jax.random.normal(ks[2], (D, 2 * I), dtype=jnp.float32) * std, 'shared_b1': jnp.zeros((2 * I,), dtype=jnp.float32), 'shared_w2': jax.random.normal(ks[3], (I, D), dtype=jnp.float32) * std, 'shared_b2': jnp.zeros((D,), dtype=jnp.float32), 'shared_act': act, 'expert_w1': jax.random.normal(ks[4], (E, D, 2 * I), dtype=jnp.float32) * std, 'expert_b1': jnp.zeros((E, 2 * I), dtype=jnp.float32), 'expert_w2': jax.random.normal(ks[5], (E, I, D), dtype=jnp.float32) * std, 'expert_b2': jnp.zeros((E, D), dtype=jnp.float32), 'expert_act': jnp.tile(act[None, :], (E, 1))}
    _L0_ffn_all = _L0_ffn_setup()
    _L0_ffn_in = {k: v for k, v in _L0_ffn_all.items() if k in ('gate_w', 'gate_b', 'shared_w1', 'shared_b1', 'shared_w2', 'shared_b2', 'shared_act', 'expert_w1', 'expert_b1', 'expert_w2', 'expert_b2', 'expert_act')}
    del _L0_ffn_all
    return {'x': x, 'L0_tok_weight1': _L0_tok_in['weight1'], 'L0_attn_gamma': _L0_attn_in['gamma'], 'L0_attn_beta': _L0_attn_in['beta'], 'L0_attn_wq': _L0_attn_in['wq'], 'L0_attn_bq': _L0_attn_in['bq'], 'L0_attn_wk': _L0_attn_in['wk'], 'L0_attn_bk': _L0_attn_in['bk'], 'L0_attn_wv': _L0_attn_in['wv'], 'L0_attn_bv': _L0_attn_in['bv'], 'L0_attn_wp': _L0_attn_in['wp'], 'L0_attn_bp': _L0_attn_in['bp'], 'L0_ffn_gate_w': _L0_ffn_in['gate_w'], 'L0_ffn_gate_b': _L0_ffn_in['gate_b'], 'L0_ffn_shared_w1': _L0_ffn_in['shared_w1'], 'L0_ffn_shared_b1': _L0_ffn_in['shared_b1'], 'L0_ffn_shared_w2': _L0_ffn_in['shared_w2'], 'L0_ffn_shared_b2': _L0_ffn_in['shared_b2'], 'L0_ffn_shared_act': _L0_ffn_in['shared_act'], 'L0_ffn_expert_w1': _L0_ffn_in['expert_w1'], 'L0_ffn_expert_b1': _L0_ffn_in['expert_b1'], 'L0_ffn_expert_w2': _L0_ffn_in['expert_w2'], 'L0_ffn_expert_b2': _L0_ffn_in['expert_b2'], 'L0_ffn_expert_act': _L0_ffn_in['expert_act']}

def reference(x, L0_tok_weight1, L0_attn_gamma, L0_attn_beta, L0_attn_wq, L0_attn_bq, L0_attn_wk, L0_attn_bk, L0_attn_wv, L0_attn_bv, L0_attn_wp, L0_attn_bp, L0_ffn_gate_w, L0_ffn_gate_b, L0_ffn_shared_w1, L0_ffn_shared_b1, L0_ffn_shared_w2, L0_ffn_shared_b2, L0_ffn_shared_act, L0_ffn_expert_w1, L0_ffn_expert_b1, L0_ffn_expert_w2, L0_ffn_expert_b2, L0_ffn_expert_act):
    import jax
    import jax.numpy as jnp

    def _L0_tok_ref(x, weight1):
        import jax, jax.numpy as jnp
        import numpy as np
        P = 2
        B, N, D = x.shape
        p = weight1.shape[0]
        steps = -(-N // p)
        pad = steps * p - N
        if pad:
            x = jnp.pad(x, ((0, 0), (0, pad), (0, 0)))
        xw = x.reshape(B, steps, p, D)
        return jnp.einsum('bspd,pd->bsd', xw, weight1)

    def _L0_attn_ref(x, gamma, beta, wq, bq, wk, bk, wv, bv, wp, bp):
        import jax, jax.numpy as jnp
        import numpy as np
        GROUPS = 8
        EPS = 0.001

        def group_norm(x, gamma, beta):
            B, L, C = x.shape
            xg = x.reshape(B, L, GROUPS, C // GROUPS)
            mean = jnp.mean(xg, axis=(1, 3), keepdims=True)
            var = jnp.var(xg, axis=(1, 3), keepdims=True)
            xn = ((xg - mean) * jax.lax.rsqrt(var + EPS)).reshape(B, L, C)
            return xn * gamma + beta
        C = x.shape[-1]
        scale = jnp.float32(C) ** (-0.5)
        h = group_norm(x, gamma, beta)
        q = h @ wq + bq
        k = h @ wk + bk
        v = h @ wv + bv
        attn = jnp.einsum('blc,bLc->blL', q, k) * scale
        attn = jax.nn.softmax(attn, axis=-1)
        o = jnp.einsum('blL,bLc->blc', attn, v)
        o = o @ wp + bp
        return h + o

    def _L0_ffn_ref(x, gate_w, gate_b, shared_w1, shared_b1, shared_w2, shared_b2, shared_act, expert_w1, expert_b1, expert_w2, expert_b2, expert_act):
        import jax, jax.numpy as jnp
        import numpy as np
        B, S, D = (4, 512, 128)
        I = 96
        E = 16
        K = 2

        def _inv_softplus(v):
            return float(np.log(np.expm1(v)))

        def swiglu5(h, alpha, gate_scale, up_shift, gate_clamp_raw, up_clamp_raw):
            gate_clamp = jax.nn.softplus(gate_clamp_raw)
            up_clamp = jax.nn.softplus(up_clamp_raw)
            g = jnp.clip(h[..., ::2], -gate_clamp, gate_clamp)
            u = jnp.clip(h[..., 1::2], -up_clamp, up_clamp)
            return g * jax.nn.sigmoid(g * alpha) * gate_scale * (u + up_shift)
        shape = x.shape
        xf = x.reshape(-1, shape[-1])
        h = xf @ shared_w1 + shared_b1
        t = swiglu5(h, shared_act[0], shared_act[1], shared_act[2], shared_act[3], shared_act[4])
        z = t @ shared_w2 + shared_b2
        gate_logits = xf @ gate_w + gate_b
        gate_probs = jax.nn.softmax(gate_logits, -1)
        w, idx = jax.lax.top_k(gate_probs, K)
        w = w / jnp.sum(w, axis=-1, keepdims=True)
        cw = jnp.sum(jax.nn.one_hot(idx, E, dtype=xf.dtype) * w[..., None], axis=1)
        he = jnp.einsum('nd,edh->enh', xf, expert_w1) + expert_b1[:, None, :]
        a = expert_act
        te = swiglu5(he, a[:, 0, None, None], a[:, 1, None, None], a[:, 2, None, None], a[:, 3, None, None], a[:, 4, None, None])
        oe = jnp.einsum('enh,ehd->end', te, expert_w2) + expert_b2[:, None, :]
        y = jnp.einsum('ne,end->nd', cw, oe)
        return (y + z).reshape(shape)
    h = _L0_tok_ref(x, L0_tok_weight1)
    h = h + _L0_attn_ref(_layernorm(h, axis=-1), L0_attn_gamma, L0_attn_beta, L0_attn_wq, L0_attn_bq, L0_attn_wk, L0_attn_bk, L0_attn_wv, L0_attn_bv, L0_attn_wp, L0_attn_bp)
    h = h + _L0_ffn_ref(_layernorm(h, axis=-1), L0_ffn_gate_w, L0_ffn_gate_b, L0_ffn_shared_w1, L0_ffn_shared_b1, L0_ffn_shared_w2, L0_ffn_shared_b2, L0_ffn_shared_act, L0_ffn_expert_w1, L0_ffn_expert_b1, L0_ffn_expert_w2, L0_ffn_expert_b2, L0_ffn_expert_act)
    return h

_drawn_inputs = setup_inputs


def setup_inputs(seed=0):
    import zlib

    import numpy as np

    out = dict(_drawn_inputs(seed))
    spreads = {'L0_attn_gamma': (1.0, 0.2),
     'L0_attn_beta': (0.0, 0.1),
     'L0_attn_bq': (0.0, 0.8),
     'L0_attn_bk': (0.0, 0.8),
     'L0_attn_bv': (0.0, 0.376),
     'L0_attn_bp': (0.0, 0.1),
     'L0_ffn_gate_b': (0.0, 0.1),
     'L0_ffn_shared_b1': (0.0, 0.8),
     'L0_ffn_shared_b2': (0.0, 0.1),
     'L0_ffn_expert_b1': (0.0, 0.8),
     'L0_ffn_expert_b2': (0.0, 0.1)}
    factors = {'L0_attn_wq': 8.0,
     'L0_attn_wk': 8.0,
     'L0_attn_wv': 8.0,
     'L0_attn_wp': 2.959,
     'L0_ffn_shared_w1': 2.717,
     'L0_ffn_expert_w1': 3.803,
     'L0_ffn_expert_w2': 3.456}
    for name, (base, spread) in spreads.items():
        noise = np.random.default_rng([zlib.crc32(name.encode()), seed]).standard_normal(out[name].shape)
        drawn = base * np.exp(spread * noise) if base else spread * noise
        out[name] = jnp.asarray(drawn.astype(out[name].dtype))
    for name, factor in factors.items():
        out[name] = (out[name] * factor).astype(out[name].dtype)
    return out
```

```python
from contextlib import ExitStack

import concourse.bass as bass
from concourse import mybir

F32 = mybir.dt.float32
I32 = mybir.dt.int32
U32 = mybir.dt.uint32
BF16 = mybir.dt.bfloat16
ALU = mybir.AluOpType
ACT = mybir.ActivationFunctionType
AX = mybir.AxisListType.X

LN_EPS = 1e-5
GN_EPS = 1e-3
GN_GROUPS = 8
TOP_K = 2


class Turn:

    def __init__(self, c, m=None, step=1):
        self.first = c if m is None else None
        self.n = c if m is None else m * step + c
        self.parity, self.place = c % 2, c % 4
        self.half = c // 2 if m is None else m * (step // 2) + c // 2
        self.round = c // 4 if m is None else m * (step // 4) + c // 4

    def reuses(self, buffers):
        return self.first is None or self.first >= buffers


def wait_done(eng, sem, per_turn, n, lag=0):
    value = (n + (1 - lag)) * per_turn
    if not isinstance(value, int) or value > 0:
        eng.wait_ge(sem, value)


def hold(eng, held):
    eng.sem_inc(held, 1)


class Steps:

    def __init__(self, sem, per_turn):
        self.sem, self.per_turn = sem, per_turn

    def begin(self, eng, n):
        self.eng, self.n, self.k = eng, n, 0

    def did(self, ins):
        ins.then_inc(self.sem, 1)
        self.k += 1
        assert self.k <= self.per_turn

    def settle(self):
        self.eng.wait_ge(self.sem, self.n * self.per_turn + self.k)

    def end(self):
        assert self.k == self.per_turn, (self.k, self.per_turn)


def audio_tower(nc, a, out):
    x = a["x"]
    B, ROWS, D = x.shape
    POOL = a["L0_tok_weight1"].shape[0]
    L = ROWS // POOL
    J = 3
    P = L // J
    E = a["L0_ffn_gate_w"].shape[1]
    HID = a["L0_ffn_shared_w2"].shape[0]
    N = B * L
    SCALE = float(D) ** -0.5
    XROW = POOL * D
    GC = D // GN_GROUPS
    assert P * J == L and D == 128 and P <= 128

    TILE = 256
    HALVES = TILE // 128
    NT = (TOP_K * N + E * (TILE - 1)) // TILE
    CAP = N + TILE
    PAD_ROW = E * CAP
    ROW = D + 2
    DEST, WEIGHT = D, D + 1
    SKIP = 1 << 20

    W2 = 2 * HID
    COLS = W2 + D
    B_G, B_U, ALPHA2, SHIFT, GMAX, GMIN, UMAX, UMIN = range(COLS, COLS + 8)
    WP = COLS + 8

    with ExitStack() as ctx:
        def sb(name, shape, dt=F32):
            return ctx.enter_context(nc.sbuf_tensor(name, shape, dt))

        def sem(name):
            return ctx.enter_context(nc.semaphore(name))

        routed = nc.dram_tensor("routed", [E * CAP + TILE, ROW], F32, kind="Internal").ap()
        slots = nc.dram_tensor("slots", [TOP_K * N, D], F32, kind="Internal").ap()

        bank = [ctx.enter_context(nc.psum_tensor(f"bank{i}", [128, 512], F32)) for i in range(8)]

        ident = sb("ident", [128, 128])
        group_avg = sb("group_avg", [128, 128])
        before = sb("before", [128, 128], BF16)
        ones_bf = sb("ones_bf", [128, 128], BF16)
        iota_e = sb("iota_e", [128, E])
        base = sb("base", [128, E])
        base0 = sb("base0", [128, E])
        dest_id = sb("dest_id", [128, J * TOP_K], I32)
        eps = sb("eps", [128, 2])
        tile_no = sb("tile_no", [128, 1])
        wpool = sb("wpool", [128, XROW])
        gate_w = sb("gate_w", [128, E])
        gate_b = sb("gate_b", [128, E])
        wq = sb("wq", [128, D])
        wk = sb("wk", [128, D])
        wv = sb("wv", [128, D])
        wp = sb("wp", [128, D])
        wvT = sb("wvT", [128, D])
        wvp = sb("wvp", [128, D])
        vec = sb("vec", [128, 8])
        GAMMA, BETA, BQ, BK, BV, BP, BQS, BVP = range(8)
        pack = sb("pack", [128, (E + 1) * WP])
        b1 = sb("b1", [E + 1, W2])
        act_raw = sb("act_raw", [128, (E + 1) * 5])
        soft = sb("soft", [128, 4 * 2 * (E + 1)])
        pads = sb("pads", [128, HALVES * ROW])

        xin = sb("xin", [128, 2, J * XROW])
        xm = sb("xm", [128, 2, J * XROW])
        h0 = sb("h0", [128, 2, J * D])
        st1 = sb("st1", [128, 2, J * 6])
        mv1 = sb("mv1", [128, 2, J * 2])
        rs1 = sb("rs1", [128, 2, 2 * J])
        ln1 = sb("ln1", [128, 2, J * D])
        gst = sb("gst", [128, 2, 8])
        gsm = sb("gsm", [128, 2, 2])
        gco = sb("gco", [128, 2, 12])
        hT = sb("hT", [128, 2, L])
        hTc = sb("hTc", [128, 2, L])
        qT = sb("qT", [128, 2, L])
        kT = sb("kT", [128, 2, L])
        vs = sb("vs", [128, 2, J * D])
        nmax = sb("nmax", [128, 2, J])
        rsum = sb("rsum", [128, 2, J])
        rinv = sb("rinv", [128, 2, J])
        probs = sb("probs", [128, J, L])
        probsT = sb("probsT", [128, J, L])
        res = sb("res", [128, 2, J * D])
        h1 = sb("h1", [128, 2, J * D])
        st2 = sb("st2", [128, 2, J * 6])
        mv2 = sb("mv2", [128, 2, J * 2])
        rs2 = sb("rs2", [128, 2, 2 * J])
        xrow = sb("xrow", [128, 2, J * TOP_K * ROW])
        x2t = sb("x2t", [128, 2, L])
        lg = sb("lg", [128, J * E])
        mx = sb("mx", [128, J * 8])
        ix = sb("ix", [128, J * 8], U32)
        ixf = sb("ixf", [128, J * TOP_K])
        gap = sb("gap", [128, 2, 4 * J])
        hot = sb("hot", [128, J * TOP_K * E])
        mask = sb("mask", [128, 2, J * E], BF16)
        posall = sb("posall", [128, J * E])
        posm = sb("posm", [128, J * TOP_K * E])
        posf = sb("posf", [128, J * TOP_K])
        pos = sb("pos", [128, 2, J * TOP_K], I32)

        H1 = sb("H1", [128, B * J * D])
        X2T = sb("X2T", [128, B * L])

        tab = sb("tab", [128, 16 * E])
        tabi = sb("tabi", [128, 2 * E], I32)
        where = sb("where", [1, 2 * 128 + E], I32)
        xs = sb("xs", [128, 4, HALVES * ROW])
        xt = sb("xt", [128, 2, TILE])
        wt = sb("wt", [128, 2, WP])
        hg = sb("hg", [128, 2, L])
        hu = sb("hu", [128, 2, L])
        th = sb("th", [128, 2, L])
        ga = sb("ga", [128, 2, L])
        tt = sb("tt", [128, 2, L])
        ys = sb("ys", [128, 4, HALVES * D])
        z0 = sb("z0", [128, 2, J * D])
        z1 = sb("z1", [128, 2, J * D])
        fin = sb("fin", [128, 2, J * D])

        s_const = sem("const_ready")
        s_clear = sem("pack_cleared")
        s_held_dve = sem("held_dve")
        s_held_pool = sem("held_pool")
        s_params = sem("params_loaded")
        s_expw = sem("expert_weights_loaded")
        s_setup_pe = sem("setup_products")
        setup_dve = Steps(sem("setup_dve_steps"), 17)
        s_soft = sem("softplus_tail")
        s_x = [sem(f"x_loaded{q}") for q in range(2)]
        s_mul = sem("pool_products")
        s_h0 = sem("pooled")
        ln1_stats = Steps(sem("ln1_stats"), 2 * J)
        ln1_rstd = Steps(sem("ln1_rstd"), 2)
        s_ln1 = sem("ln1_applied")
        s_lnT = sem("ln1_transposed")
        gn_stats = Steps(sem("gn_channel_stats"), 3)
        s_group = sem("gn_group_means")
        gn_var = Steps(sem("gn_variance"), 2)
        gn_rstd = Steps(sem("gn_rstd"), 2)
        gn_coef = Steps(sem("gn_coefficients"), 4)
        s_hT = sem("h_ready")
        s_hTc = sem("h_with_offset_ready")
        s_q = sem("q_product")
        s_k = sem("k_product")
        s_v = sem("v_product")
        s_qkv = sem("qkv_in_sbuf")
        s_S = sem("scores")
        s_nmax = sem("row_maxima")
        s_exp = sem("probabilities")
        s_PT = sem("probabilities_transposed")
        s_PTe = sem("transposed_in_sbuf_even")
        s_PTo = sem("transposed_in_sbuf_odd")
        s_O = sem("attention_out")
        s_hback = sem("h_token_major")
        s_res = sem("residual_ready")
        s_rinv = sem("row_sums_inverted")
        s_h1 = sem("h1_ready")
        s_h1kept = [sem(f"h1_kept{q}") for q in range(2)]
        ln2_stats = Steps(sem("ln2_stats"), 2 * J)
        ln2_rstd = Steps(sem("ln2_rstd"), 2)
        s_ln2 = sem("ln2_applied")
        s_copy2 = sem("second_row_copied")
        s_x2T = sem("x2_transposed")
        s_x2t = sem("x2T_in_sbuf")
        s_x2kept = [sem(f"x2T_kept{q}") for q in range(2)]
        s_gate = sem("gate_logits")
        topk = Steps(sem("topk_steps"), 3 + 2 * J)
        s_gap = sem("second_weight_exp")
        topw = Steps(sem("top_weights_and_mask"), 5)
        s_rank = sem("ranks")
        place = Steps(sem("places"), 5)
        ids = Steps(sem("dest_ids_written"), 2)
        s_scat = [sem(f"rows_scattered{q}") for q in range(2)]

        table = Steps(sem("tile_table"), 25)
        s_row = sem("tile_table_row")
        s_pad = sem("pad_rows_written")
        s_sh_h = sem("shared_hidden")
        s_sh_b = sem("shared_biased")
        s_sh_c = sem("shared_clipped")
        s_sh_t = sem("shared_tanh")
        s_sh_g = sem("shared_gated")
        s_sh_tt = sem("shared_activated")
        s_sh_z = sem("shared_out")
        s_sh_add = sem("shared_added")
        s_xs = [sem(f"tile_loaded{q}") for q in range(4)]
        s_wt = sem("tile_weights")
        s_xT = sem("tile_transposed")
        s_xt = sem("tile_x_in_sbuf")
        s_hid = sem("tile_hidden")
        s_bias = sem("tile_biased")
        s_clip = sem("tile_clipped")
        s_tanh = sem("tile_tanh")
        s_gated = sem("tile_gated")
        s_act = sem("tile_activated")
        s_y = sem("tile_out")
        s_ys = sem("tile_weighted")
        s_back = [sem(f"tile_scattered{q}") for q in range(4)]
        s_z = [sem(f"slots_loaded{q}") for q in range(2)]
        s_zz = sem("slots_added")
        s_fin = sem("result_ready")
        s_out = [sem(f"stored{q}") for q in range(2)]

        def cols(t, b):
            return t[:, b.parity, :]

        psF, psO = bank[0], bank[0]
        psQ, psK, psV = bank[1], bank[2], bank[3]
        psG = bank[1][:, 0:2]
        psL = bank[2][:, 0:J * E]
        psR = bank[1][:, 0:J * E]
        psTot = bank[1][:, J * E:(J + 1) * E]
        psS = [bank[4], bank[5]]

        def score_bank(m, j):
            return psS[(m.parity * J + j) % 2]

        psPT = [bank[6], bank[7]]
        psX, psH = bank[6], bank[7]
        where_row = bank[0][0:1, 0:128]
        where_exp = bank[0][0:1, 128:256]


        N_CONST = 19
        N_PARAMS = 13
        N_EXPW = 10
        SETUP_ABS = 3
        TABLE_COLUMNS = 24
        CL = 2 * (E + 1)
        shared_pack = pack[:, E * WP:(E + 1) * WP]

        def w1_of(w, two):
            return w[:, 0:W2].rearrange("d (i two) -> d two i", two=2)[:, two, :]

        def psHid(t, two):
            return bank[2 + t.parity][0:HID, two * TILE:(two + 1) * TILE]

        def attention_iterations(eng, body):
            lo, hi = 4, B - 2

            def edge(i):
                body(*(Turn(n) if 0 <= n < B else None for n in (i + 2, i + 1, i, i - 1)))

            for i in range(-2, lo):
                edge(i)
            with eng.Fori(0, (hi - lo) // 2) as m:
                for i in (lo, lo + 1):
                    body(*(Turn(n, m, 2) for n in (i + 2, i + 1, i, i - 1)))
            for i in range(hi, B + 1):
                edge(i)

        def shared_iterations(eng, body):
            def edge(i):
                body(*(Turn(n) if 0 <= n < B else None for n in (i, i - 1)))

            for i in range(0, 4):
                edge(i)
            with eng.Fori(0, (B - 4) // 2) as m:
                for i in (4, 5):
                    body(*(Turn(n, m, 2) for n in (i, i - 1)))
            edge(B)

        def tile_iterations(eng, body):
            lo = 3
            loops = (NT - 1 - lo) // 4

            def edge(i):
                body(*(Turn(n) if 0 <= n < NT else None for n in (i + 1, i, i - 1)))

            for i in range(-1, lo):
                edge(i)
            with eng.Fori(0, loops) as m:
                for i in range(lo, lo + 4):
                    body(*(Turn(n, m, 4) for n in (i + 1, i, i - 1)))
            for i in range(lo + 4 * loops, NT + 1):
                edge(i)

        def batches(eng, body):
            for n in range(2):
                body(Turn(n))
            with eng.Fori(0, (B - 2) // 2) as m:
                for n in (2, 3):
                    body(Turn(n, m, 2))

        block = ctx.enter_context(nc.Block())

        @block.sync
        def _(sp):
            sp.dma_start(wpool[0:P, :], a["L0_tok_weight1"].rearrange("(o p) d -> o (p d)", o=1).broadcast_to([P, XROW])).then_inc(s_params, 16)
            for t, name in ((wq, "wq"), (wk, "wk"), (wv, "wv"), (wp, "wp")):
                sp.dma_start(t[:], a["L0_attn_" + name]).then_inc(s_params, 16)
            for c, name in ((GAMMA, "gamma"), (BETA, "beta"), (BQ, "bq"), (BK, "bk"), (BV, "bv"), (BP, "bp")):
                sp.dma_start(vec[:, c:c + 1], a["L0_attn_" + name].rearrange("(d o) -> d o", o=1)).then_inc(s_params, 16)
            sp.dma_start(gate_w[:], a["L0_ffn_gate_w"]).then_inc(s_params, 16)
            sp.dma_start(gate_b[:], a["L0_ffn_gate_b"].rearrange("(o e) -> o e", o=1).broadcast_to([128, E])).then_inc(s_params, 16)

            def load_x(b):
                wait_done(sp, s_mul, 1, b.n, 2)
                sp.dma_start(xin[0:P, b.parity, :], x[bass.ds(b.n, 1)].rearrange("o (p r) d -> p (o r d)", p=P)).then_inc(s_x[b.parity], 16)

            def keep(e, f, m, k):
                if e:
                    load_x(e)
                if k:
                    wait_done(sp, s_x2t, 1, k.n)
                    sp.dma_start(X2T[:, bass.ds(k.n * L, L)], cols(x2t, k)).then_inc(s_x2kept[k.parity], 16)
                if m:
                    wait_done(sp, s_h1, J, m.n)
                    sp.dma_start(H1[0:P, bass.ds(m.n * (J * D), J * D)], h1[0:P, m.parity, :]).then_inc(s_h1kept[m.parity], 16)

            attention_iterations(sp, keep)

            wait_done(sp, table.sem, table.per_turn, 0)
            for e in range(E):
                r = sp.value_load(where[0:1, 256 + e:257 + e], min_val=0, max_val=E * CAP - TILE)
                sp.dma_start(routed[bass.ds(r, TILE), :].rearrange("(p h) c -> p (h c)", h=HALVES), pads[:]).then_inc(s_pad, 16)
            sp.dma_start(routed[PAD_ROW:PAD_ROW + TILE, :].rearrange("(p h) c -> p (h c)", h=HALVES), pads[:]).then_inc(s_pad, 16)
            sp.wait_ge(s_pad, 16 * (E + 1))
            for q in range(2):
                sp.wait_ge(s_scat[q], 16 * J * TOP_K * (B // 2))

            def load_tile(nxt, cur, prev):
                if nxt:
                    if nxt.reuses(4):
                        sp.wait_ge(s_back[nxt.place], nxt.round * (16 * HALVES))
                    r = sp.value_load(where[0:1, bass.ds(nxt.n, 1)], min_val=0, max_val=PAD_ROW)
                    sp.dma_start(xs[:, nxt.place, :], routed[bass.ds(r, TILE), :].rearrange("(p h) c -> p (h c)", h=HALVES)).then_inc(s_xs[nxt.place], 16)

            tile_iterations(sp, load_tile)
            for q in range(4):
                sp.wait_ge(s_back[q], 16 * HALVES * len(range(q, NT, 4)))

            def load_slots(b):
                wait_done(sp, s_fin, 1, b.n, 2)
                sp.dma_start(z0[0:P, b.parity, :], slots[bass.ds(b.n * L, L), :].rearrange("(p j) d -> p (j d)", p=P)).then_inc(s_z[b.parity], 16)
                sp.dma_start(z1[0:P, b.parity, :], slots[bass.ds(b.n * L + N, L), :].rearrange("(p j) d -> p (j d)", p=P)).then_inc(s_z[b.parity], 16)

            batches(sp, load_slots)

        @block.gpsimd
        def _(pool):
            pp = pack[:].rearrange("p (e c) -> p e c", c=WP)
            pool.memset(pp[HID:128, :, W2:COLS], 0.0).then_inc(s_clear, 1)
            pool.memset(pp[HID:128, :, B_G:B_U + 1], 0.0).then_inc(s_clear, 1)
            pool.wait_ge(s_clear, 2)
            pool.memset(ident[:], 0.0).then_inc(s_const, 1)
            pool.memset(group_avg[:], 1.0 / GC).then_inc(s_const, 1)
            pool.memset(before[:], 1.0).then_inc(s_const, 1)
            pool.memset(ones_bf[:], 1.0).then_inc(s_const, 1)
            pool.memset(eps[:, 0:1], LN_EPS).then_inc(s_const, 1)
            pool.memset(eps[:, 1:2], GN_EPS).then_inc(s_const, 1)
            pool.memset(pads[:], 0.0).then_inc(s_const, 1)
            pool.memset(tt[:], 1.0).then_inc(s_const, 1)
            pool.iota(iota_e[:], pattern=[[1, E]], base=0, channel_multiplier=0, allow_small_or_imprecise_dtypes=True).then_inc(s_const, 1)
            pool.iota(base0[:], pattern=[[CAP, E]], base=0, channel_multiplier=0, allow_small_or_imprecise_dtypes=True).then_inc(s_const, 1)
            pool.iota(tile_no[:], pattern=[[0, 1]], base=0, channel_multiplier=1, allow_small_or_imprecise_dtypes=True).then_inc(s_const, 1)
            pool.iota(dest_id[:].rearrange("p (j k) -> p j k", k=TOP_K), pattern=[[1, J], [N, TOP_K]], base=0, channel_multiplier=J).then_inc(s_const, 1)
            pool.wait_ge(s_const, 12)
            pool.tensor_copy(base[:], base0[:]).then_inc(s_const, 1)
            for h in range(HALVES):
                pool.memset(pads[:, h * ROW + DEST:h * ROW + DEST + 1].bitcast(I32), SKIP).then_inc(s_const, 1)
            pool.affine_select(out=ident[:], in_=ident[:], compare_op=ALU.not_equal, fill=1.0, base=0,
                               pattern=[[-1, 128]], channel_multiplier=1).then_inc(s_const, 1)
            pool.affine_select(out=before[:], in_=before[:], compare_op=ALU.is_gt, fill=0.0, base=0,
                               pattern=[[1, 128]], channel_multiplier=-1).then_inc(s_const, 1)
            g3 = group_avg[:].rearrange("p (g c) -> p g c", c=GC)
            pool.affine_select(out=g3, in_=g3, compare_op=ALU.is_ge, fill=0.0, base=0,
                               pattern=[[-GC, GN_GROUPS], [0, GC]], channel_multiplier=1).then_inc(s_const, 1)
            pool.wait_ge(s_const, 18)
            pool.affine_select(out=g3, in_=g3, compare_op=ALU.is_ge, fill=0.0, base=GC - 1,
                               pattern=[[GC, GN_GROUPS], [0, GC]], channel_multiplier=-1).then_inc(s_const, 1)

            def rows_out(e, f, m, k):
                if e:
                    wait_done(pool, s_mul, 1, e.n)
                    wait_done(pool, s_res, 1, e.n, 2)
                    wait_done(pool, s_ln1, J, e.n, 2)
                    v = xm[0:P, e.parity, :].rearrange("p (j r d) -> p j r d", j=J, r=POOL)
                    pool.tensor_tensor(h0[0:P, e.parity, :].rearrange("p (j d) -> p j d", j=J), v[:, :, 0, :], v[:, :, 1, :], ALU.add).then_inc(s_h0, 1)
                if k:
                    ids.begin(pool, k.n)
                    if k.reuses(2):
                        pool.wait_ge(s_scat[k.parity], k.half * (16 * J * TOP_K))
                    wait_done(pool, ids.sem, ids.per_turn, k.n, 1)
                    rows = xrow[0:P, k.parity, :].rearrange("p (s c) -> p s c", c=ROW)
                    hold(pool, s_held_pool)
                    ids.did(pool.tensor_copy(rows[:, :, DEST].bitcast(I32), dest_id[0:P, :]))
                    ids.settle()
                    hold(pool, s_held_pool)
                    ids.did(pool.tensor_scalar(dest_id[0:P, :], dest_id[0:P, :], L, None, ALU.add))
                    ids.end()
                    wait_done(pool, s_ln2, J, k.n)
                    wait_done(pool, s_copy2, 1, k.n)
                    wait_done(pool, topw.sem, topw.per_turn, k.n)
                    wait_done(pool, place.sem, place.per_turn, k.n)
                    hold(pool, s_held_pool)
                    for s in range(J * TOP_K):
                        pool.indirect_dma_start(out=routed[:, :], out_offset=bass.IndirectOffsetOnAxis(ap=pos[0:P, k.parity, s:s + 1], axis=0),
                                                in_=xrow[0:P, k.parity, s * ROW:(s + 1) * ROW], in_offset=None).then_inc(s_scat[k.parity], 16)

            attention_iterations(pool, rows_out)

            def scatter_tile(nxt, cur, prev):
                if prev:
                    q = prev.place
                    wait_done(pool, s_ys, 1, prev.n)
                    hold(pool, s_held_pool)
                    for h in range(HALVES):
                        pool.indirect_dma_start(out=slots[:, :], out_offset=bass.IndirectOffsetOnAxis(ap=xs[:, q, h * ROW + DEST:h * ROW + DEST + 1].bitcast(I32), axis=0),
                                                in_=ys[:, q, h * D:(h + 1) * D], in_offset=None,
                                                bounds_check=TOP_K * N - 1, oob_is_err=False).then_inc(s_back[q], 16)

            tile_iterations(pool, scatter_tile)

            def add_slots(b):
                pool.wait_ge(s_z[b.parity], (b.half + 1) * 32)
                wait_done(pool, s_fin, 1, b.n, 2)
                pool.tensor_tensor(z0[0:P, b.parity, :], z0[0:P, b.parity, :], z1[0:P, b.parity, :], ALU.add).then_inc(s_zz, 1)

            batches(pool, add_slots)

        @block.tensor
        def _(pe):
            pe.wait_ge(s_const, N_CONST)
            pe.wait_ge(s_params, 16 * N_PARAMS)
            pe.transpose(bank[0][:, 0:D], wv[:], ident[:]).then_inc(s_setup_pe, 1)
            pe.wait_ge(setup_dve.sem, 1)
            pe.matmul(bank[1][:, 0:D], wvT[:], wp[:], start=True, stop=True)
            pe.matmul(bank[1][:, D:D + 1], wp[:], vec[:, BV:BV + 1], start=True, stop=True).then_inc(s_setup_pe, 1)
            pe.wait_ge(s_expw, 16 * N_EXPW)
            b1v = b1[:].rearrange("e (i two) -> e two i", two=2)
            for two in range(2):
                last = pe.transpose(bank[2][0:HID, two * 32:two * 32 + E + 1], b1v[:, two, :], ident[0:E + 1, 0:E + 1])
            last.then_inc(s_setup_pe, 1)
            pe.wait_ge(setup_dve.sem, setup_dve.per_turn)

            def body(e, f, m, k):
                if f:
                    wait_done(pe, s_ln1, J, f.n)
                    wait_done(pe, s_h1, J, f.n, 2)
                    for j in range(J):
                        last = pe.transpose(psF[:, j * P:(j + 1) * P], ln1[0:P, f.parity, j * D:(j + 1) * D], ident[0:P, 0:P])
                    last.then_inc(s_lnT, 1)
                if m:
                    for j in range(J):
                        if j == 0:
                            wait_done(pe, s_qkv, 3, m.n)
                        if j == J - 1:
                            if f:
                                wait_done(pe, gn_stats.sem, gn_stats.per_turn, f.n)
                                wait_done(pe, place.sem, place.per_turn, f.n, 3)
                                pe.matmul(psG, group_avg[:], gst[:, f.parity, 6:8], start=True, stop=True).then_inc(s_group, 1)
                        if m.reuses(1) or j >= 2:
                            pe.wait_ge(s_exp, m.n * J + (j - 1))
                        pe.matmul(score_bank(m, j)[0:P, 0:L], qT[:, m.parity, j * P:(j + 1) * P], cols(kT, m), start=True, stop=True).then_inc(s_S, 1)
                elif f:
                    wait_done(pe, gn_stats.sem, gn_stats.per_turn, f.n)
                    pe.matmul(psG, group_avg[:], gst[:, f.parity, 6:8], start=True, stop=True).then_inc(s_group, 1)
                if k:
                    wait_done(pe, s_ln2, J, k.n)
                    wait_done(pe, s_PTe, 2, k.n)
                    for j in range(J):
                        last = pe.transpose(psX[:, j * P:(j + 1) * P], xrow[0:P, k.parity, j * TOP_K * ROW:j * TOP_K * ROW + D], ident[0:P, 0:P])
                    last.then_inc(s_x2T, 1)
                if m:
                    wait_done(pe, s_hTc, 1, m.n)
                    wait_done(pe, s_PTo, 1, m.n, 1)
                    for j in range(J):
                        last = pe.transpose(psH[0:P, j * D:(j + 1) * D], hTc[:, m.parity, j * P:(j + 1) * P], ident[:])
                    last.then_inc(s_hback, 1)
                if k:
                    wait_done(pe, s_x2t, 1, k.n)
                    wait_done(pe, topk.sem, topk.per_turn, k.n, 1)
                    for j in range(J):
                        last = pe.matmul(psL[0:P, j * E:(j + 1) * E], x2t[:, k.parity, j * P:(j + 1) * P], gate_w[:], start=True, stop=True)
                    last.then_inc(s_gate, 1)
                if f:
                    wait_done(pe, s_hT, 1, f.n)
                    wait_done(pe, s_qkv, 3, f.n, 1)
                    pe.matmul(psQ[:, 0:L], wq[:], cols(hT, f), start=True, stop=True).then_inc(s_q, 1)
                    if k:
                        pe.wait_ge(topk.sem, k.n * topk.per_turn + 1)
                    pe.matmul(psK[:, 0:L], wk[:], cols(hT, f), start=True, stop=True).then_inc(s_k, 1)
                    for j in range(J):
                        last = pe.matmul(psV[0:P, j * D:(j + 1) * D], hT[:, f.parity, j * P:(j + 1) * P], wvp[:], start=True, stop=True)
                    last.then_inc(s_v, 1)
                if m:
                    def transpose_probs(j):
                        pe.wait_ge(s_exp, m.n * J + (j + 1))
                        if j == 0:
                            wait_done(pe, s_x2t, 1, m.n, 1)
                        elif j == 1:
                            wait_done(pe, s_res, 1, m.n)
                        else:
                            pe.wait_ge(s_PTe, m.n * 2 + 1)
                        for c in range(J):
                            last = pe.transpose(psPT[j % 2][0:P, c * P:(c + 1) * P], probs[0:P, j, c * P:(c + 1) * P], ident[0:P, 0:P])
                        last.then_inc(s_PT, 1)

                    def attend(j):
                        if j == 1:
                            wait_done(pe, s_PTo, 1, m.n)
                        else:
                            pe.wait_ge(s_PTe, m.n * 2 + (1 + j // 2))
                        if j == 0 and f:
                            wait_done(pe, s_hTc, 1, f.n)
                        for c in range(J):
                            last = pe.matmul(psO[0:P, j * D:(j + 1) * D], probsT[0:P, j, c * P:(c + 1) * P], vs[0:P, m.parity, c * D:(c + 1) * D],
                                             start=(c == 0), stop=(c == J - 1))
                        last.then_inc(s_O, 1)

                    transpose_probs(0)
                    transpose_probs(1)
                    attend(0)
                    transpose_probs(2)
                    attend(1)
                    attend(2)
                if k:
                    wait_done(pe, topw.sem, topw.per_turn, k.n)
                    wait_done(pe, place.sem, place.per_turn, k.n, 1)
                    if f:
                        wait_done(pe, s_qkv, 3, f.n)
                    mk = mask[0:P, k.parity, :]
                    for j in range(J):
                        for i in range(j):
                            pe.matmul(psR[0:P, j * E:(j + 1) * E], ones_bf[0:P, 0:P], mk[:, i * E:(i + 1) * E], start=(i == 0), stop=False)
                        pe.matmul(psR[0:P, j * E:(j + 1) * E], before[0:P, 0:P], mk[:, j * E:(j + 1) * E], start=(j == 0), stop=True)
                    for j in range(J):
                        last = pe.matmul(psTot[:, :], ones_bf[0:P, :], mk[:, j * E:(j + 1) * E], start=(j == 0), stop=(j == J - 1))
                    last.then_inc(s_rank, 1)

            attention_iterations(pe, body)

            pe.wait_ge(table.sem, TABLE_COLUMNS)
            pe.matmul(where_row, tab[:, 0:1], ident[:], start=True, stop=True)
            pe.matmul(where_exp, tab[:, 1:2], ident[:], start=True, stop=True).then_inc(s_row, 1)

            def shared(cur, prev):
                if cur:
                    if cur.first == 0:
                        for q in range(2):
                            pe.wait_ge(s_x2kept[q], 16 * (B // 2))
                        wait_done(pe, table.sem, table.per_turn, 0)
                    wait_done(pe, s_sh_b, 2, cur.n, 2)
                    xT = X2T[:, bass.ds(cur.n * L, L)]
                    pe.matmul(bank[cur.parity][0:HID, 0:L], w1_of(shared_pack, 0), xT, start=True, stop=True)
                    pe.matmul(bank[2 + cur.parity][0:HID, 0:L], w1_of(shared_pack, 1), xT, start=True, stop=True).then_inc(s_sh_h, 1)
                if prev:
                    wait_done(pe, s_sh_tt, 1, prev.n)
                    wait_done(pe, s_sh_add, 1, prev.n, 2)
                    for j in range(J):
                        last = pe.matmul(bank[4 + prev.parity][0:P, j * D:(j + 1) * D], tt[0:HID + 1, prev.parity, j * P:(j + 1) * P],
                                         shared_pack[0:HID + 1, W2:W2 + D], start=True, stop=True)
                    last.then_inc(s_sh_z, 1)

            shared_iterations(pe, shared)
            pe.wait_ge(s_sh_add, B)

            def tile(nxt, cur, prev):
                if cur:
                    wait_done(pe, s_wt, 1, cur.n)
                    wait_done(pe, s_xt, 1, cur.n)
                    wait_done(pe, s_bias, 2, cur.n, 2)
                    for two in range(2):
                        last = pe.matmul(psHid(cur, two), w1_of(wt[:, cur.parity, :], two), xt[:, cur.parity, :], start=True, stop=True)
                    last.then_inc(s_hid, 1)
                if nxt:
                    pe.wait_ge(s_xs[nxt.place], (nxt.round + 1) * 16)
                    wait_done(pe, s_xt, 1, nxt.n, 2)
                    for h in range(HALVES):
                        last = pe.transpose(bank[nxt.parity][:, h * 128:(h + 1) * 128], xs[:, nxt.place, h * ROW:h * ROW + D], ident[:])
                    last.then_inc(s_xT, 1)
                if prev:
                    wait_done(pe, s_act, 1, prev.n)
                    wait_done(pe, s_ys, 1, prev.n, 2)
                    for h in range(HALVES):
                        last = pe.matmul(bank[4 + prev.parity][:, h * D:(h + 1) * D], tt[0:HID + 1, prev.parity, h * 128:(h + 1) * 128],
                                         wt[0:HID + 1, prev.parity, W2:W2 + D], start=True, stop=True)
                    last.then_inc(s_y, 1)

            tile_iterations(pe, tile)

        @block.scalar
        def _(act):
            p3 = pack[:].rearrange("p (e c) -> p e c", c=WP)
            act.preload_act_table_set("natural_log_exp_and_others")
            act.dma_start(act_raw[:, 0:5 * E], a["L0_ffn_expert_act"].rearrange("(o e) f -> o (e f)", o=1).broadcast_to([128, 5 * E])).then_inc(s_expw, 16)
            act.dma_start(act_raw[:, 5 * E:], a["L0_ffn_shared_act"].rearrange("(o f) -> o f", o=1).broadcast_to([128, 5])).then_inc(s_expw, 16)
            act.dma_start(b1[0:E, :], a["L0_ffn_expert_b1"]).then_inc(s_expw, 16)
            act.dma_start(b1[E:E + 1, :], a["L0_ffn_shared_b1"].rearrange("(o f) -> o f", o=1)).then_inc(s_expw, 16)
            act.dma_start(p3[:, 0:E, 0:W2], a["L0_ffn_expert_w1"].rearrange("e d i -> d e i")).then_inc(s_expw, 16)
            act.dma_start(p3[:, E, 0:W2], a["L0_ffn_shared_w1"]).then_inc(s_expw, 16)
            act.dma_start(p3[0:HID, 0:E, W2:COLS], a["L0_ffn_expert_w2"].rearrange("e i d -> i e d")).then_inc(s_expw, 16)
            act.dma_start(p3[0:HID, E, W2:COLS], a["L0_ffn_shared_w2"]).then_inc(s_expw, 16)
            act.wait_ge(s_clear, 2)
            act.dma_start(p3[HID:HID + 1, 0:E, W2:COLS], a["L0_ffn_expert_b2"].rearrange("(o e) d -> o e d", o=1)).then_inc(s_expw, 16)
            act.dma_start(p3[HID:HID + 1, E, W2:COLS], a["L0_ffn_shared_b2"].rearrange("(o d) -> o d", o=1)).then_inc(s_expw, 16)
            act.wait_ge(s_const, N_CONST)
            act.wait_ge(setup_dve.sem, SETUP_ABS)
            act.activation(soft[:, 2 * CL:3 * CL], soft[:, CL:2 * CL], ACT.Exp).then_inc(s_soft, 1)
            act.wait_ge(s_soft, 1)
            act.activation(soft[:, 3 * CL:4 * CL], soft[:, 2 * CL:3 * CL], ACT.Ln, bias=1.0).then_inc(s_soft, 1)

            def rstd(steps, b, out_ln, out_rstd, var, scale, eps_col):
                steps.begin(act, b.n)
                steps.did(act.activation(out_ln, var, ACT.Ln, scale=scale, bias=eps_col))
                steps.settle()
                steps.did(act.activation(out_rstd, out_ln, ACT.Exp, scale=-0.5))
                steps.end()

            def body(e, f, m, k):
                if k:
                    wait_done(act, s_ln2, J, k.n)
                    r4 = xrow[0:P, k.parity, :].rearrange("p (j s c) -> p j s c", j=J, s=TOP_K)
                    act.activation(r4[:, :, 1, 0:D], r4[:, :, 0, 0:D], ACT.Copy).then_inc(s_copy2, 1)

                def exponentiate(j):
                    wait_done(act, s_nmax, 1, m.n * J + j)
                    if m.reuses(1):
                        act.wait_ge(s_PT, (m.n - 1) * J + (j + 1))
                    act.activation(probs[0:P, j, :], score_bank(m, j)[0:P, 0:L], ACT.Exp, bias=nmax[0:P, m.parity, j:j + 1],
                                   accum_out=rsum[0:P, m.parity, j:j + 1]).then_inc(s_exp, 1)

                if m:
                    exponentiate(0)
                    exponentiate(1)
                if f:
                    wait_done(act, gn_var.sem, gn_var.per_turn, f.n)
                    g = gco[:, f.parity, :]
                    rstd(gn_rstd, f, g[:, 1:2], g[:, 2:3], g[:, 0:1], -1.0, eps[:, 1:2])
                if m:
                    exponentiate(2)
                if k:
                    wait_done(act, s_x2T, 1, k.n)
                    if k.reuses(2):
                        act.wait_ge(s_x2kept[k.parity], k.half * 16)
                    act.activation(cols(x2t, k), psX[:, 0:L], ACT.Copy).then_inc(s_x2t, 1)
                if f:
                    wait_done(act, gn_coef.sem, gn_coef.per_turn, f.n)
                    wait_done(act, s_hT, 1, f.n)
                    act.activation(cols(hTc, f), psF[:, 0:L], ACT.Identity, scale=gco[:, f.parity, 3:4], bias=gco[:, f.parity, 6:7]).then_inc(s_hTc, 1)
                    wait_done(act, s_q, 1, f.n)
                    act.activation(cols(qT, f), psQ[:, 0:L], ACT.Identity, scale=SCALE, bias=vec[:, BQS:BQS + 1]).then_inc(s_qkv, 1)
                    wait_done(act, s_k, 1, f.n)
                    act.activation(cols(kT, f), psK[:, 0:L], ACT.Identity, bias=vec[:, BK:BK + 1]).then_inc(s_qkv, 1)
                    wait_done(act, s_v, 1, f.n)
                    act.activation(vs[0:P, f.parity, :], psV[0:P, 0:J * D], ACT.Copy).then_inc(s_qkv, 1)

                def take_transposed(j):
                    wait_done(act, s_PT, 1, m.n * J + j)
                    if m.reuses(1):
                        act.wait_ge(s_O, (m.n - 1) * J + (j + 1))
                    act.activation(probsT[0:P, j, :], psPT[0][0:P, 0:L], ACT.Copy).then_inc(s_PTe, 1)

                if m:
                    take_transposed(0)
                if k:
                    wait_done(act, topk.sem, topk.per_turn, k.n)
                    act.activation(gap[0:P, k.parity, J:2 * J], gap[0:P, k.parity, 0:J], ACT.Exp).then_inc(s_gap, 1)
                if m:
                    take_transposed(2)
                if e:
                    wait_done(act, ln1_stats.sem, ln1_stats.per_turn, e.n)
                    r = rs1[0:P, e.parity, :]
                    rstd(ln1_rstd, e, r[:, 0:J], r[:, J:2 * J], mv1[0:P, e.parity, :].rearrange("p (j s) -> p s j", s=2)[:, 1, :], 1.0, eps[0:P, 0:1])
                if m:
                    wait_done(act, ln2_stats.sem, ln2_stats.per_turn, m.n)
                    r = rs2[0:P, m.parity, :]
                    rstd(ln2_rstd, m, r[:, 0:J], r[:, J:2 * J], mv2[0:P, m.parity, :].rearrange("p (j s) -> p s j", s=2)[:, 1, :], 1.0, eps[0:P, 0:1])

            attention_iterations(act, body)

            def shared(cur, prev):
                if cur:
                    for two, (t, c) in enumerate(((hg, B_G), (hu, B_U))):
                        wait_done(act, s_sh_h, 1, cur.n)
                        act.activation(t[0:HID, cur.parity, :], bank[2 * two + cur.parity][0:HID, 0:L], ACT.Identity,
                                       bias=shared_pack[0:HID, c:c + 1]).then_inc(s_sh_b, 1)
                    wait_done(act, s_sh_c, 2, cur.n)
                    act.activation(th[0:HID, cur.parity, :], hg[0:HID, cur.parity, :], ACT.Tanh,
                                   scale=shared_pack[0:HID, ALPHA2:ALPHA2 + 1]).then_inc(s_sh_t, 1)

            act.preload_act_table_set("exp_and_others")
            shared_iterations(act, shared)

            def tile(nxt, cur, prev):
                if cur:
                    w = wt[:, cur.parity, :]
                    wait_done(act, s_hid, 1, cur.n)
                    for two, (t, c) in enumerate(((hg, B_G), (hu, B_U))):
                        act.activation(t[0:HID, cur.parity, 0:TILE], psHid(cur, two), ACT.Identity, bias=w[0:HID, c:c + 1]).then_inc(s_bias, 1)
                if nxt:
                    wait_done(act, s_xT, 1, nxt.n)
                    act.activation(xt[:, nxt.parity, :], bank[nxt.parity][:, 0:TILE], ACT.Copy).then_inc(s_xt, 1)
                if cur:
                    wait_done(act, s_clip, 2, cur.n)
                    act.activation(th[0:HID, cur.parity, 0:TILE], hg[0:HID, cur.parity, 0:TILE], ACT.Tanh, scale=w[0:HID, ALPHA2:ALPHA2 + 1]).then_inc(s_tanh, 1)

            tile_iterations(act, tile)

            def store(b):
                wait_done(act, s_fin, 1, b.n)
                act.dma_start(out[bass.ds(b.n, 1)].rearrange("o (p j) d -> p (o j d)", p=P), fin[0:P, b.parity, :]).then_inc(s_out[b.parity], 16)

            batches(act, store)
            for q in range(2):
                act.wait_ge(s_out[q], 16 * (B // 2))

        @block.vector
        def _(dve):
            p3 = pack[:].rearrange("p (e c) -> p e c", c=WP)
            dve.wait_ge(s_const, N_CONST)
            dve.wait_ge(s_params, 16 * N_PARAMS)
            setup = setup_dve
            setup.begin(dve, 0)
            dve.wait_ge(s_setup_pe, 1)
            setup.did(dve.tensor_copy(wvT[:], bank[0][:, 0:D]))
            dve.wait_ge(s_expw, 16 * N_EXPW)
            acts = act_raw[:].rearrange("p (e f) -> p f e", f=5)
            raw = acts[:, 3:5, :]

            def sp(i):
                return soft[:, i * CL:(i + 1) * CL].rearrange("p (f e) -> p f e", f=2)

            setup.did(dve.tensor_scalar(sp(0), raw, -1.0, None, ALU.mult))
            setup.settle()
            setup.did(dve.tensor_tensor(sp(1), raw, sp(0), ALU.min))
            assert setup.k == SETUP_ABS
            dve.wait_ge(s_setup_pe, 2)
            setup.did(dve.tensor_copy(wvp[:], bank[1][:, 0:D]))
            setup.did(dve.tensor_tensor(vec[:, BVP:BVP + 1], bank[1][:, D:D + 1], vec[:, BP:BP + 1], ALU.add))
            setup.did(dve.tensor_scalar(vec[:, BQS:BQS + 1], vec[:, BQ:BQ + 1], SCALE, None, ALU.mult))
            dve.wait_ge(s_setup_pe, 3)
            for two, c in ((0, B_G), (1, B_U)):
                setup.did(dve.tensor_copy(p3[0:HID, :, c], bank[2][0:HID, two * 32:two * 32 + E + 1]))
            setup.settle()
            setup.did(dve.tensor_scalar(sp(0), raw, 0.0, None, ALU.max))
            setup.settle()
            dve.wait_ge(s_soft, 2)
            setup.did(dve.tensor_tensor(p3[:, :, GMAX], sp(0)[:, 0, :], sp(3)[:, 0, :], ALU.add))
            setup.did(dve.tensor_tensor(p3[:, :, UMAX], sp(0)[:, 1, :], sp(3)[:, 1, :], ALU.add))
            setup.settle()
            setup.did(dve.tensor_scalar(p3[:, :, GMIN], p3[:, :, GMAX], -1.0, None, ALU.mult))
            setup.did(dve.tensor_scalar(p3[:, :, UMIN], p3[:, :, UMAX], -1.0, None, ALU.mult))
            setup.did(dve.tensor_scalar(p3[:, :, ALPHA2], acts[:, 0, :], 0.5, None, ALU.mult))
            setup.did(dve.tensor_copy(p3[:, :, SHIFT], acts[:, 2, :]))
            setup.did(dve.tensor_scalar(sp(1)[:, 0, :], acts[:, 1, :], 0.5, None, ALU.mult))
            setup.settle()
            w2 = p3[0:HID, :, W2:COLS]
            setup.did(dve.tensor_tensor(w2, w2, sp(1)[0:HID, 0, :].unsqueeze(2).broadcast_to([HID, E + 1, D]), ALU.mult))
            setup.settle()
            setup.end()

            def ln_stats(steps, b, src, st, mv):
                steps.begin(dve, b.n)
                for j in range(J):
                    steps.did(dve.bn_stats(st[0:P, b.parity, j * 6:(j + 1) * 6], src[0:P, b.parity, j * D:(j + 1) * D]))
                steps.settle()
                hold(dve, s_held_dve)
                for j in range(J):
                    steps.did(dve.bn_aggr(mv[0:P, b.parity, j * 2:(j + 1) * 2], st[0:P, b.parity, j * 6:(j + 1) * 6]))
                steps.end()

            def ln_apply(b, dst, stride, src, mv, rs, done):
                for j in range(J):
                    dve.tensor_scalar(dst[0:P, b.parity, j * stride:j * stride + D], src[0:P, b.parity, j * D:(j + 1) * D],
                                      mv[0:P, b.parity, j * 2:j * 2 + 1], rs[0:P, b.parity, J + j:J + j + 1],
                                      ALU.subtract, ALU.mult).then_inc(done, 1)

            def body(e, f, m, k):
                if k:
                    wait_done(dve, ln2_rstd.sem, ln2_rstd.per_turn, k.n)
                    if k.reuses(2):
                        dve.wait_ge(s_scat[k.parity], k.half * (16 * J * TOP_K))
                    ln_apply(k, xrow, TOP_K * ROW, h1, mv2, rs2, s_ln2)
                if f:
                    g = gst[:, f.parity, :]
                    wait_done(dve, s_lnT, 1, f.n)
                    gn_stats.begin(dve, f.n)
                    gn_stats.did(dve.bn_stats(g[:, 0:6], psF[:, 0:L]))
                    gn_stats.settle()
                    hold(dve, s_held_dve)
                    gn_stats.did(dve.bn_aggr(g[:, 6:8], g[:, 0:6]))
                    gn_stats.settle()
                    gn_stats.did(dve.scalar_tensor_tensor(g[:, 7:8], g[:, 6:7], g[:, 6:7], g[:, 7:8], ALU.mult, ALU.add))
                    gn_stats.end()

                def row_max(j):
                    wait_done(dve, s_S, 1, m.n * J + j)
                    dve.tensor_reduce(nmax[0:P, m.parity, j:j + 1], score_bank(m, j)[0:P, 0:L], AX, ALU.max, negate=True).then_inc(s_nmax, 1)

                if m:
                    row_max(0)
                    row_max(1)
                if f:
                    wait_done(dve, s_group, 1, f.n)
                    gm, g = gsm[:, f.parity, :], gco[:, f.parity, :]
                    gn_var.begin(dve, f.n)
                    gn_var.did(dve.tensor_copy(gm, psG))
                    gn_var.settle()
                    gn_var.did(dve.scalar_tensor_tensor(g[:, 0:1], gm[:, 0:1], gm[:, 0:1], gm[:, 1:2], ALU.mult, ALU.subtract))
                    gn_var.end()
                if m:
                    row_max(2)
                if f:
                    wait_done(dve, gn_rstd.sem, gn_rstd.per_turn, f.n)
                    gn_coef.begin(dve, f.n)
                    gn_coef.did(dve.tensor_tensor(g[:, 3:4], g[:, 2:3], vec[:, GAMMA:GAMMA + 1], ALU.mult))
                    gn_coef.settle()
                    gn_coef.did(dve.tensor_tensor(g[:, 4:5], gm[:, 0:1], g[:, 3:4], ALU.mult))
                    gn_coef.settle()
                    gn_coef.did(dve.tensor_tensor(g[:, 5:6], vec[:, BETA:BETA + 1], g[:, 4:5], ALU.subtract))
                    gn_coef.settle()
                    gn_coef.did(dve.tensor_tensor(g[:, 6:7], g[:, 5:6], vec[:, BVP:BVP + 1], ALU.add))
                    gn_coef.end()
                    dve.tensor_scalar(cols(hT, f), psF[:, 0:L], g[:, 3:4], g[:, 5:6], ALU.mult, ALU.add).then_inc(s_hT, 1)
                if m:
                    wait_done(dve, s_hback, 1, m.n)
                    dve.tensor_tensor(res[0:P, m.parity, :], psH[0:P, 0:J * D], h0[0:P, m.parity, :], ALU.add).then_inc(s_res, 1)
                if k:
                    wait_done(dve, s_gate, 1, k.n)
                    topk.begin(dve, k.n)
                    l3 = lg[0:P, :].rearrange("p (j e) -> p j e", e=E)
                    topk.did(dve.tensor_tensor(l3, psL[0:P, :].rearrange("p (j e) -> p j e", e=E),
                                               gate_b[0:P, :].unsqueeze(1).broadcast_to([P, J, E]), ALU.add))
                    topk.settle()
                    hold(dve, s_held_dve)
                    for j in range(J):
                        topk.did(dve.max(mx[0:P, j * 8:(j + 1) * 8], lg[0:P, j * E:(j + 1) * E]))
                    topk.settle()
                    hold(dve, s_held_dve)
                    for j in range(J):
                        topk.did(dve.max_index(ix[0:P, j * 8:(j + 1) * 8], mx[0:P, j * 8:(j + 1) * 8], lg[0:P, j * E:(j + 1) * E]))
                    topk.settle()
                    m3 = mx[0:P, :].rearrange("p (j s) -> p s j", s=8)
                    topk.did(dve.tensor_copy(ixf[0:P, :].rearrange("p (j s) -> p j s", s=TOP_K), ix[0:P, :].rearrange("p (j s) -> p j s", s=8)[:, :, 0:TOP_K]))
                    gp = gap[0:P, k.parity, :]
                    topk.did(dve.tensor_tensor(gp[:, 0:J], m3[:, 1, :], m3[:, 0, :], ALU.subtract))
                    topk.end()
                if e:
                    dve.wait_ge(s_x[e.parity], (e.half + 1) * 16)
                    wait_done(dve, s_h0, 1, e.n, 2)
                    dve.tensor_tensor(xm[0:P, e.parity, :].rearrange("p (j c) -> p j c", j=J), xin[0:P, e.parity, :].rearrange("p (j c) -> p j c", j=J),
                                      wpool[0:P, :].unsqueeze(1).broadcast_to([P, J, XROW]), ALU.mult).then_inc(s_mul, 1)
                if m:
                    wait_done(dve, s_PT, 1, m.n * J + 1)
                    if m.reuses(1):
                        dve.wait_ge(s_O, (m.n - 1) * J + 2)
                    dve.tensor_copy(probsT[0:P, 1, :], psPT[1][0:P, 0:L]).then_inc(s_PTo, 1)
                if k:
                    wait_done(dve, s_gap, 1, k.n)
                    topw.begin(dve, k.n)
                    rows = xrow[0:P, k.parity, :].rearrange("p (j s c) -> p s c j", j=J, s=TOP_K)
                    topw.did(dve.tensor_scalar(gp[:, 2 * J:3 * J], gp[:, J:2 * J], 1.0, None, ALU.add))
                    h4 = hot[0:P, :].rearrange("p (j s e) -> p (j s) e", s=TOP_K, e=E)
                    topw.did(dve.tensor_tensor(h4, iota_e[0:P, :].unsqueeze(1).broadcast_to([P, J * TOP_K, E]),
                                               ixf[0:P, :].unsqueeze(2).broadcast_to([P, J * TOP_K, E]), ALU.is_equal))
                    topw.settle()
                    topw.did(dve.reciprocal(rows[:, 0, WEIGHT, :], gp[:, 2 * J:3 * J]))
                    hs = hot[0:P, :].rearrange("p (j s e) -> p s j e", s=TOP_K, e=E)
                    topw.did(dve.tensor_tensor(mask[0:P, k.parity, :].rearrange("p (j e) -> p j e", e=E), hs[:, 0], hs[:, 1], ALU.add))
                    topw.settle()
                    topw.did(dve.tensor_tensor(rows[:, 1, WEIGHT, :], rows[:, 0, WEIGHT, :], gp[:, J:2 * J], ALU.mult))
                    topw.end()
                if e:
                    wait_done(dve, s_h0, 1, e.n)
                    ln_stats(ln1_stats, e, h0, st1, mv1)
                if m:
                    wait_done(dve, s_exp, J, m.n)
                    dve.reciprocal(rinv[0:P, m.parity, :], rsum[0:P, m.parity, :]).then_inc(s_rinv, 1)
                    wait_done(dve, s_rinv, 1, m.n)
                    if m.reuses(2):
                        dve.wait_ge(s_h1kept[m.parity], m.half * 16)
                    wait_done(dve, s_O, J, m.n)
                    for j in range(J):
                        dve.scalar_tensor_tensor(h1[0:P, m.parity, j * D:(j + 1) * D], psO[0:P, j * D:(j + 1) * D], rinv[0:P, m.parity, j:j + 1],
                                                 res[0:P, m.parity, j * D:(j + 1) * D], ALU.mult, ALU.add).then_inc(s_h1, 1)
                if k:
                    wait_done(dve, s_rank, 1, k.n)
                    place.begin(dve, k.n)
                    place.did(dve.tensor_tensor(posall[0:P, :].rearrange("p (j e) -> p j e", e=E), psR[0:P, :].rearrange("p (j e) -> p j e", e=E),
                                                base[0:P, :].unsqueeze(1).broadcast_to([P, J, E]), ALU.add))
                    place.settle()
                    place.did(dve.tensor_tensor(base[:], base[:], psTot, ALU.add))
                    place.settle()
                    place.did(dve.tensor_tensor(posm[0:P, :].rearrange("p (j s e) -> p j s e", s=TOP_K, e=E), hot[0:P, :].rearrange("p (j s e) -> p j s e", s=TOP_K, e=E),
                                                posall[0:P, :].rearrange("p (j e) -> p j e", e=E).unsqueeze(2).broadcast_to([P, J, TOP_K, E]), ALU.mult))
                    place.settle()
                    place.did(dve.tensor_reduce(posf[0:P, :], posm[0:P, :].rearrange("p (s e) -> p s e", e=E), AX, ALU.add))
                    place.settle()
                    place.did(dve.tensor_copy(pos[0:P, k.parity, :], posf[0:P, :]))
                    place.end()
                if e:
                    wait_done(dve, ln1_rstd.sem, ln1_rstd.per_turn, e.n)
                    ln_apply(e, ln1, D, h0, mv1, rs1, s_ln1)
                if m:
                    wait_done(dve, s_h1, J, m.n)
                    ln_stats(ln2_stats, m, h1, st2, mv2)

            attention_iterations(dve, body)

            wait_done(dve, place.sem, place.per_turn, B - 1)
            table.begin(dve, 0)

            def T(i):
                return tab[:, i * E:(i + 1) * E]

            def step(ins):
                table.did(ins)
                table.settle()

            shift = TILE.bit_length() - 1
            assert 1 << shift == TILE
            step(dve.tensor_tensor(T(1), base[:], base0[:], ALU.subtract))
            step(dve.tensor_scalar(tabi[:, 0:E], T(1), float(TILE - 1), None, ALU.add))
            step(dve.tensor_scalar(tabi[:, E:2 * E], tabi[:, 0:E], shift, None, ALU.arith_shift_right))
            step(dve.tensor_copy(T(2), tabi[:, E:2 * E]))
            src, dst = T(2), T(3)
            for s in (1, 2, 4, 8):
                step(dve.tensor_copy(dst[:, 0:s], src[:, 0:s]))
                step(dve.tensor_tensor(dst[:, s:E], src[:, s:E], src[:, 0:E - s], ALU.add))
                src, dst = dst, (T(4) if dst is not None and s in (1, 4) else T(3))
            upto = src
            one = T(7)
            step(dve.tensor_tensor(T(5), upto, tile_no[:, 0:1].broadcast_to([128, E]), ALU.is_le))
            step(dve.tensor_tensor(T(6), T(5), T(2), ALU.mult))
            step(dve.tensor_reduce(one[:, 0:1], T(5), AX, ALU.add))
            step(dve.tensor_reduce(one[:, 1:2], T(6), AX, ALU.add))
            step(dve.tensor_tensor(one[:, 2:3], tile_no[:], upto[:, E - 1:E], ALU.is_lt))
            step(dve.tensor_tensor(one[:, 3:4], tile_no[:], one[:, 1:2], ALU.subtract))
            step(dve.tensor_scalar(one[:, 4:5], one[:, 3:4], float(TILE), float(-PAD_ROW), ALU.mult, ALU.add))
            step(dve.scalar_tensor_tensor(one[:, 5:6], one[:, 0:1], float(CAP), one[:, 4:5], ALU.mult, ALU.add))
            step(dve.tensor_tensor(one[:, 6:7], one[:, 5:6], one[:, 2:3], ALU.mult))
            step(dve.tensor_scalar(tab[:, 0:1], one[:, 6:7], float(PAD_ROW), None, ALU.add))
            step(dve.tensor_scalar(tab[:, 1:2], one[:, 0:1], float(E - 1), float(WP), ALU.min, ALU.mult))
            step(dve.tensor_copy(where[0:1, 256:256 + E], base[0:1, :]))
            assert table.k == TABLE_COLUMNS
            dve.wait_ge(s_row, 1)
            step(dve.tensor_copy(where[0:1, 0:256], bank[0][0:1, 0:256]))
            table.end()
            for q in range(2):
                dve.wait_ge(s_h1kept[q], 16 * (B // 2))

            def gate(sems, cur, width, w):
                s_clipped, s_tanhed, s_gate_done, s_done = sems
                g, u, q = hg[0:HID, cur.parity, 0:width], hu[0:HID, cur.parity, 0:width], cur.parity
                wait_done(dve, s_tanhed, 1, cur.n)
                dve.scalar_tensor_tensor(ga[0:HID, q, 0:width], th[0:HID, q, 0:width], 1.0, g, ALU.add, ALU.mult).then_inc(s_gate_done, 1)
                wait_done(dve, s_clipped, 2, cur.n)
                wait_done(dve, s_gate_done, 1, cur.n)
                dve.scalar_tensor_tensor(tt[0:HID, q, 0:width], u, w[0:HID, SHIFT:SHIFT + 1], ga[0:HID, q, 0:width], ALU.add, ALU.mult).then_inc(s_done, 1)

            def clip(s_biased, s_clipped, cur, width, w):
                for two, (t, lo, hi) in enumerate(((hg, GMIN, GMAX), (hu, UMIN, UMAX))):
                    v = t[0:HID, cur.parity, 0:width]
                    dve.wait_ge(s_biased, cur.n * 2 + (two + 1))
                    dve.tensor_scalar(v, v, w[0:HID, lo:lo + 1], w[0:HID, hi:hi + 1], ALU.max, ALU.min).then_inc(s_clipped, 1)

            def shared(cur, prev):
                if cur:
                    clip(s_sh_b, s_sh_c, cur, L, shared_pack)
                if prev:
                    wait_done(dve, s_sh_z, 1, prev.n)
                    r = H1[0:P, bass.ds(prev.n * (J * D), J * D)]
                    dve.tensor_tensor(r, r, bank[4 + prev.parity][0:P, 0:J * D], ALU.add).then_inc(s_sh_add, 1)
                if cur:
                    gate((s_sh_c, s_sh_t, s_sh_g, s_sh_tt), cur, L, shared_pack)

            shared_iterations(dve, shared)

            def tile(nxt, cur, prev):
                if cur:
                    w = wt[:, cur.parity, :]
                    clip(s_bias, s_clip, cur, TILE, w)
                if prev:
                    q = prev.place
                    wait_done(dve, s_y, 1, prev.n)
                    wgt = xs[:, q, :].rearrange("p (h c) -> p h c", c=ROW)[:, :, WEIGHT:WEIGHT + 1].broadcast_to([128, HALVES, D])
                    dve.tensor_tensor(ys[:, q, :].rearrange("p (h d) -> p h d", h=HALVES),
                                      bank[4 + prev.parity][:, 0:HALVES * D].rearrange("p (h d) -> p h d", h=HALVES), wgt, ALU.mult).then_inc(s_ys, 1)
                if nxt:
                    r = dve.value_load(where[0:1, bass.ds(nxt.n + 128, 1)], min_val=0, max_val=(E - 1) * WP)
                    dve.tensor_copy(wt[:, nxt.parity, :], pack[:, bass.ds(r, WP)]).then_inc(s_wt, 1)
                if cur:
                    gate((s_clip, s_tanh, s_gated, s_act), cur, TILE, w)

            tile_iterations(dve, tile)

            def result(b):
                wait_done(dve, s_zz, 1, b.n)
                if b.reuses(2):
                    dve.wait_ge(s_out[b.parity], b.half * 16)
                dve.tensor_tensor(fin[0:P, b.parity, :], z0[0:P, b.parity, :], H1[0:P, bass.ds(b.n * (J * D), J * D)], ALU.add).then_inc(s_fin, 1)

            batches(dve, result)

    return nc


_INS = ['x', 'L0_tok_weight1', 'L0_attn_gamma', 'L0_attn_beta', 'L0_attn_wq', 'L0_attn_bq', 'L0_attn_wk', 'L0_attn_bk', 'L0_attn_wv', 'L0_attn_bv',
        'L0_attn_wp', 'L0_attn_bp', 'L0_ffn_gate_w', 'L0_ffn_gate_b', 'L0_ffn_shared_w1', 'L0_ffn_shared_b1', 'L0_ffn_shared_w2', 'L0_ffn_shared_b2',
        'L0_ffn_shared_act', 'L0_ffn_expert_w1', 'L0_ffn_expert_b1', 'L0_ffn_expert_w2', 'L0_ffn_expert_b2', 'L0_ffn_expert_act']


def kernel(**inputs):
    import numpy as _np
    import concourse.bacc as _bacc
    from concourse import mybir as _mybir
    from concourse.bass_utils import run_bass_kernel_spmd as _run

    nc = _bacc.Bacc("TRN2", target_bir_lowering=False, num_devices=1)
    arrays, args = {}, {}
    for name in _INS:
        v = _np.ascontiguousarray(inputs[name])
        arrays[f"in_{name}"] = v
        args[name] = nc.dram_tensor(f"in_{name}", v.shape, _mybir.dt.from_np(v.dtype), kind="ExternalInput").ap()
    b, rows, d = arrays["in_x"].shape
    out = nc.dram_tensor("out", (b, rows // 2, d), _mybir.dt.float32, kind="ExternalOutput").ap()
    audio_tower(nc, args, out)
    r = _run(nc, [arrays], core_ids=[0])
    return r.results[0]["out"]
```

```python
from contextlib import ExitStack

import concourse.bass as bass
from concourse import mybir

F32 = mybir.dt.float32
I32 = mybir.dt.int32
U32 = mybir.dt.uint32
BF16 = mybir.dt.bfloat16
ALU = mybir.AluOpType
ACT = mybir.ActivationFunctionType
AX = mybir.AxisListType.X

LN_EPS = 1e-5
GN_EPS = 1e-3
GN_GROUPS = 8
TOP_K = 2


class Turn:

    def __init__(self, c, m=None, step=1):
        self.c, self.m, self.step = c, m, step
        self.first = c if m is None else None
        self.n = c if m is None else m * step + c
        self.parity, self.half = self.place(2), self.round(2)

    def place(self, buffers):
        return self.c % buffers

    def round(self, buffers):
        return self.c // buffers if self.m is None else self.m * (self.step // buffers) + self.c // buffers

    def next(self):
        return Turn(self.c + 1, self.m, self.step)

    def reuses(self, buffers):
        return self.first is None or self.first >= buffers


def wait_done(eng, sem, per_turn, n, lag=0):
    value = (n + (1 - lag)) * per_turn
    if not isinstance(value, int) or value > 0:
        eng.wait_ge(sem, value)


def hold(eng, held):
    eng.sem_inc(held, 1)


class Steps:

    def __init__(self, sem, per_turn):
        self.sem, self.per_turn = sem, per_turn

    def begin(self, eng, n):
        self.eng, self.n, self.k = eng, n, 0

    def did(self, ins):
        ins.then_inc(self.sem, 1)
        self.k += 1
        assert self.k <= self.per_turn

    def settle(self):
        self.eng.wait_ge(self.sem, self.n * self.per_turn + self.k)

    def end(self):
        assert self.k == self.per_turn, (self.k, self.per_turn)


def audio_tower(nc, a, out):
    x = a["x"]
    B, ROWS, D = x.shape
    POOL = a["L0_tok_weight1"].shape[0]
    L = ROWS // POOL
    J = 3
    P = L // J
    E = a["L0_ffn_gate_w"].shape[1]
    HID = a["L0_ffn_shared_w2"].shape[0]
    N = B * L
    SCALE = float(D) ** -0.5
    XROW = POOL * D
    GC = D // GN_GROUPS
    assert P * J == L and D == 128 and P <= 128

    TILE = 256
    HALVES = TILE // 128
    NT = (TOP_K * N + E * (TILE - 1)) // TILE
    CAP = N + TILE
    PAD_ROW = E * CAP
    ROW = D + 2
    DEST, WEIGHT = D, D + 1
    SKIP = 1 << 20
    RING = 8
    ZRING = 4

    W2 = 2 * HID
    COLS = W2 + D
    B_G, U_ADD, ALPHA, ALPHA_B, G_LO, G_HI, U_LO, U_HI = range(COLS, COLS + 8)
    WP = COLS + 8

    with ExitStack() as ctx:
        def sb(name, shape, dt=F32):
            return ctx.enter_context(nc.sbuf_tensor(name, shape, dt))

        def sem(name):
            return ctx.enter_context(nc.semaphore(name))

        routed = nc.dram_tensor("routed", [E * CAP + TILE, ROW], F32, kind="Internal").ap()
        slots = nc.dram_tensor("slots", [TOP_K * N, D], F32, kind="Internal").ap()

        bank = [ctx.enter_context(nc.psum_tensor(f"bank{i}", [128, 512], F32)) for i in range(8)]

        ident = sb("ident", [128, 128])
        group_avg = sb("group_avg", [128, 128])
        before = sb("before", [128, 128], BF16)
        ones_bf = sb("ones_bf", [128, 128], BF16)
        iota_e = sb("iota_e", [128, E])
        base = sb("base", [128, E])
        base0 = sb("base0", [128, E])
        dest_id = sb("dest_id", [128, J * TOP_K], I32)
        eps = sb("eps", [128, 2])
        tile_no = sb("tile_no", [128, 1])
        wpool = sb("wpool", [128, XROW])
        gate_w = sb("gate_w", [128, E])
        gate_b = sb("gate_b", [128, E])
        wq = sb("wq", [128, D])
        wk = sb("wk", [128, D])
        wv = sb("wv", [128, D])
        wp = sb("wp", [128, D])
        wvT = sb("wvT", [128, D])
        wvp = sb("wvp", [128, D])
        vec = sb("vec", [128, 8])
        GAMMA, BETA, BQ, BK, BV, BP, BQS, BVP = range(8)
        pack = sb("pack", [128, (E + 1) * WP])
        b1 = sb("b1", [E + 1, W2])
        act_raw = sb("act_raw", [128, (E + 1) * 5])
        soft = sb("soft", [128, 4 * 2 * (E + 1)])
        b_up = sb("b_up", [128, E + 1])
        pads = sb("pads", [128, HALVES * ROW])

        xin = sb("xin", [128, 2, J * XROW])
        xm = sb("xm", [128, 2, J * XROW])
        nb1 = sb("nb1", [128, 2, J])
        nb2 = sb("nb2", [128, 2, J])
        h0 = sb("h0", [128, 2, J * D])
        st1 = sb("st1", [128, 2, J * 6])
        mv1 = sb("mv1", [128, 2, J * 2])
        rs1 = sb("rs1", [128, 2, 2 * J])
        ln1 = sb("ln1", [128, 2, J * D])
        gst = sb("gst", [128, 2, 8])
        gsm = sb("gsm", [128, 2, 2])
        gco = sb("gco", [128, 2, 12])
        hT = sb("hT", [128, 2, L])
        hTc = sb("hTc", [128, 2, L])
        qT = sb("qT", [128, 2, L])
        kT = sb("kT", [128, 2, L])
        vs = sb("vs", [128, 2, J * D])
        nmax = sb("nmax", [128, 2, J])
        rsum = sb("rsum", [128, 2, J])
        rinv = sb("rinv", [128, 2, J])
        probs = sb("probs", [128, J, L])
        probsT = sb("probsT", [128, J, L])
        res = sb("res", [128, 2, J * D])
        h1 = sb("h1", [128, 2, J * D])
        st2 = sb("st2", [128, 2, J * 6])
        mv2 = sb("mv2", [128, 2, J * 2])
        rs2 = sb("rs2", [128, 2, 2 * J])
        xrow = sb("xrow", [128, 2, J * TOP_K * ROW])
        x2t = sb("x2t", [128, 2, L])
        lg = sb("lg", [128, J * E])
        mx = sb("mx", [128, J * 8])
        ix = sb("ix", [128, J * 8], U32)
        ixf = sb("ixf", [128, J * TOP_K])
        gap = sb("gap", [128, 2, 4 * J])
        hot = sb("hot", [128, J * TOP_K * E])
        mask = sb("mask", [128, 2, J * E], BF16)
        posall = sb("posall", [128, J * E])
        posm = sb("posm", [128, J * TOP_K * E])
        posf = sb("posf", [128, J * TOP_K])
        pos = sb("pos", [128, 2, J * TOP_K], I32)

        H1 = sb("H1", [128, B * J * D])
        X2T = sb("X2T", [128, B * L])

        tab = sb("tab", [128, 16 * E])
        tabi = sb("tabi", [128, 2 * E], I32)
        where = sb("where", [1, 2 * 128], I32)
        ends = sb("ends", [1, E], I32)
        xs = sb("xs", [128, RING, HALVES * ROW])
        wt = sb("wt", [128, RING, WP])
        ys = sb("ys", [128, RING, HALVES * D])
        xt = sb("xt", [128, 2, TILE])
        hg = sb("hg", [128, 2, TILE])
        hu = sb("hu", [128, 2, TILE])
        sg = sb("sg", [128, 2, TILE])
        tt = sb("tt", [128, 2, TILE])
        sh_g = sb("sh_g", [128, L])
        sh_u = sb("sh_u", [128, L])
        sh_s = sb("sh_s", [128, L])
        sh_t = sb("sh_t", [128, L])
        z = sb("z", [128, ZRING, TOP_K, J * D])
        zz = sb("zz", [128, 2, J * D])
        fin = sb("fin", [128, 2, J * D])

        s_const = sem("const_ready")
        s_clear = sem("pack_cleared")
        s_held_dve = sem("held_dve")
        s_held_pool = sem("held_pool")
        s_params = sem("params_loaded")
        s_expw = sem("expert_weights_loaded")
        s_setup_pe = sem("setup_products")
        setup_dve = Steps(sem("setup_dve_steps"), 17)
        s_soft = sem("softplus_tail")
        s_x = [sem(f"x_loaded{q}") for q in range(2)]
        s_mul = sem("pool_products")
        s_h0 = sem("pooled")
        ln1_stats = Steps(sem("ln1_stats"), 2 * J)
        ln1_rstd = Steps(sem("ln1_rstd"), 2)
        s_ln1 = sem("ln1_applied")
        s_lnT = sem("ln1_transposed")
        gn_stats = Steps(sem("gn_channel_stats"), 3)
        s_group = sem("gn_group_means")
        gn_var = Steps(sem("gn_variance"), 2)
        gn_rstd = Steps(sem("gn_rstd"), 2)
        gn_coef = Steps(sem("gn_coefficients"), 4)
        s_hT = sem("h_ready")
        s_hTc = sem("h_with_offset_ready")
        s_q = sem("q_product")
        s_k = sem("k_product")
        s_v = sem("v_product")
        s_qkv = sem("qkv_in_sbuf")
        s_S = sem("scores")
        s_nmax = sem("row_maxima")
        s_exp = sem("probabilities")
        s_PT = sem("probabilities_transposed")
        s_PTs = sem("transposed_in_sbuf")
        s_O = sem("attention_out")
        s_hback = sem("h_token_major")
        s_res = sem("residual_ready")
        s_rinv = sem("row_sums_inverted")
        s_h1 = sem("h1_ready")
        s_h1kept = [sem(f"h1_kept{q}") for q in range(2)]
        ln2_stats = Steps(sem("ln2_stats"), 2 * J)
        ln2_rstd = Steps(sem("ln2_rstd"), 2)
        s_ln2 = sem("ln2_applied")
        s_h0kept = [sem(f"h0_kept{q}") for q in range(2)]
        s_nb1 = sem("ln1_offsets")
        s_nb2 = sem("ln2_offsets")
        s_x2T = sem("x2_transposed")
        s_x2t = sem("x2T_in_sbuf")
        s_x2kept = [sem(f"x2T_kept{q}") for q in range(2)]
        s_gate = sem("gate_logits")
        topk = Steps(sem("topk_steps"), 3 + 2 * J)
        s_gap = sem("second_weight_exp")
        topw = Steps(sem("top_weights_and_mask"), 5)
        s_rank = sem("ranks")
        place = Steps(sem("places"), 5)
        ids = Steps(sem("dest_ids_written"), 2)
        s_scat = [sem(f"rows_scattered{q}") for q in range(2)]

        table = Steps(sem("tile_table"), 24)
        s_ends = sem("expert_ends")
        s_row = sem("tile_table_row")
        s_pad = sem("pad_rows_written")
        s_sh_gate = sem("shared_gate_product")
        s_sh_up = sem("shared_up_product")
        s_sh_clip = sem("shared_gate_clipped")
        s_sh_clipu = sem("shared_up_clipped")
        s_sh_sig = sem("shared_sigmoid")
        s_sh_gated = sem("shared_gated")
        s_sh_act = sem("shared_activated")
        s_sh_z = sem("shared_out")
        s_sh_add = sem("shared_added")
        s_xs = [sem(f"tile_loaded{q}") for q in range(RING)]
        s_xT = sem("tile_transposed")
        s_xt = sem("tile_x_in_sbuf")
        s_hid = sem("tile_hidden")
        s_clip = sem("tile_gate_clipped")
        s_clipu = sem("tile_up_clipped")
        s_sig = sem("tile_sigmoid")
        s_gated = sem("tile_gated")
        s_act = sem("tile_activated")
        s_y = sem("tile_out")
        s_ys = sem("tile_weighted")
        s_back = [sem(f"tile_scattered{q}") for q in range(RING)]
        s_z = [sem(f"slots_loaded{q}") for q in range(ZRING)]
        s_zz = sem("slots_added")
        s_fin = sem("result_ready")
        s_out = [sem(f"stored{q}") for q in range(2)]

        def cols(t, b):
            return t[:, b.parity, :]

        psF, psG = bank[0], bank[0][:, 384:386]
        psQ, psK, psV = bank[1], bank[2], bank[3]
        psL = bank[2][:, 0:J * E]
        psO = bank[3]
        psS = [bank[4], bank[5], bank[1]]
        psPT = [bank[6], bank[7]]
        psX, psH = bank[6], bank[7]
        psR = bank[6][:, 0:J * E]
        psTot = bank[6][:, J * E:(J + 1) * E]
        where_row = bank[0][0:1, 0:128]
        where_exp = bank[0][0:1, 128:256]

        N_CONST = 20
        N_PARAMS = 13
        N_EXPW = 10
        SETUP_ATTENTION = 4
        SETUP_ABS = 6
        TABLE_COLUMNS = 23
        CL = 2 * (E + 1)
        shared_pack = pack[:, E * WP:(E + 1) * WP]

        def w1_of(w, two):
            return w[:, 0:W2].rearrange("d (i two) -> d two i", two=2)[:, two, :]

        psXT = [bank[0], bank[1]]
        psHid = [bank[2], bank[3]]
        psY = [bank[4], bank[5]]
        psShG, psShU, psShZ = bank[6], bank[7], bank[7]

        def attention_iterations(eng, body):
            lo, hi = 3, B - 5
            assert (hi - lo) % 2 == 0

            def edge(i):
                body(*(Turn(n) if 0 <= n < B else None for n in (i + 3, i + 2, i + 1, i, i - 1)))

            for i in range(-3, lo):
                edge(i)
            with eng.Fori(0, (hi - lo) // 2) as m:
                for i in (lo, lo + 1):
                    body(*(Turn(n, m, 2) for n in (i + 3, i + 2, i + 1, i, i - 1)))
            for i in range(hi, B + 1):
                edge(i)

        def tile_iterations(eng, body):
            lo, total = 4, max(NT + 3, 4 * B + 1)
            loops = (min(NT, 4 * B) - lo) // RING

            def edge(u):
                sh = Turn(u // 4) if u // 4 < B else None
                before_ = Turn(u // 4 - 1) if u % 4 == 0 and u > 0 and u // 4 <= B else None
                body(*(Turn(n) if 0 <= n < NT else None for n in (u, u - 1, u - 2, u - 3)), u % 4, sh, before_)

            for u in range(0, lo):
                edge(u)
            with eng.Fori(0, loops) as m:
                for u in range(lo, lo + RING):
                    sh, before_ = Turn(u // 4, m, RING // 4), Turn(u // 4 - 1, m, RING // 4)
                    body(*(Turn(n, m, RING) for n in (u, u - 1, u - 2, u - 3)), u % 4, sh, before_)
            for u in range(lo + RING * loops, total):
                edge(u)

        def batches(eng, body):
            for n in range(ZRING):
                body(Turn(n))
            with eng.Fori(0, (B - ZRING) // ZRING) as m:
                for n in range(ZRING, 2 * ZRING):
                    body(Turn(n, m, ZRING))

        def write_pads(eng, first):
            eng.wait_ge(s_ends, 1)
            for e in range(first, E, 2):
                r = eng.value_load(ends[0:1, e:e + 1], min_val=0, max_val=E * CAP - TILE)
                eng.dma_start(routed[bass.ds(r, TILE), :].rearrange("(p h) c -> p (h c)", h=HALVES), pads[:]).then_inc(s_pad, 16)

        def setup_dve_done(eng):
            eng.wait_ge(setup_dve.sem, setup_dve.per_turn)

        block = ctx.enter_context(nc.Block())

        @block.sync
        def _(sp):
            sp.dma_start(wpool[0:P, :], a["L0_tok_weight1"].rearrange("(o p) d -> o (p d)", o=1).broadcast_to([P, XROW])).then_inc(s_params, 16)
            for t, name in ((wq, "wq"), (wk, "wk"), (wv, "wv"), (wp, "wp")):
                sp.dma_start(t[:], a["L0_attn_" + name]).then_inc(s_params, 16)
            for c, name in ((GAMMA, "gamma"), (BETA, "beta"), (BQ, "bq"), (BK, "bk"), (BV, "bv"), (BP, "bp")):
                sp.dma_start(vec[:, c:c + 1], a["L0_attn_" + name].rearrange("(d o) -> d o", o=1)).then_inc(s_params, 16)
            sp.dma_start(gate_w[:], a["L0_ffn_gate_w"]).then_inc(s_params, 16)
            sp.dma_start(gate_b[:], a["L0_ffn_gate_b"].rearrange("(o e) -> o e", o=1).broadcast_to([128, E])).then_inc(s_params, 16)

            def load_x(b):
                wait_done(sp, s_mul, 1, b.n, 2)
                sp.dma_start(xin[0:P, b.parity, :], x[bass.ds(b.n, 1)].rearrange("o (p r) d -> p (o r d)", p=P)).then_inc(s_x[b.parity], 16)

            def keep(a, b, c, d, k):
                if a:
                    if a.first == 0:
                        load_x(a)
                    if a.first != B - 1:
                        load_x(a.next())
                    wait_done(sp, s_h0, 1, a.n)
                    sp.dma_start(H1[0:P, bass.ds(a.n * (J * D), J * D)], h0[0:P, a.parity, :]).then_inc(s_h0kept[a.parity], 16)
                if k:
                    wait_done(sp, s_x2t, 1, k.n)
                    sp.dma_start(X2T[:, bass.ds(k.n * L, L)], cols(x2t, k)).then_inc(s_x2kept[k.parity], 16)
                if d:
                    wait_done(sp, s_h1, J, d.n)
                    sp.dma_start(H1[0:P, bass.ds(d.n * (J * D), J * D)], h1[0:P, d.parity, :]).then_inc(s_h1kept[d.parity], 16)

            attention_iterations(sp, keep)

            write_pads(sp, 0)
            sp.dma_start(routed[PAD_ROW:PAD_ROW + TILE, :].rearrange("(p h) c -> p (h c)", h=HALVES), pads[:]).then_inc(s_pad, 16)
            sp.wait_ge(s_pad, 16 * (E + 1))
            wait_done(sp, table.sem, table.per_turn, 0)
            for q in range(2):
                sp.wait_ge(s_scat[q], 16 * J * TOP_K * (B // 2))

            setup_dve_done(sp)

            def load_tile(x, h, g, y, part, sh, shp):
                if x:
                    q = x.place(RING)
                    if x.reuses(RING):
                        sp.wait_ge(s_back[q], x.round(RING) * (16 * HALVES))
                    r = sp.value_load(where[0:1, bass.ds(x.n, 1)], min_val=0, max_val=PAD_ROW)
                    sp.dma_start(xs[:, q, :], routed[bass.ds(r, TILE), :].rearrange("(p h) c -> p (h c)", h=HALVES)).then_inc(s_xs[q], 16)
                    w = sp.value_load(where[0:1, bass.ds(x.n + 128, 1)], min_val=0, max_val=(E - 1) * WP)
                    sp.dma_start(wt[:, q, :], pack[:, bass.ds(w, WP)]).then_inc(s_xs[q], 16)

            tile_iterations(sp, load_tile)
            for q in range(RING):
                sp.wait_ge(s_back[q], 16 * HALVES * len(range(q, NT, RING)))

            def load_slots(b):
                wait_done(sp, s_zz, 1, b.n, ZRING)
                q = b.place(ZRING)
                sp.dma_start(z[0:P, q], slots.rearrange("(s n) d -> n s d", s=TOP_K)[bass.ds(b.n * L, L)]
                             .rearrange("(p j) s d -> p s j d", p=P)).then_inc(s_z[q], 16)

            batches(sp, load_slots)

        @block.gpsimd
        def _(pool):
            pp = pack[:].rearrange("p (e c) -> p e c", c=WP)
            pool.memset(pp[HID:128, :, W2:WP], 0.0).then_inc(s_clear, 1)
            pool.wait_ge(s_clear, 1)
            pool.memset(ident[:], 0.0).then_inc(s_const, 1)
            pool.memset(group_avg[:], 1.0 / GC).then_inc(s_const, 1)
            pool.memset(before[:], 1.0).then_inc(s_const, 1)
            pool.memset(ones_bf[:], 1.0).then_inc(s_const, 1)
            pool.memset(eps[:, 0:1], LN_EPS).then_inc(s_const, 1)
            pool.memset(eps[:, 1:2], GN_EPS).then_inc(s_const, 1)
            pool.memset(pads[:], 0.0).then_inc(s_const, 1)
            pool.memset(tt[:], 1.0).then_inc(s_const, 1)
            pool.memset(sh_t[:], 1.0).then_inc(s_const, 1)
            pool.iota(iota_e[:], pattern=[[1, E]], base=0, channel_multiplier=0, allow_small_or_imprecise_dtypes=True).then_inc(s_const, 1)
            pool.iota(base0[:], pattern=[[CAP, E]], base=0, channel_multiplier=0, allow_small_or_imprecise_dtypes=True).then_inc(s_const, 1)
            pool.iota(tile_no[:], pattern=[[0, 1]], base=0, channel_multiplier=1, allow_small_or_imprecise_dtypes=True).then_inc(s_const, 1)
            pool.iota(dest_id[:].rearrange("p (j k) -> p j k", k=TOP_K), pattern=[[1, J], [N, TOP_K]], base=0, channel_multiplier=J).then_inc(s_const, 1)
            pool.wait_ge(s_const, 13)
            pool.tensor_copy(base[:], base0[:]).then_inc(s_const, 1)
            for h in range(HALVES):
                pool.memset(pads[:, h * ROW + DEST:h * ROW + DEST + 1].bitcast(I32), SKIP).then_inc(s_const, 1)
            pool.affine_select(out=ident[:], in_=ident[:], compare_op=ALU.not_equal, fill=1.0, base=0,
                               pattern=[[-1, 128]], channel_multiplier=1).then_inc(s_const, 1)
            pool.affine_select(out=before[:], in_=before[:], compare_op=ALU.is_gt, fill=0.0, base=0,
                               pattern=[[1, 128]], channel_multiplier=-1).then_inc(s_const, 1)
            g3 = group_avg[:].rearrange("p (g c) -> p g c", c=GC)
            pool.affine_select(out=g3, in_=g3, compare_op=ALU.is_ge, fill=0.0, base=0,
                               pattern=[[-GC, GN_GROUPS], [0, GC]], channel_multiplier=1).then_inc(s_const, 1)
            pool.wait_ge(s_const, 19)
            pool.affine_select(out=g3, in_=g3, compare_op=ALU.is_ge, fill=0.0, base=GC - 1,
                               pattern=[[GC, GN_GROUPS], [0, GC]], channel_multiplier=-1).then_inc(s_const, 1)

            def rows_out(a, b, c, d, k):
                if a:
                    wait_done(pool, s_mul, 1, a.n)
                    wait_done(pool, s_ln1, J, a.n, 2)
                    if a.reuses(2):
                        pool.wait_ge(s_h0kept[a.parity], a.half * 16)
                    v = xm[0:P, a.parity, :].rearrange("p (j r d) -> p j r d", j=J, r=POOL)
                    pool.tensor_tensor(h0[0:P, a.parity, :].rearrange("p (j d) -> p j d", j=J), v[:, :, 0, :], v[:, :, 1, :], ALU.add).then_inc(s_h0, 1)
                if k:
                    ids.begin(pool, k.n)
                    if k.reuses(2):
                        pool.wait_ge(s_scat[k.parity], k.half * (16 * J * TOP_K))
                    wait_done(pool, ids.sem, ids.per_turn, k.n, 1)
                    rows = xrow[0:P, k.parity, :].rearrange("p (s c) -> p s c", c=ROW)
                    hold(pool, s_held_pool)
                    ids.did(pool.tensor_copy(rows[:, :, DEST].bitcast(I32), dest_id[0:P, :]))
                    ids.settle()
                    hold(pool, s_held_pool)
                    ids.did(pool.tensor_scalar(dest_id[0:P, :], dest_id[0:P, :], L, None, ALU.add))
                    ids.end()
                    wait_done(pool, s_ln2, J, k.n)
                    wait_done(pool, topw.sem, topw.per_turn, k.n)
                    wait_done(pool, place.sem, place.per_turn, k.n)
                    hold(pool, s_held_pool)
                    for s in range(J * TOP_K):
                        pool.indirect_dma_start(out=routed[:, :], out_offset=bass.IndirectOffsetOnAxis(ap=pos[0:P, k.parity, s:s + 1], axis=0),
                                                in_=xrow[0:P, k.parity, s * ROW:(s + 1) * ROW], in_offset=None).then_inc(s_scat[k.parity], 16)

            attention_iterations(pool, rows_out)

            def scatter_tile(x, h, g, y, part, sh, shp):
                if y:
                    q = y.place(RING)
                    wait_done(pool, s_ys, HALVES, y.n)
                    hold(pool, s_held_pool)
                    for h in range(HALVES):
                        pool.indirect_dma_start(out=slots[:, :], out_offset=bass.IndirectOffsetOnAxis(ap=xs[:, q, h * ROW + DEST:h * ROW + DEST + 1].bitcast(I32), axis=0),
                                                in_=ys[:, q, h * D:(h + 1) * D], in_offset=None,
                                                bounds_check=TOP_K * N - 1, oob_is_err=False).then_inc(s_back[q], 16)

            tile_iterations(pool, scatter_tile)

            def add_slots(b):
                q = b.place(ZRING)
                pool.wait_ge(s_z[q], (b.round(ZRING) + 1) * 16)
                wait_done(pool, s_fin, 1, b.n, 2)
                pool.tensor_tensor(zz[0:P, b.parity, :], z[0:P, q, 0], z[0:P, q, 1], ALU.add).then_inc(s_zz, 1)

            batches(pool, add_slots)

        @block.tensor
        def _(pe):
            pe.wait_ge(s_const, N_CONST)
            pe.wait_ge(s_params, 16 * N_PARAMS)
            pe.transpose(bank[0][:, 0:D], wv[:], ident[:]).then_inc(s_setup_pe, 1)
            pe.wait_ge(setup_dve.sem, 1)
            pe.matmul(bank[1][:, 0:D], wvT[:], wp[:], start=True, stop=True)
            pe.matmul(bank[1][:, D:D + 1], wp[:], vec[:, BV:BV + 1], start=True, stop=True).then_inc(s_setup_pe, 1)
            pe.wait_ge(setup_dve.sem, SETUP_ATTENTION)

            def body(a, b, c, d, k):
                if d:
                    wait_done(pe, s_hTc, 1, d.n)
                    wait_done(pe, s_PTs, J, d.n, 1)
                    for j in range(J):
                        last = pe.transpose(psH[0:P, j * D:(j + 1) * D], hTc[:, d.parity, j * P:(j + 1) * P], ident[:])
                    last.then_inc(s_hback, 1)
                if b:
                    wait_done(pe, s_ln1, J, b.n)
                    wait_done(pe, s_hTc, 1, b.n, 1)
                    for j in range(J):
                        last = pe.transpose(psF[:, j * P:(j + 1) * P], ln1[0:P, b.parity, j * D:(j + 1) * D], ident[0:P, 0:P])
                    last.then_inc(s_lnT, 1)
                if c:
                    wait_done(pe, s_hT, 1, c.n)
                    wait_done(pe, s_exp, J, c.n, 1)
                    pe.matmul(psQ[:, 0:L], wq[:], cols(hT, c), start=True, stop=True).then_inc(s_q, 1)
                    if c.reuses(3):
                        pe.wait_ge(topk.sem, (c.n - 3) * topk.per_turn + 1)
                    pe.matmul(psK[:, 0:L], wk[:], cols(hT, c), start=True, stop=True).then_inc(s_k, 1)
                    wait_done(pe, s_h1, J, c.n, 2)
                    for j in range(J):
                        last = pe.matmul(psV[0:P, j * D:(j + 1) * D], hT[:, c.parity, j * P:(j + 1) * P], wvp[:], start=True, stop=True)
                    last.then_inc(s_v, 1)
                if k:
                    wait_done(pe, s_ln2, J, k.n)
                    wait_done(pe, place.sem, place.per_turn, k.n, 1)
                    for j in range(J):
                        last = pe.transpose(psX[:, j * P:(j + 1) * P], xrow[0:P, k.parity, j * TOP_K * ROW:j * TOP_K * ROW + D], ident[0:P, 0:P])
                    last.then_inc(s_x2T, 1)
                if d:
                    def transpose_probs(j):
                        pe.wait_ge(s_exp, d.n * J + (j + 1))
                        if j == 0:
                            wait_done(pe, s_x2t, 1, d.n, 1)
                        elif j == 1:
                            wait_done(pe, s_res, 1, d.n)
                        else:
                            pe.wait_ge(s_PTs, d.n * J + 1)
                        for i in range(J):
                            last = pe.transpose(psPT[j % 2][0:P, i * P:(i + 1) * P], probs[0:P, j, i * P:(i + 1) * P], ident[0:P, 0:P])
                        last.then_inc(s_PT, 1)

                    def attend(j):
                        wait_done(pe, s_PTs, 1, d.n * J + j)
                        if j == 0:
                            wait_done(pe, s_qkv, 3, *((c.n,) if c else (d.n,)))
                        for i in range(J):
                            last = pe.matmul(psO[0:P, j * D:(j + 1) * D], probsT[0:P, j, i * P:(i + 1) * P], vs[0:P, d.parity, i * D:(i + 1) * D],
                                             start=(i == 0), stop=(i == J - 1))
                        last.then_inc(s_O, 1)

                    transpose_probs(0)
                    transpose_probs(1)
                    attend(0)
                    transpose_probs(2)
                    attend(1)
                    attend(2)
                if b:
                    wait_done(pe, gn_stats.sem, gn_stats.per_turn, b.n)
                    pe.matmul(psG, group_avg[:], gst[:, b.parity, 6:8], start=True, stop=True).then_inc(s_group, 1)
                if k:
                    wait_done(pe, s_x2t, 1, k.n)
                    if c:
                        wait_done(pe, s_qkv, 3, c.n)
                    wait_done(pe, topk.sem, topk.per_turn, k.n, 1)
                    for j in range(J):
                        last = pe.matmul(psL[0:P, j * E:(j + 1) * E], x2t[:, k.parity, j * P:(j + 1) * P], gate_w[:], start=True, stop=True)
                    last.then_inc(s_gate, 1)
                if c:
                    wait_done(pe, s_qkv, 3, c.n)
                    wait_done(pe, s_exp, J, c.n, 1)
                    for j in range(J):
                        pe.matmul(psS[j][0:P, 0:L], qT[:, c.parity, j * P:(j + 1) * P], cols(kT, c), start=True, stop=True).then_inc(s_S, 1)
                if k:
                    wait_done(pe, topw.sem, topw.per_turn, k.n)
                    if d:
                        wait_done(pe, s_PTs, J, d.n)
                    mk = mask[0:P, k.parity, :]
                    for j in range(J):
                        for i in range(j):
                            pe.matmul(psR[0:P, j * E:(j + 1) * E], ones_bf[0:P, 0:P], mk[:, i * E:(i + 1) * E], start=(i == 0), stop=False)
                        pe.matmul(psR[0:P, j * E:(j + 1) * E], before[0:P, 0:P], mk[:, j * E:(j + 1) * E], start=(j == 0), stop=True)
                    for j in range(J):
                        last = pe.matmul(psTot[:, :], ones_bf[0:P, :], mk[:, j * E:(j + 1) * E], start=(j == 0), stop=(j == J - 1))
                    last.then_inc(s_rank, 1)

            attention_iterations(pe, body)

            pe.wait_ge(s_expw, 16 * N_EXPW)
            wait_done(pe, place.sem, place.per_turn, B - 1)
            b1v = b1[:].rearrange("e (i two) -> e two i", two=2)
            for two in range(2):
                last = pe.transpose(bank[2][0:HID, two * 32:two * 32 + E + 1], b1v[:, two, :], ident[0:E + 1, 0:E + 1])
            last.then_inc(s_setup_pe, 1)

            pe.wait_ge(table.sem, TABLE_COLUMNS)
            pe.matmul(where_row, tab[:, 0:1], ident[:], start=True, stop=True)
            pe.matmul(where_exp, tab[:, 1:2], ident[:], start=True, stop=True).then_inc(s_row, 1)

            for q in range(2):
                pe.wait_ge(s_x2kept[q], 16 * (B // 2))
            setup_dve_done(pe)
            wait_done(pe, table.sem, table.per_turn, 0)

            def tile(x, h, g, y, part, sh, shp):
                if h:
                    q = h.place(RING)
                    wait_done(pe, s_xt, 1, h.n)
                    wait_done(pe, s_clipu, 1, h.n, 2)
                    for two in range(2):
                        last = pe.matmul(psHid[h.parity][0:HID, two * TILE:(two + 1) * TILE], w1_of(wt[:, q, :], two), xt[:, h.parity, :], start=True, stop=True)
                    last.then_inc(s_hid, 1)
                if x:
                    q = x.place(RING)
                    pe.wait_ge(s_xs[q], (x.round(RING) + 1) * 32)
                    wait_done(pe, s_xt, 1, x.n, 2)
                    for k in range(HALVES):
                        last = pe.transpose(psXT[x.parity][:, k * 128:(k + 1) * 128], xs[:, q, k * ROW:k * ROW + D], ident[:])
                    last.then_inc(s_xT, 1)
                if y:
                    q = y.place(RING)
                    wait_done(pe, s_act, 1, y.n)
                    wait_done(pe, s_ys, HALVES, y.n, 2)
                    for k in range(HALVES):
                        last = pe.matmul(psY[y.parity][:, k * D:(k + 1) * D], tt[0:HID + 1, y.parity, k * 128:(k + 1) * 128],
                                         wt[0:HID + 1, q, W2:W2 + D], start=True, stop=True)
                    last.then_inc(s_y, 1)
                if sh and part == 0:
                    wait_done(pe, s_sh_clip, 1, sh.n, 1)
                    pe.matmul(psShG[0:HID, 0:L], w1_of(shared_pack, 0), X2T[:, bass.ds(sh.n * L, L)], start=True, stop=True).then_inc(s_sh_gate, 1)
                if sh and part == 1:
                    wait_done(pe, s_sh_add, 1, sh.n, 1)
                    pe.matmul(psShU[0:HID, 0:L], w1_of(shared_pack, 1), X2T[:, bass.ds(sh.n * L, L)], start=True, stop=True).then_inc(s_sh_up, 1)
                if shp and part == 0:
                    wait_done(pe, s_sh_act, 1, shp.n)
                    for j in range(J):
                        last = pe.matmul(psShZ[0:P, j * D:(j + 1) * D], sh_t[0:HID + 1, j * P:(j + 1) * P],
                                         shared_pack[0:HID + 1, W2:W2 + D], start=True, stop=True)
                    last.then_inc(s_sh_z, 1)

            tile_iterations(pe, tile)

        @block.scalar
        def _(act):
            p3 = pack[:].rearrange("p (e c) -> p e c", c=WP)
            act.preload_act_table_set("natural_log_exp_and_others")
            act.dma_start(act_raw[:, 0:5 * E], a["L0_ffn_expert_act"].rearrange("(o e) f -> o (e f)", o=1).broadcast_to([128, 5 * E])).then_inc(s_expw, 16)
            act.dma_start(act_raw[:, 5 * E:], a["L0_ffn_shared_act"].rearrange("(o f) -> o f", o=1).broadcast_to([128, 5])).then_inc(s_expw, 16)
            act.dma_start(b1[0:E, :], a["L0_ffn_expert_b1"]).then_inc(s_expw, 16)
            act.dma_start(b1[E:E + 1, :], a["L0_ffn_shared_b1"].rearrange("(o f) -> o f", o=1)).then_inc(s_expw, 16)
            act.dma_start(p3[:, 0:E, 0:W2], a["L0_ffn_expert_w1"].rearrange("e d i -> d e i")).then_inc(s_expw, 16)
            act.dma_start(p3[:, E, 0:W2], a["L0_ffn_shared_w1"]).then_inc(s_expw, 16)
            act.dma_start(p3[0:HID, 0:E, W2:COLS], a["L0_ffn_expert_w2"].rearrange("e i d -> i e d")).then_inc(s_expw, 16)
            act.dma_start(p3[0:HID, E, W2:COLS], a["L0_ffn_shared_w2"]).then_inc(s_expw, 16)
            act.wait_ge(s_clear, 1)
            act.dma_start(p3[HID:HID + 1, 0:E, W2:COLS], a["L0_ffn_expert_b2"].rearrange("(o e) d -> o e d", o=1)).then_inc(s_expw, 16)
            act.dma_start(p3[HID:HID + 1, E, W2:COLS], a["L0_ffn_shared_b2"].rearrange("(o d) -> o d", o=1)).then_inc(s_expw, 16)
            act.wait_ge(s_const, N_CONST)
            act.wait_ge(setup_dve.sem, SETUP_ATTENTION)

            def rstd(steps, b, out_ln, out_rstd, var, scale, eps_col):
                steps.begin(act, b.n)
                steps.did(act.activation(out_ln, var, ACT.Ln, scale=scale, bias=eps_col))
                steps.settle()
                steps.did(act.activation(out_rstd, out_ln, ACT.Exp, scale=-0.5))
                steps.end()

            def ln_apply(b, dst, copies, stride, src, nb, rs, done):
                for j in range(J):
                    o = dst[0:P, b.parity, j * copies * stride:(j + 1) * copies * stride].rearrange("p (s c) -> p s c", s=copies)[:, :, 0:D]
                    i = src[0:P, b.parity, j * D:(j + 1) * D].unsqueeze(1).broadcast_to([P, copies, D])
                    act.activation(o, i, ACT.Identity, scale=rs[0:P, b.parity, J + j:J + j + 1], bias=nb[0:P, b.parity, j:j + 1]).then_inc(done, 1)

            def body(a, b, c, d, k):
                if k:
                    wait_done(act, s_nb2, 1, k.n)
                    if k.reuses(2):
                        act.wait_ge(s_scat[k.parity], k.half * (16 * J * TOP_K))
                    ln_apply(k, xrow, TOP_K, ROW, h1, nb2, rs2, s_ln2)
                if c:
                    wait_done(act, s_q, 1, c.n)
                    act.activation(cols(qT, c), psQ[:, 0:L], ACT.Identity, scale=SCALE, bias=vec[:, BQS:BQS + 1]).then_inc(s_qkv, 1)
                    wait_done(act, s_k, 1, c.n)
                    act.activation(cols(kT, c), psK[:, 0:L], ACT.Identity, bias=vec[:, BK:BK + 1]).then_inc(s_qkv, 1)
                    wait_done(act, s_v, 1, c.n)
                    act.activation(vs[0:P, c.parity, :], psV[0:P, 0:J * D], ACT.Copy).then_inc(s_qkv, 1)
                if k:
                    wait_done(act, s_x2T, 1, k.n)
                    if k.reuses(2):
                        act.wait_ge(s_x2kept[k.parity], k.half * 16)
                    act.activation(cols(x2t, k), psX[:, 0:L], ACT.Copy).then_inc(s_x2t, 1)
                if d:
                    for j in range(J):
                        wait_done(act, s_PT, 1, d.n * J + j)
                        if d.reuses(1):
                            act.wait_ge(s_O, (d.n - 1) * J + (j + 1))
                        act.activation(probsT[0:P, j, :], psPT[j % 2][0:P, 0:L], ACT.Copy).then_inc(s_PTs, 1)
                if b:
                    wait_done(act, gn_var.sem, gn_var.per_turn, b.n)
                    g = gco[:, b.parity, :]
                    rstd(gn_rstd, b, g[:, 1:2], g[:, 2:3], g[:, 0:1], -1.0, eps[:, 1:2])
                if d:
                    wait_done(act, ln2_stats.sem, ln2_stats.per_turn, d.n)
                    r = rs2[0:P, d.parity, :]
                    rstd(ln2_rstd, d, r[:, 0:J], r[:, J:2 * J], mv2[0:P, d.parity, :].rearrange("p (j s) -> p s j", s=2)[:, 1, :], 1.0, eps[0:P, 0:1])
                if c:
                    for j in range(J):
                        wait_done(act, s_nmax, 1, c.n * J + j)
                        if c.reuses(1):
                            act.wait_ge(s_PT, (c.n - 1) * J + (j + 1))
                        act.activation(probs[0:P, j, :], psS[j][0:P, 0:L], ACT.Exp, bias=nmax[0:P, c.parity, j:j + 1],
                                       accum_out=rsum[0:P, c.parity, j:j + 1]).then_inc(s_exp, 1)
                if b:
                    wait_done(act, gn_coef.sem, gn_coef.per_turn, b.n)
                    act.activation(cols(hT, b), psF[:, 0:L], ACT.Identity, scale=g[:, 3:4], bias=g[:, 5:6]).then_inc(s_hT, 1)
                    act.activation(cols(hTc, b), psF[:, 0:L], ACT.Identity, scale=g[:, 3:4], bias=g[:, 6:7]).then_inc(s_hTc, 1)
                if k:
                    wait_done(act, topk.sem, topk.per_turn, k.n)
                    act.activation(gap[0:P, k.parity, J:2 * J], gap[0:P, k.parity, 0:J], ACT.Exp).then_inc(s_gap, 1)
                if a:
                    wait_done(act, ln1_stats.sem, ln1_stats.per_turn, a.n)
                    r = rs1[0:P, a.parity, :]
                    rstd(ln1_rstd, a, r[:, 0:J], r[:, J:2 * J], mv1[0:P, a.parity, :].rearrange("p (j s) -> p s j", s=2)[:, 1, :], 1.0, eps[0:P, 0:1])
                    wait_done(act, s_nb1, 1, a.n)
                    ln_apply(a, ln1, 1, D, h0, nb1, rs1, s_ln1)

            attention_iterations(act, body)

            write_pads(act, 1)

            act.wait_ge(setup_dve.sem, SETUP_ABS)
            act.activation(soft[:, 2 * CL:3 * CL], soft[:, CL:2 * CL], ACT.Exp).then_inc(s_soft, 1)
            act.wait_ge(s_soft, 1)
            act.activation(soft[:, 3 * CL:4 * CL], soft[:, 2 * CL:3 * CL], ACT.Ln, bias=1.0).then_inc(s_soft, 1)
            act.preload_act_table_set("sigmoid_and_others")

            setup_dve_done(act)

            def tile(x, h, g, y, part, sh, shp):
                if x:
                    wait_done(act, s_xT, 1, x.n)
                    wait_done(act, s_hid, 1, x.n, 2)
                    act.activation(xt[:, x.parity, :], psXT[x.parity][:, 0:TILE], ACT.Copy).then_inc(s_xt, 1)
                if y:
                    q = y.place(RING)
                    wait_done(act, s_y, 1, y.n)
                    if y.reuses(RING):
                        act.wait_ge(s_back[q], y.round(RING) * (16 * HALVES))
                    for k in range(HALVES):
                        act.activation(ys[:, q, k * D:(k + 1) * D], psY[y.parity][:, k * D:(k + 1) * D], ACT.Copy,
                                       scale=xs[:, q, k * ROW + WEIGHT:k * ROW + WEIGHT + 1]).then_inc(s_ys, 1)
                if h:
                    w = wt[:, h.place(RING), :]
                    wait_done(act, s_clip, 1, h.n)
                    wait_done(act, s_gated, 1, h.n, 2)
                    act.activation(sg[0:HID, h.parity, :], hg[0:HID, h.parity, :], ACT.Sigmoid,
                                   scale=w[0:HID, ALPHA:ALPHA + 1], bias=w[0:HID, ALPHA_B:ALPHA_B + 1]).then_inc(s_sig, 1)
                if sh and part == 1:
                    wait_done(act, s_sh_clip, 1, sh.n)
                    wait_done(act, s_sh_gated, 1, sh.n, 1)
                    act.activation(sh_s[0:HID, :], sh_g[0:HID, :], ACT.Sigmoid,
                                   scale=shared_pack[0:HID, ALPHA:ALPHA + 1], bias=shared_pack[0:HID, ALPHA_B:ALPHA_B + 1]).then_inc(s_sh_sig, 1)

            tile_iterations(act, tile)

            def store(b):
                wait_done(act, s_fin, 1, b.n)
                act.dma_start(out[bass.ds(b.n, 1)].rearrange("o (p j) d -> p (o j d)", p=P), fin[0:P, b.parity, :]).then_inc(s_out[b.parity], 16)

            batches(act, store)
            for q in range(2):
                act.wait_ge(s_out[q], 16 * (B // 2))

        @block.vector
        def _(dve):
            p3 = pack[:].rearrange("p (e c) -> p e c", c=WP)
            dve.wait_ge(s_const, N_CONST)
            dve.wait_ge(s_params, 16 * N_PARAMS)
            setup = setup_dve
            setup.begin(dve, 0)
            dve.wait_ge(s_setup_pe, 1)
            setup.did(dve.tensor_copy(wvT[:], bank[0][:, 0:D]))
            dve.wait_ge(s_setup_pe, 2)
            setup.did(dve.tensor_copy(wvp[:], bank[1][:, 0:D]))
            setup.did(dve.tensor_tensor(vec[:, BVP:BVP + 1], bank[1][:, D:D + 1], vec[:, BP:BP + 1], ALU.add))
            setup.did(dve.tensor_scalar(vec[:, BQS:BQS + 1], vec[:, BQ:BQ + 1], SCALE, None, ALU.mult))
            setup.settle()
            assert setup.k == SETUP_ATTENTION

            def ln_stats(steps, b, src, st, mv):
                steps.begin(dve, b.n)
                for j in range(J):
                    steps.did(dve.bn_stats(st[0:P, b.parity, j * 6:(j + 1) * 6], src[0:P, b.parity, j * D:(j + 1) * D]))
                steps.settle()
                hold(dve, s_held_dve)
                for j in range(J):
                    steps.did(dve.bn_aggr(mv[0:P, b.parity, j * 2:(j + 1) * 2], st[0:P, b.parity, j * 6:(j + 1) * 6]))
                steps.end()

            def offsets(b, nb, mv, rs, done):
                dve.scalar_tensor_tensor(nb[0:P, b.parity, :], mv[0:P, b.parity, :].rearrange("p (j s) -> p s j", s=2)[:, 0, :], -1.0,
                                         rs[0:P, b.parity, J:2 * J], ALU.mult, ALU.mult).then_inc(done, 1)

            def body(a, b, c, d, k):
                if k:
                    wait_done(dve, ln2_rstd.sem, ln2_rstd.per_turn, k.n)
                    offsets(k, nb2, mv2, rs2, s_nb2)
                if d:
                    wait_done(dve, s_hback, 1, d.n)
                    dve.wait_ge(s_h0kept[d.parity], (d.half + 1) * 16)
                    dve.tensor_tensor(res[0:P, d.parity, :], psH[0:P, 0:J * D], H1[0:P, bass.ds(d.n * (J * D), J * D)], ALU.add).then_inc(s_res, 1)
                if b:
                    g, gm, gc = gst[:, b.parity, :], gsm[:, b.parity, :], gco[:, b.parity, :]
                    wait_done(dve, s_lnT, 1, b.n)
                    gn_stats.begin(dve, b.n)
                    gn_stats.did(dve.bn_stats(g[:, 0:6], psF[:, 0:L]))
                    gn_stats.settle()
                    hold(dve, s_held_dve)
                    gn_stats.did(dve.bn_aggr(g[:, 6:8], g[:, 0:6]))
                    gn_stats.settle()
                    gn_stats.did(dve.scalar_tensor_tensor(g[:, 7:8], g[:, 6:7], g[:, 6:7], g[:, 7:8], ALU.mult, ALU.add))
                    gn_stats.end()
                if a:
                    dve.wait_ge(s_x[a.parity], (a.half + 1) * 16)
                    wait_done(dve, s_h0, 1, a.n, 2)
                    dve.tensor_tensor(xm[0:P, a.parity, :].rearrange("p (j c) -> p j c", j=J), xin[0:P, a.parity, :].rearrange("p (j c) -> p j c", j=J),
                                      wpool[0:P, :].unsqueeze(1).broadcast_to([P, J, XROW]), ALU.mult).then_inc(s_mul, 1)
                if d:
                    wait_done(dve, s_exp, J, d.n)
                    dve.reciprocal(rinv[0:P, d.parity, :], rsum[0:P, d.parity, :]).then_inc(s_rinv, 1)
                    wait_done(dve, s_rinv, 1, d.n)
                    if d.reuses(2):
                        dve.wait_ge(s_h1kept[d.parity], d.half * 16)
                    wait_done(dve, s_O, J, d.n)
                    for j in range(J):
                        dve.scalar_tensor_tensor(h1[0:P, d.parity, j * D:(j + 1) * D], psO[0:P, j * D:(j + 1) * D], rinv[0:P, d.parity, j:j + 1],
                                                 res[0:P, d.parity, j * D:(j + 1) * D], ALU.mult, ALU.add).then_inc(s_h1, 1)
                if b:
                    wait_done(dve, s_group, 1, b.n)
                    gn_var.begin(dve, b.n)
                    gn_var.did(dve.tensor_copy(gm, psG))
                    gn_var.settle()
                    gn_var.did(dve.scalar_tensor_tensor(gc[:, 0:1], gm[:, 0:1], gm[:, 0:1], gm[:, 1:2], ALU.mult, ALU.subtract))
                    gn_var.end()
                if d:
                    wait_done(dve, s_h1, J, d.n)
                    ln_stats(ln2_stats, d, h1, st2, mv2)
                if k:
                    wait_done(dve, s_gate, 1, k.n)
                    topk.begin(dve, k.n)
                    topk.did(dve.tensor_tensor(lg[0:P, :].rearrange("p (j e) -> p j e", e=E), psL[0:P, :].rearrange("p (j e) -> p j e", e=E),
                                               gate_b[0:P, :].unsqueeze(1).broadcast_to([P, J, E]), ALU.add))
                if b:
                    wait_done(dve, gn_rstd.sem, gn_rstd.per_turn, b.n)
                    gn_coef.begin(dve, b.n)
                    gn_coef.did(dve.tensor_tensor(gc[:, 3:4], gc[:, 2:3], vec[:, GAMMA:GAMMA + 1], ALU.mult))
                    gn_coef.settle()
                    gn_coef.did(dve.tensor_tensor(gc[:, 4:5], gm[:, 0:1], gc[:, 3:4], ALU.mult))
                    gn_coef.settle()
                    gn_coef.did(dve.tensor_tensor(gc[:, 5:6], vec[:, BETA:BETA + 1], gc[:, 4:5], ALU.subtract))
                    gn_coef.settle()
                    gn_coef.did(dve.tensor_tensor(gc[:, 6:7], gc[:, 5:6], vec[:, BVP:BVP + 1], ALU.add))
                    gn_coef.end()

                def row_max(j):
                    wait_done(dve, s_S, 1, c.n * J + j)
                    dve.tensor_reduce(nmax[0:P, c.parity, j:j + 1], psS[j][0:P, 0:L], AX, ALU.max, negate=True).then_inc(s_nmax, 1)

                if c:
                    row_max(0)
                if k:
                    topk.settle()
                    hold(dve, s_held_dve)
                    for j in range(J):
                        topk.did(dve.max(mx[0:P, j * 8:(j + 1) * 8], lg[0:P, j * E:(j + 1) * E]))
                if c:
                    row_max(1)
                if k:
                    topk.settle()
                    hold(dve, s_held_dve)
                    for j in range(J):
                        topk.did(dve.max_index(ix[0:P, j * 8:(j + 1) * 8], mx[0:P, j * 8:(j + 1) * 8], lg[0:P, j * E:(j + 1) * E]))
                    m3 = mx[0:P, :].rearrange("p (j s) -> p s j", s=8)
                    gp = gap[0:P, k.parity, :]
                    topk.did(dve.tensor_tensor(gp[:, 0:J], m3[:, 1, :], m3[:, 0, :], ALU.subtract))
                    topk.settle()
                    topk.did(dve.tensor_copy(ixf[0:P, :].rearrange("p (j s) -> p j s", s=TOP_K), ix[0:P, :].rearrange("p (j s) -> p j s", s=8)[:, :, 0:TOP_K]))
                    topk.end()
                if c:
                    row_max(2)
                if a:
                    wait_done(dve, s_h0, 1, a.n)
                    ln_stats(ln1_stats, a, h0, st1, mv1)
                if k:
                    topk.settle()
                    wait_done(dve, s_gap, 1, k.n)
                    topw.begin(dve, k.n)
                    rows = xrow[0:P, k.parity, :].rearrange("p (j s c) -> p s c j", j=J, s=TOP_K)
                    topw.did(dve.tensor_scalar(gp[:, 2 * J:3 * J], gp[:, J:2 * J], 1.0, None, ALU.add))
                    h4 = hot[0:P, :].rearrange("p (j s e) -> p (j s) e", s=TOP_K, e=E)
                    topw.did(dve.tensor_tensor(h4, iota_e[0:P, :].unsqueeze(1).broadcast_to([P, J * TOP_K, E]),
                                               ixf[0:P, :].unsqueeze(2).broadcast_to([P, J * TOP_K, E]), ALU.is_equal))
                    topw.settle()
                    topw.did(dve.reciprocal(rows[:, 0, WEIGHT, :], gp[:, 2 * J:3 * J]))
                    hs = hot[0:P, :].rearrange("p (j s e) -> p s j e", s=TOP_K, e=E)
                    topw.did(dve.tensor_tensor(mask[0:P, k.parity, :].rearrange("p (j e) -> p j e", e=E), hs[:, 0], hs[:, 1], ALU.add))
                    topw.settle()
                    topw.did(dve.tensor_tensor(rows[:, 1, WEIGHT, :], rows[:, 0, WEIGHT, :], gp[:, J:2 * J], ALU.mult))
                    topw.end()
                if a:
                    wait_done(dve, ln1_rstd.sem, ln1_rstd.per_turn, a.n)
                    offsets(a, nb1, mv1, rs1, s_nb1)
                if k:
                    wait_done(dve, s_rank, 1, k.n)
                    place.begin(dve, k.n)
                    place.did(dve.tensor_tensor(posall[0:P, :].rearrange("p (j e) -> p j e", e=E), psR[0:P, :].rearrange("p (j e) -> p j e", e=E),
                                                base[0:P, :].unsqueeze(1).broadcast_to([P, J, E]), ALU.add))
                    place.settle()
                    place.did(dve.tensor_tensor(base[:], base[:], psTot, ALU.add))
                    place.did(dve.tensor_tensor(posm[0:P, :].rearrange("p (j s e) -> p j s e", s=TOP_K, e=E), hot[0:P, :].rearrange("p (j s e) -> p j s e", s=TOP_K, e=E),
                                                posall[0:P, :].rearrange("p (j e) -> p j e", e=E).unsqueeze(2).broadcast_to([P, J, TOP_K, E]), ALU.mult))
                    place.settle()
                    place.did(dve.tensor_reduce(posf[0:P, :], posm[0:P, :].rearrange("p (s e) -> p s e", e=E), AX, ALU.add))
                    place.settle()
                    place.did(dve.tensor_copy(pos[0:P, k.parity, :], posf[0:P, :]))
                    place.end()

            attention_iterations(dve, body)

            wait_done(dve, place.sem, place.per_turn, B - 1)
            dve.tensor_copy(ends[0:1, :], base[0:1, :]).then_inc(s_ends, 1)
            table.begin(dve, 0)

            def T(i):
                return tab[:, i * E:(i + 1) * E]

            def step(ins):
                table.did(ins)
                table.settle()

            shift = TILE.bit_length() - 1
            assert 1 << shift == TILE
            step(dve.tensor_tensor(T(1), base[:], base0[:], ALU.subtract))
            step(dve.tensor_scalar(tabi[:, 0:E], T(1), float(TILE - 1), None, ALU.add))
            step(dve.tensor_scalar(tabi[:, E:2 * E], tabi[:, 0:E], shift, None, ALU.arith_shift_right))
            step(dve.tensor_copy(T(2), tabi[:, E:2 * E]))
            src, dst = T(2), T(3)
            for s in (1, 2, 4, 8):
                step(dve.tensor_copy(dst[:, 0:s], src[:, 0:s]))
                step(dve.tensor_tensor(dst[:, s:E], src[:, s:E], src[:, 0:E - s], ALU.add))
                src, dst = dst, (T(4) if dst is not None and s in (1, 4) else T(3))
            upto = src
            one = T(7)
            step(dve.tensor_tensor(T(5), upto, tile_no[:, 0:1].broadcast_to([128, E]), ALU.is_le))
            step(dve.tensor_tensor(T(6), T(5), T(2), ALU.mult))
            step(dve.tensor_reduce(one[:, 0:1], T(5), AX, ALU.add))
            step(dve.tensor_reduce(one[:, 1:2], T(6), AX, ALU.add))
            step(dve.tensor_tensor(one[:, 2:3], tile_no[:], upto[:, E - 1:E], ALU.is_lt))
            step(dve.tensor_tensor(one[:, 3:4], tile_no[:], one[:, 1:2], ALU.subtract))
            step(dve.tensor_scalar(one[:, 4:5], one[:, 3:4], float(TILE), float(-PAD_ROW), ALU.mult, ALU.add))
            step(dve.scalar_tensor_tensor(one[:, 5:6], one[:, 0:1], float(CAP), one[:, 4:5], ALU.mult, ALU.add))
            step(dve.tensor_tensor(one[:, 6:7], one[:, 5:6], one[:, 2:3], ALU.mult))
            step(dve.tensor_scalar(tab[:, 0:1], one[:, 6:7], float(PAD_ROW), None, ALU.add))
            step(dve.tensor_scalar(tab[:, 1:2], one[:, 0:1], float(E - 1), float(WP), ALU.min, ALU.mult))
            assert table.k == TABLE_COLUMNS
            dve.wait_ge(s_row, 1)
            step(dve.tensor_copy(where[0:1, 0:256], bank[0][0:1, 0:256]))
            table.end()

            dve.wait_ge(s_expw, 16 * N_EXPW)
            acts = act_raw[:].rearrange("p (e f) -> p f e", f=5)
            raw = acts[:, 3:5, :]

            def sp(i):
                return soft[:, i * CL:(i + 1) * CL].rearrange("p (f e) -> p f e", f=2)

            setup.did(dve.tensor_scalar(sp(0), raw, -1.0, None, ALU.mult))
            setup.settle()
            setup.did(dve.tensor_tensor(sp(1), raw, sp(0), ALU.min))
            assert setup.k == SETUP_ABS
            dve.wait_ge(s_setup_pe, 3)
            b_gate = p3[0:HID, :, B_G]
            setup.did(dve.tensor_copy(b_gate, bank[2][0:HID, 0:E + 1]))
            setup.did(dve.tensor_copy(b_up[0:HID, :], bank[2][0:HID, 32:32 + E + 1]))
            dve.wait_ge(s_soft, 2)
            setup.settle()
            setup.did(dve.scalar_tensor_tensor(sp(1), raw, 0.0, sp(3), ALU.max, ALU.add))
            setup.did(dve.tensor_copy(p3[0:HID, :, ALPHA], acts[0:HID, 0, :]))
            setup.did(dve.tensor_tensor(p3[0:HID, :, ALPHA_B], acts[0:HID, 0, :], b_gate, ALU.mult))
            setup.did(dve.tensor_tensor(p3[0:HID, :, U_ADD], acts[0:HID, 2, :], b_up[0:HID, :], ALU.add))
            w2 = p3[0:HID, :, W2:COLS]
            setup.did(dve.tensor_tensor(w2, w2, acts[0:HID, 1, :].unsqueeze(2).broadcast_to([HID, E + 1, D]), ALU.mult))
            setup.settle()
            for f, bias, lo, hi in ((0, b_gate, G_LO, G_HI), (1, b_up[0:HID, :], U_LO, U_HI)):
                setup.did(dve.tensor_tensor(p3[0:HID, :, hi], sp(1)[0:HID, f, :], bias, ALU.subtract))
                setup.did(dve.scalar_tensor_tensor(p3[0:HID, :, lo], sp(1)[0:HID, f, :], -1.0, bias, ALU.mult, ALU.subtract))
            setup.settle()
            setup.end()
            for q in range(2):
                dve.wait_ge(s_h1kept[q], 16 * (B // 2))

            def tile(x, h, g, y, part, sh, shp):
                def clip(two, t, lo, hi, done):
                    w = wt[:, h.place(RING), :]
                    wait_done(dve, s_hid, 1, h.n)
                    wait_done(dve, s_act, 1, h.n, 2)
                    dve.tensor_scalar(t[0:HID, h.parity, :], psHid[h.parity][0:HID, two * TILE:(two + 1) * TILE], w[0:HID, lo:lo + 1], w[0:HID, hi:hi + 1],
                                      ALU.max, ALU.min).then_inc(done, 1)

                if h:
                    clip(0, hg, G_LO, G_HI, s_clip)
                if g:
                    w = wt[:, g.place(RING), :]
                    gt, ut = hg[0:HID, g.parity, :], hu[0:HID, g.parity, :]
                    wait_done(dve, s_sig, 1, g.n)
                    dve.scalar_tensor_tensor(gt, gt, w[0:HID, B_G:B_G + 1], sg[0:HID, g.parity, :], ALU.add, ALU.mult).then_inc(s_gated, 1)
                if h:
                    clip(1, hu, U_LO, U_HI, s_clipu)
                if g:
                    wait_done(dve, s_gated, 1, g.n)
                    wait_done(dve, s_y, 1, g.n, 2)
                    dve.scalar_tensor_tensor(tt[0:HID, g.parity, :], ut, w[0:HID, U_ADD:U_ADD + 1], gt, ALU.add, ALU.mult).then_inc(s_act, 1)
                if sh and part == 1:
                    wait_done(dve, s_sh_gate, 1, sh.n)
                    wait_done(dve, s_sh_act, 1, sh.n, 1)
                    dve.tensor_scalar(sh_g[0:HID, :], psShG[0:HID, 0:L], shared_pack[0:HID, G_LO:G_LO + 1], shared_pack[0:HID, G_HI:G_HI + 1],
                                      ALU.max, ALU.min).then_inc(s_sh_clip, 1)
                if sh and part == 2:
                    wait_done(dve, s_sh_up, 1, sh.n)
                    wait_done(dve, s_sh_act, 1, sh.n, 1)
                    dve.tensor_scalar(sh_u[0:HID, :], psShU[0:HID, 0:L], shared_pack[0:HID, U_LO:U_LO + 1], shared_pack[0:HID, U_HI:U_HI + 1],
                                      ALU.max, ALU.min).then_inc(s_sh_clipu, 1)
                    wait_done(dve, s_sh_sig, 1, sh.n)
                    dve.scalar_tensor_tensor(sh_g[0:HID, :], sh_g[0:HID, :], shared_pack[0:HID, B_G:B_G + 1], sh_s[0:HID, :], ALU.add, ALU.mult).then_inc(s_sh_gated, 1)
                if sh and part == 3:
                    wait_done(dve, s_sh_gated, 1, sh.n)
                    wait_done(dve, s_sh_clipu, 1, sh.n)
                    wait_done(dve, s_sh_z, 1, sh.n, 1)
                    dve.scalar_tensor_tensor(sh_t[0:HID, :], sh_u[0:HID, :], shared_pack[0:HID, U_ADD:U_ADD + 1], sh_g[0:HID, :], ALU.add, ALU.mult).then_inc(s_sh_act, 1)
                if shp and part == 0:
                    wait_done(dve, s_sh_z, 1, shp.n)
                    r = H1[0:P, bass.ds(shp.n * (J * D), J * D)]
                    dve.tensor_tensor(r, r, psShZ[0:P, 0:J * D], ALU.add).then_inc(s_sh_add, 1)

            tile_iterations(dve, tile)

            def result(b):
                wait_done(dve, s_zz, 1, b.n)
                if b.reuses(2):
                    dve.wait_ge(s_out[b.parity], b.half * 16)
                dve.tensor_tensor(fin[0:P, b.parity, :], zz[0:P, b.parity, :], H1[0:P, bass.ds(b.n * (J * D), J * D)], ALU.add).then_inc(s_fin, 1)

            batches(dve, result)

    return nc


_INS = ['x', 'L0_tok_weight1', 'L0_attn_gamma', 'L0_attn_beta', 'L0_attn_wq', 'L0_attn_bq', 'L0_attn_wk', 'L0_attn_bk', 'L0_attn_wv', 'L0_attn_bv',
        'L0_attn_wp', 'L0_attn_bp', 'L0_ffn_gate_w', 'L0_ffn_gate_b', 'L0_ffn_shared_w1', 'L0_ffn_shared_b1', 'L0_ffn_shared_w2', 'L0_ffn_shared_b2',
        'L0_ffn_shared_act', 'L0_ffn_expert_w1', 'L0_ffn_expert_b1', 'L0_ffn_expert_w2', 'L0_ffn_expert_b2', 'L0_ffn_expert_act']


def kernel(**inputs):
    import numpy as _np
    import concourse.bacc as _bacc
    from concourse import mybir as _mybir
    from concourse.bass_utils import run_bass_kernel_spmd as _run

    nc = _bacc.Bacc("TRN2", target_bir_lowering=False, num_devices=1)
    arrays, args = {}, {}
    for name in _INS:
        v = _np.ascontiguousarray(inputs[name])
        arrays[f"in_{name}"] = v
        args[name] = nc.dram_tensor(f"in_{name}", v.shape, _mybir.dt.from_np(v.dtype), kind="ExternalInput").ap()
    b, rows, d = arrays["in_x"].shape
    out = nc.dram_tensor("out", (b, rows // 2, d), _mybir.dt.float32, kind="ExternalOutput").ap()
    audio_tower(nc, args, out)
    r = _run(nc, [arrays], core_ids=[0])
    return r.results[0]["out"]
```

```python
from contextlib import ExitStack

import concourse.bass as bass
from concourse import mybir

F32 = mybir.dt.float32
I32 = mybir.dt.int32
U32 = mybir.dt.uint32
BF16 = mybir.dt.bfloat16
ALU = mybir.AluOpType
ACT = mybir.ActivationFunctionType
AX = mybir.AxisListType.X

LN_EPS = 1e-5
GN_EPS = 1e-3
GN_GROUPS = 8
TOP_K = 2


class Turn:

    def __init__(self, c, m=None, step=1):
        self.c, self.m, self.step = c, m, step
        self.first = c if m is None else None
        self.n = c if m is None else m * step + c
        self.parity, self.half = self.place(2), self.round(2)

    def place(self, buffers):
        return self.c % buffers

    def round(self, buffers):
        return self.c // buffers if self.m is None else self.m * (self.step // buffers) + self.c // buffers

    def next(self):
        return Turn(self.c + 1, self.m, self.step)

    def reuses(self, buffers):
        return self.first is None or self.first >= buffers


def wait_done(eng, sem, per_turn, n, lag=0):
    value = (n + (1 - lag)) * per_turn
    if not isinstance(value, int) or value > 0:
        eng.wait_ge(sem, value)


def hold(eng, held):
    eng.sem_inc(held, 1)


class Steps:

    def __init__(self, sem, per_turn):
        self.sem, self.per_turn = sem, per_turn

    def begin(self, eng, n):
        self.eng, self.n, self.k = eng, n, 0

    def did(self, ins):
        ins.then_inc(self.sem, 1)
        self.k += 1
        assert self.k <= self.per_turn

    def settle(self):
        self.eng.wait_ge(self.sem, self.n * self.per_turn + self.k)

    def end(self):
        assert self.k == self.per_turn, (self.k, self.per_turn)


def audio_tower(nc, a, out):
    x = a["x"]
    B, ROWS, D = x.shape
    POOL = a["L0_tok_weight1"].shape[0]
    L = ROWS // POOL
    J = 3
    P = L // J
    E = a["L0_ffn_gate_w"].shape[1]
    HID = a["L0_ffn_shared_w2"].shape[0]
    N = B * L
    SCALE = float(D) ** -0.5
    XROW = POOL * D
    GC = D // GN_GROUPS
    assert P * J == L and D == 128 and P <= 128

    TILE = 256
    HALVES = TILE // 128
    NT = (TOP_K * N + E * (TILE - 1)) // TILE
    CAP = N + TILE
    PAD_ROW = E * CAP
    ROW = D + 2
    DEST, WEIGHT = D, D + 1
    SKIP = 1 << 20
    RING = 8
    AHEAD = 8
    ZRING = 4

    W2 = 2 * HID
    COLS = W2 + D
    B_G, U_ADD, ALPHA, ALPHA_B, G_LO, G_HI, U_LO, U_HI = range(COLS, COLS + 8)
    WP = COLS + 8

    with ExitStack() as ctx:
        def sb(name, shape, dt=F32):
            return ctx.enter_context(nc.sbuf_tensor(name, shape, dt))

        def sem(name):
            return ctx.enter_context(nc.semaphore(name))

        routed = nc.dram_tensor("routed", [E * CAP + TILE, ROW], F32, kind="Internal").ap()
        slots = nc.dram_tensor("slots", [TOP_K * N, D], F32, kind="Internal").ap()

        bank = [ctx.enter_context(nc.psum_tensor(f"bank{i}", [128, 512], F32)) for i in range(8)]

        ident = sb("ident", [128, 128])
        group_avg = sb("group_avg", [128, 128])
        before = sb("before", [128, 128], BF16)
        ones_bf = sb("ones_bf", [128, 128], BF16)
        iota_e = sb("iota_e", [128, E])
        base = sb("base", [128, E])
        base0 = sb("base0", [128, E])
        dest_id = sb("dest_id", [128, J * TOP_K], I32)
        eps = sb("eps", [128, 2])
        tile_no = sb("tile_no", [128, 1])
        wpool = sb("wpool", [128, XROW])
        gate_w = sb("gate_w", [128, E])
        gate_b = sb("gate_b", [128, E])
        wq = sb("wq", [128, D])
        wk = sb("wk", [128, D])
        wv = sb("wv", [128, D])
        wp = sb("wp", [128, D])
        wvT = sb("wvT", [128, D])
        wvp = sb("wvp", [128, D])
        vec = sb("vec", [128, 8])
        GAMMA, BETA, BQ, BK, BV, BQS = range(6)
        bv_cols = sb("bv_cols", [128, 128])
        out_bias = sb("out_bias", [128, D])
        pack = sb("pack", [128, (E + 1) * WP])
        b1 = sb("b1", [E + 1, W2])
        act_raw = sb("act_raw", [128, (E + 1) * 5])
        soft = sb("soft", [128, 4 * 2 * (E + 1)])
        b_up = sb("b_up", [128, E + 1])
        pads = sb("pads", [128, HALVES * ROW])

        xin = sb("xin", [128, 2, J * XROW])
        xm = sb("xm", [128, 2, J * XROW])
        nb1 = sb("nb1", [128, 2, J])
        nb2 = sb("nb2", [128, 2, J])
        h0 = sb("h0", [128, 2, J * D])
        st1 = sb("st1", [128, 2, J * 6])
        mv1 = sb("mv1", [128, 2, J * 2])
        rs1 = sb("rs1", [128, 2, 2 * J])
        ln1 = sb("ln1", [128, 2, J * D])
        gst = sb("gst", [128, 2, 8])
        gsm = sb("gsm", [128, 2, 2])
        gco = sb("gco", [128, 2, 12])
        hT = sb("hT", [128, 2, L])
        qT = sb("qT", [128, 2, L])
        kT = sb("kT", [128, 2, L])
        vs = sb("vs", [128, 2, J * D])
        nmax = sb("nmax", [128, 2, J])
        rsum = sb("rsum", [128, 2, J])
        rinv = sb("rinv", [128, 2, J])
        probs = sb("probs", [128, J, L])
        probsT = sb("probsT", [128, J, L])
        res = sb("res", [128, 2, J * D])
        h1 = sb("h1", [128, 2, J * D])
        st2 = sb("st2", [128, 2, J * 6])
        mv2 = sb("mv2", [128, 2, J * 2])
        rs2 = sb("rs2", [128, 2, 2 * J])
        xrow = sb("xrow", [128, 2, J * TOP_K * ROW])
        x2t = sb("x2t", [128, 2, L])
        lg = sb("lg", [128, J * E])
        mx = sb("mx", [128, J * 8])
        ix = sb("ix", [128, J * 8], U32)
        ixf = sb("ixf", [128, J * TOP_K])
        gap = sb("gap", [128, 2, 4 * J])
        hot = sb("hot", [128, 2, J * TOP_K * E])
        mask = sb("mask", [128, 2, J * E], BF16)
        posall = sb("posall", [128, J * E])
        posm = sb("posm", [128, J * TOP_K * E])
        posf = sb("posf", [128, J * TOP_K])
        pos = sb("pos", [128, 2, J * TOP_K], I32)

        H1 = sb("H1", [128, B * J * D])
        X2T = sb("X2T", [128, B * J * D])

        tab = sb("tab", [128, 16 * E])
        tabi = sb("tabi", [128, 2 * E], I32)
        where = sb("where", [1, 2 * 128], I32)
        ends = sb("ends", [1, E], I32)
        xs = sb("xs", [128, RING, HALVES * ROW])
        wt = sb("wt", [128, RING, WP])
        ys = sb("ys", [128, RING, HALVES * D])
        xt = sb("xt", [128, 2, TILE])
        hg = sb("hg", [128, 2, TILE])
        hu = sb("hu", [128, 2, TILE])
        sg = sb("sg", [128, 2, TILE])
        tt = sb("tt", [128, 2, TILE])
        sh_g = sb("sh_g", [128, L])
        sh_u = sb("sh_u", [128, L])
        sh_s = sb("sh_s", [128, L])
        sh_t = sb("sh_t", [128, L])
        z = sb("z", [128, ZRING, TOP_K, J * D])
        fin = sb("fin", [128, ZRING, J * D])

        s_const = sem("const_ready")
        s_clear = sem("pack_cleared")
        s_held_sp = sem("held_sp")
        s_held_dve = sem("held_dve")
        s_held_pool = sem("held_pool")
        s_params = sem("params_loaded")
        s_wpool = sem("pool_weights_loaded")
        s_late = sem("late_constants_ready")
        s_expw = sem("expert_weights_loaded")
        s_setup_pe = sem("setup_products")
        setup_dve = Steps(sem("setup_dve_steps"), 18)
        s_soft = sem("softplus_tail")
        s_x = [sem(f"x_loaded{q}") for q in range(2)]
        s_mul = sem("pool_products")
        s_h0 = sem("pooled")
        ln1_stats = Steps(sem("ln1_stats"), 2 * J)
        ln1_rstd = Steps(sem("ln1_rstd"), 2)
        s_ln1 = sem("ln1_applied")
        s_lnT = sem("ln1_transposed")
        gn_stats = Steps(sem("gn_channel_stats"), 3)
        s_group = sem("gn_group_means")
        gn_var = Steps(sem("gn_variance"), 2)
        gn_rstd = Steps(sem("gn_rstd"), 2)
        gn_coef = Steps(sem("gn_coefficients"), 3)
        s_hT = sem("h_ready")
        s_q = sem("q_product")
        s_k = sem("k_product")
        s_v = sem("v_product")
        s_qkv = sem("qkv_in_sbuf")
        s_S = sem("scores")
        s_nmax = sem("row_maxima")
        s_exp = sem("probabilities")
        s_PT = sem("probabilities_transposed")
        s_PTs = sem("transposed_in_sbuf")
        s_O = sem("attention_out")
        s_hback = sem("h_token_major")
        s_res = sem("residual_ready")
        s_rinv = sem("row_sums_inverted")
        s_h1 = sem("h1_ready")
        s_h1kept = [sem(f"h1_kept{q}") for q in range(2)]
        ln2_stats = Steps(sem("ln2_stats"), 2 * J)
        ln2_rstd = Steps(sem("ln2_rstd"), 2)
        s_ln2 = sem("ln2_applied")
        s_resid = sem("pooled_with_out_bias")
        s_nb1 = sem("ln1_offsets")
        s_nb2 = sem("ln2_offsets")
        s_x2T = sem("x2_transposed")
        s_x2t = sem("x2T_in_sbuf")
        s_x2kept = [sem(f"x2T_kept{q}") for q in range(2)]
        s_gate = sem("gate_logits")
        topk = Steps(sem("topk_steps"), 3 + 2 * J)
        s_gap = sem("second_weight_exp")
        topw = Steps(sem("top_weights_and_mask"), 5)
        s_rank = sem("ranks")
        place = Steps(sem("places"), 5)
        ids = Steps(sem("dest_ids_written"), 2)
        s_scat = [sem(f"rows_scattered{q}") for q in range(2)]

        table = Steps(sem("tile_table"), 24)
        s_ends = sem("expert_ends")
        s_row = sem("tile_table_row")
        s_pad = sem("pad_rows_written")
        s_sh_gate = sem("shared_gate_product")
        s_sh_up = sem("shared_up_product")
        s_sh_clip = sem("shared_gate_clipped")
        s_sh_clipu = sem("shared_up_clipped")
        s_sh_sig = sem("shared_sigmoid")
        s_sh_gated = sem("shared_gated")
        s_sh_act = sem("shared_activated")
        s_sh_z = sem("shared_out")
        s_sh_kept = sem("shared_kept")
        s_xs = [sem(f"tile_loaded{q}") for q in range(RING)]
        s_xT = sem("tile_transposed")
        s_xt = sem("tile_x_in_sbuf")
        s_hid = sem("tile_hidden")
        s_clip = sem("tile_gate_clipped")
        s_clipu = sem("tile_up_clipped")
        s_sig = sem("tile_sigmoid")
        s_gated = sem("tile_gated")
        s_act = sem("tile_activated")
        s_y = sem("tile_out")
        s_ys = sem("tile_weighted")
        s_back = [sem(f"tile_scattered{q}") for q in range(RING)]
        s_z = [sem(f"slots_loaded{q}") for q in range(ZRING)]
        s_zz = sem("slots_added")
        s_own = sem("residual_and_shared_added")
        s_fin = sem("result_ready")
        s_out = [sem(f"stored{q}") for q in range(ZRING)]

        def cols(t, b):
            return t[:, b.parity, :]

        psF, psG = bank[0], bank[0][:, 384:386]
        psQ, psK, psV = bank[1], bank[4], bank[3]
        psO = bank[3]
        psS = [bank[4], bank[5], bank[1]]
        psPT = [bank[6], bank[7]]
        psH = bank[5]
        psX = bank[2]
        psR = bank[2][:, 0:J * E]
        psTot = bank[2][:, J * E:(J + 1) * E]
        psL = bank[2][:, 384:384 + J * E]
        where_row = bank[0][0:1, 0:128]
        where_exp = bank[0][0:1, 128:256]

        N_CONST = 15
        N_LATE = 3 + HALVES
        N_PARAMS = 12
        N_EXPW = 10
        SETUP_ATTENTION = 5
        SETUP_ABS = 7
        TABLE_COLUMNS = 23
        CL = 2 * (E + 1)
        shared_pack = pack[:, E * WP:(E + 1) * WP]

        def w1_of(w, two):
            return w[:, 0:W2].rearrange("d (i two) -> d two i", two=2)[:, two, :]

        psXT = [bank[0], bank[1]]
        psHid = [bank[2], bank[3]]
        psY = [bank[4], bank[5]]
        psShG, psShU, psShZ = bank[6], bank[7], bank[6]

        def attention_iterations(eng, body):
            lo, hi = 3, B - 5
            assert (hi - lo) % 2 == 0

            def edge(i):
                body(*(Turn(n) if 0 <= n < B else None for n in (i + 3, i + 2, i + 1, i, i - 1, i - 2)))

            for i in range(-3, lo):
                edge(i)
            with eng.Fori(0, (hi - lo) // 2) as m:
                for i in (lo, lo + 1):
                    body(*(Turn(n, m, 2) for n in (i + 3, i + 2, i + 1, i, i - 1, i - 2)))
            for i in range(hi, B + 2):
                edge(i)

        def tile_iterations(eng, body):
            lo, total = AHEAD + 4, max(AHEAD + NT + 3, 4 * B + 4)
            loops = (min(AHEAD + NT, 4 * B) - lo) // RING

            def edge(u):
                tiles = (Turn(t) if 0 <= t < NT else None for t in range(u - AHEAD, u - AHEAD - 4, -1))
                now, last = u // 4, u // 4 - 1
                body(*tiles, u % 4, Turn(now) if now < B else None, Turn(last) if 0 <= last < B else None)

            for u in range(0, lo):
                edge(u)
            with eng.Fori(0, loops) as m:
                for u in range(lo, lo + RING):
                    tiles = (Turn(t, m, RING) for t in range(u - AHEAD, u - AHEAD - 4, -1))
                    body(*tiles, u % 4, Turn(u // 4, m, RING // 4), Turn(u // 4 - 1, m, RING // 4))
            for u in range(lo + RING * loops, total):
                edge(u)

        def batches(eng, body):
            for n in range(ZRING):
                body(Turn(n))
            with eng.Fori(0, (B - ZRING) // ZRING) as m:
                for n in range(ZRING, 2 * ZRING):
                    body(Turn(n, m, ZRING))

        def write_pads(eng, first):
            eng.wait_ge(s_late, N_LATE)
            eng.wait_ge(s_ends, 1)
            for e in range(first, E, 2):
                r = eng.value_load(ends[0:1, e:e + 1], min_val=0, max_val=E * CAP - TILE)
                eng.dma_start(routed[bass.ds(r, TILE), :].rearrange("(p h) c -> p (h c)", h=HALVES), pads[:]).then_inc(s_pad, 16)

        def setup_dve_done(eng):
            eng.wait_ge(setup_dve.sem, setup_dve.per_turn)

        block = ctx.enter_context(nc.Block())

        @block.sync
        def _(sp):
            def load_x(b):
                wait_done(sp, s_mul, 1, b.n, 2)
                sp.dma_start(xin[0:P, b.parity, :], x[bass.ds(b.n, 1)].rearrange("o (p r) d -> p (o r d)", p=P)).then_inc(s_x[b.parity], 16)

            load_x(Turn(0))
            sp.dma_start(wpool[0:P, :], a["L0_tok_weight1"].rearrange("(o p) d -> o (p d)", o=1).broadcast_to([P, XROW])).then_inc(s_wpool, 16)
            for t, name in ((wv, "wv"), (wp, "wp"), (wq, "wq"), (wk, "wk")):
                sp.dma_start(t[:], a["L0_attn_" + name]).then_inc(s_params, 16)
            params = a

            def load_experts(a=params):
                p3 = pack[:].rearrange("p (e c) -> p e c", c=WP)
                sp.dma_start(act_raw[:, 0:5 * E], a["L0_ffn_expert_act"].rearrange("(o e) f -> o (e f)", o=1).broadcast_to([128, 5 * E])).then_inc(s_expw, 16)
                sp.dma_start(act_raw[:, 5 * E:], a["L0_ffn_shared_act"].rearrange("(o f) -> o f", o=1).broadcast_to([128, 5])).then_inc(s_expw, 16)
                sp.dma_start(b1[0:E, :], a["L0_ffn_expert_b1"]).then_inc(s_expw, 16)
                sp.dma_start(b1[E:E + 1, :], a["L0_ffn_shared_b1"].rearrange("(o f) -> o f", o=1)).then_inc(s_expw, 16)
                sp.dma_start(p3[:, 0:E, 0:W2], a["L0_ffn_expert_w1"].rearrange("e d i -> d e i")).then_inc(s_expw, 16)
                sp.dma_start(p3[:, E, 0:W2], a["L0_ffn_shared_w1"]).then_inc(s_expw, 16)
                sp.dma_start(p3[0:HID, 0:E, W2:COLS], a["L0_ffn_expert_w2"].rearrange("e i d -> i e d")).then_inc(s_expw, 16)
                sp.dma_start(p3[0:HID, E, W2:COLS], a["L0_ffn_shared_w2"]).then_inc(s_expw, 16)
                sp.wait_ge(s_clear, 1)
                sp.dma_start(p3[HID:HID + 1, 0:E, W2:COLS], a["L0_ffn_expert_b2"].rearrange("(o e) d -> o e d", o=1)).then_inc(s_expw, 16)
                sp.dma_start(p3[HID:HID + 1, E, W2:COLS], a["L0_ffn_shared_b2"].rearrange("(o d) -> o d", o=1)).then_inc(s_expw, 16)

            def keep(a, b, c, d, k, r):
                if a:
                    if a.first != B - 1:
                        load_x(a.next())
                if k and k.first == B - 5:
                    load_experts()
                if k:
                    wait_done(sp, s_x2t, 1, k.n)
                    hold(sp, s_held_sp)
                    sp.dma_start(X2T[:, bass.ds(k.n * (J * D), L)], cols(x2t, k)).then_inc(s_x2kept[k.parity], 16)
                if d:
                    wait_done(sp, s_h1, J, d.n)
                    sp.dma_start(H1[0:P, bass.ds(d.n * (J * D), J * D)], h1[0:P, d.parity, :]).then_inc(s_h1kept[d.parity], 16)

            attention_iterations(sp, keep)

            write_pads(sp, 0)
            sp.dma_start(routed[PAD_ROW:PAD_ROW + TILE, :].rearrange("(p h) c -> p (h c)", h=HALVES), pads[:]).then_inc(s_pad, 16)
            sp.wait_ge(s_pad, 16 * (E + 1))
            wait_done(sp, table.sem, table.per_turn, 0)
            for q in range(2):
                sp.wait_ge(s_scat[q], 16 * J * TOP_K * (B // 2))

            setup_dve_done(sp)

            ahead = []

            def load_tile(x, h, g, y, part, sh, shp):
                if x:
                    q = x.place(RING)
                    if x.parity == 0:
                        _, ahead[:] = nc.values_load_multi_w_load_instructions(where[0:1, bass.ds(x.n * 2, 4)], engines=[mybir.EngineType.SP])
                    r = nc.s_assert_within(ahead[2 * x.parity], 0, PAD_ROW)
                    w = nc.s_assert_within(ahead[2 * x.parity + 1], 0, (E - 1) * WP)
                    if x.reuses(RING):
                        sp.wait_ge(s_back[q], x.round(RING) * (16 * HALVES))
                    sp.dma_start(xs[:, q, :], routed[bass.ds(r, TILE), :].rearrange("(p h) c -> p (h c)", h=HALVES)).then_inc(s_xs[q], 16)
                    sp.dma_start(wt[:, q, :], pack[:, bass.ds(w, WP)]).then_inc(s_xs[q], 16)

            tile_iterations(sp, load_tile)
            for q in range(RING):
                sp.wait_ge(s_back[q], 16 * HALVES * len(range(q, NT, RING)))

            def load_slots(b):
                wait_done(sp, s_fin, 1, b.n, ZRING)
                q = b.place(ZRING)
                sp.dma_start(z[0:P, q], slots.rearrange("(s n) d -> n s d", s=TOP_K)[bass.ds(b.n * L, L)]
                             .rearrange("(p j) s d -> p s j d", p=P)).then_inc(s_z[q], 16)

            batches(sp, load_slots)

        @block.gpsimd
        def _(pool):
            pool.memset(ident[:], 0.0).then_inc(s_const, 1)
            pool.memset(group_avg[:], 1.0 / GC).then_inc(s_const, 1)
            pool.memset(before[:], 1.0).then_inc(s_const, 1)
            pool.memset(ones_bf[:], 1.0).then_inc(s_const, 1)
            pool.memset(eps[:, 0:1], LN_EPS).then_inc(s_const, 1)
            pool.memset(eps[:, 1:2], GN_EPS).then_inc(s_const, 1)
            pool.iota(iota_e[:], pattern=[[1, E]], base=0, channel_multiplier=0, allow_small_or_imprecise_dtypes=True).then_inc(s_const, 1)
            pool.iota(base0[:], pattern=[[CAP, E]], base=0, channel_multiplier=0, allow_small_or_imprecise_dtypes=True).then_inc(s_const, 1)
            pool.iota(tile_no[:], pattern=[[0, 1]], base=0, channel_multiplier=1, allow_small_or_imprecise_dtypes=True).then_inc(s_const, 1)
            pool.iota(dest_id[:].rearrange("p (j k) -> p j k", k=TOP_K), pattern=[[1, J], [N, TOP_K]], base=0, channel_multiplier=J).then_inc(s_const, 1)
            pool.wait_ge(s_const, 10)
            pool.tensor_copy(base[:], base0[:]).then_inc(s_const, 1)
            pool.affine_select(out=ident[:], in_=ident[:], compare_op=ALU.not_equal, fill=1.0, base=0,
                               pattern=[[-1, 128]], channel_multiplier=1).then_inc(s_const, 1)
            pool.affine_select(out=before[:], in_=before[:], compare_op=ALU.is_gt, fill=0.0, base=0,
                               pattern=[[1, 128]], channel_multiplier=-1).then_inc(s_const, 1)
            g3 = group_avg[:].rearrange("p (g c) -> p g c", c=GC)
            pool.affine_select(out=g3, in_=g3, compare_op=ALU.is_ge, fill=0.0, base=0,
                               pattern=[[-GC, GN_GROUPS], [0, GC]], channel_multiplier=1).then_inc(s_const, 1)
            pool.wait_ge(s_const, 14)
            pool.affine_select(out=g3, in_=g3, compare_op=ALU.is_ge, fill=0.0, base=GC - 1,
                               pattern=[[GC, GN_GROUPS], [0, GC]], channel_multiplier=-1).then_inc(s_const, 1)

            def late_constants():
                wait_done(pool, s_h0, 1, 0)
                pool.memset(pack[:].rearrange("p (e c) -> p e c", c=WP)[HID:128, :, W2:WP], 0.0).then_inc(s_clear, 1)
                pool.wait_ge(s_clear, 1)
                pool.memset(pads[:], 0.0).then_inc(s_late, 1)
                pool.memset(tt[:], 1.0).then_inc(s_late, 1)
                pool.memset(sh_t[:], 1.0).then_inc(s_late, 1)
                pool.wait_ge(s_late, 3)
                for h in range(HALVES):
                    pool.memset(pads[:, h * ROW + DEST:h * ROW + DEST + 1].bitcast(I32), SKIP).then_inc(s_late, 1)
                pool.wait_ge(s_late, N_LATE)

            def rows_out(a, b, c, d, k, r):
                if a:
                    wait_done(pool, s_mul, 1, a.n)
                    wait_done(pool, s_ln1, J, a.n, 2)
                    wait_done(pool, s_resid, 1, a.n, 2)
                    v = xm[0:P, a.parity, :].rearrange("p (j r d) -> p j r d", j=J, r=POOL)
                    pool.tensor_tensor(h0[0:P, a.parity, :].rearrange("p (j d) -> p j d", j=J), v[:, :, 0, :], v[:, :, 1, :], ALU.add).then_inc(s_h0, 1)
                if r:
                    ids.begin(pool, r.n)
                    if r.reuses(2):
                        pool.wait_ge(s_scat[r.parity], r.half * (16 * J * TOP_K))
                    wait_done(pool, ids.sem, ids.per_turn, r.n, 1)
                    rows = xrow[0:P, r.parity, :].rearrange("p (s c) -> p s c", c=ROW)
                    hold(pool, s_held_pool)
                    ids.did(pool.tensor_copy(rows[:, :, DEST].bitcast(I32), dest_id[0:P, :]))
                    ids.settle()
                    hold(pool, s_held_pool)
                    ids.did(pool.tensor_scalar(dest_id[0:P, :], dest_id[0:P, :], L, None, ALU.add))
                    ids.end()
                    wait_done(pool, s_ln2, J, r.n)
                    wait_done(pool, topw.sem, topw.per_turn, r.n)
                    wait_done(pool, place.sem, place.per_turn, r.n)
                    hold(pool, s_held_pool)
                    for s in range(J * TOP_K):
                        pool.indirect_dma_start(out=routed[:, :], out_offset=bass.IndirectOffsetOnAxis(ap=pos[0:P, r.parity, s:s + 1], axis=0),
                                                in_=xrow[0:P, r.parity, s * ROW:(s + 1) * ROW], in_offset=None).then_inc(s_scat[r.parity], 16)
                if a and a.first == 0:
                    late_constants()
                    pool.wait_ge(setup_dve.sem, SETUP_ATTENTION)
                if a:
                    wait_done(pool, s_h0, 1, a.n)
                    hold(pool, s_held_pool)
                    pool.tensor_tensor(H1[0:P, bass.ds(a.n * (J * D), J * D)].rearrange("p (j d) -> p j d", j=J), h0[0:P, a.parity, :].rearrange("p (j d) -> p j d", j=J),
                                       out_bias[0:P, :].unsqueeze(1).broadcast_to([P, J, D]), ALU.add).then_inc(s_resid, 1)

            attention_iterations(pool, rows_out)

            def scatter_tile(x, h, g, y, part, sh, shp):
                if y:
                    q = y.place(RING)
                    wait_done(pool, s_ys, HALVES, y.n)
                    hold(pool, s_held_pool)
                    for h in range(HALVES):
                        pool.indirect_dma_start(out=slots[:, :], out_offset=bass.IndirectOffsetOnAxis(ap=xs[:, q, h * ROW + DEST:h * ROW + DEST + 1].bitcast(I32), axis=0),
                                                in_=ys[:, q, h * D:(h + 1) * D], in_offset=None,
                                                bounds_check=TOP_K * N - 1, oob_is_err=False).then_inc(s_back[q], 16)

            tile_iterations(pool, scatter_tile)

            def add_slots(b):
                q = b.place(ZRING)
                pool.wait_ge(s_z[q], (b.round(ZRING) + 1) * 16)
                hold(pool, s_held_pool)
                pool.tensor_tensor(z[0:P, q, 0], z[0:P, q, 0], z[0:P, q, 1], ALU.add).then_inc(s_zz, 1)

            batches(pool, add_slots)

        @block.tensor
        def _(pe):
            pe.wait_ge(s_const, N_CONST)
            pe.wait_ge(s_params, 16 * N_PARAMS)
            pe.transpose(bank[0][:, 0:D], wv[:], ident[:]).then_inc(s_setup_pe, 1)
            pe.wait_ge(setup_dve.sem, 2)
            pe.matmul(bank[1][:, 0:D], wvT[:], wp[:], start=True, stop=True)
            pe.matmul(bank[1][:, D:2 * D], bv_cols[:], wp[:], start=True, stop=True).then_inc(s_setup_pe, 1)

            def expert_biases():
                pe.wait_ge(s_expw, 16 * N_EXPW)
                b1v = b1[:].rearrange("e (i two) -> e two i", two=2)
                for two in range(2):
                    last = pe.transpose(bank[0][0:HID, two * 32:two * 32 + E + 1], b1v[:, two, :], ident[0:E + 1, 0:E + 1])
                last.then_inc(s_setup_pe, 1)

            def body(a, b, c, d, k, r):
                if k and k.first == B - 2:
                    expert_biases()
                if c and c.first == 0:
                    pe.wait_ge(setup_dve.sem, SETUP_ATTENTION)
                def transpose_probs(j):
                    pe.wait_ge(s_exp, d.n * J + (j + 1))
                    if j == 2:
                        pe.wait_ge(s_PTs, d.n * J + 1)
                    elif d.reuses(1):
                        pe.wait_ge(s_PTs, d.n * J - j)
                    for i in range(J):
                        last = pe.transpose(psPT[j % 2][0:P, i * P:(i + 1) * P], probs[0:P, j, i * P:(i + 1) * P], ident[0:P, 0:P])
                    last.then_inc(s_PT, 1)

                def attend(j):
                    wait_done(pe, s_PTs, 1, d.n * J + j)
                    if j == 0:
                        pe.wait_ge(s_qkv, c.n * 3 + 1 if c else (d.n + 1) * 3)
                    for i in range(J):
                        last = pe.matmul(psO[0:P, j * D:(j + 1) * D], probsT[0:P, j, i * P:(i + 1) * P], vs[0:P, d.parity, i * D:(i + 1) * D],
                                         start=(i == 0), stop=(i == J - 1))
                    last.then_inc(s_O, 1)

                if c:
                    wait_done(pe, s_hT, 1, c.n)
                    wait_done(pe, s_h1, J, c.n, 2)
                    for j in range(J):
                        last = pe.matmul(psV[0:P, j * D:(j + 1) * D], hT[:, c.parity, j * P:(j + 1) * P], wvp[:], start=True, stop=True)
                    last.then_inc(s_v, 1)
                if b:
                    wait_done(pe, s_ln1, J, b.n)
                    wait_done(pe, s_hT, 1, b.n, 1)
                    for j in range(J):
                        last = pe.transpose(psF[:, j * P:(j + 1) * P], ln1[0:P, b.parity, j * D:(j + 1) * D], ident[0:P, 0:P])
                    last.then_inc(s_lnT, 1)
                if d:
                    transpose_probs(0)
                if c:
                    if c.reuses(1):
                        pe.wait_ge(s_exp, (c.n - 1) * J + 1)
                    pe.matmul(psK[:, 0:L], wk[:], cols(hT, c), start=True, stop=True).then_inc(s_k, 1)
                if d:
                    transpose_probs(1)
                if r:
                    wait_done(pe, topw.sem, topw.per_turn, r.n)
                    mk = mask[0:P, r.parity, :]
                    for j in range(J):
                        for i in range(j):
                            pe.matmul(psR[0:P, j * E:(j + 1) * E], ones_bf[0:P, 0:P], mk[:, i * E:(i + 1) * E], start=(i == 0), stop=False)
                        pe.matmul(psR[0:P, j * E:(j + 1) * E], before[0:P, 0:P], mk[:, j * E:(j + 1) * E], start=(j == 0), stop=True)
                    for j in range(J):
                        last = pe.matmul(psTot[:, :], ones_bf[0:P, :], mk[:, j * E:(j + 1) * E], start=(j == 0), stop=(j == J - 1))
                    last.then_inc(s_rank, 1)
                if d:
                    for j in range(J):
                        last = pe.transpose(psH[0:P, j * D:(j + 1) * D], hT[:, d.parity, j * P:(j + 1) * P], ident[:])
                    last.then_inc(s_hback, 1)
                if c:
                    wait_done(pe, s_exp, J, c.n, 1)
                    pe.matmul(psQ[:, 0:L], wq[:], cols(hT, c), start=True, stop=True).then_inc(s_q, 1)
                if d:
                    transpose_probs(2)
                if b:
                    wait_done(pe, gn_stats.sem, gn_stats.per_turn, b.n)
                    pe.matmul(psG, group_avg[:], gst[:, b.parity, 6:8], start=True, stop=True).then_inc(s_group, 1)
                if d:
                    attend(0)
                if d:
                    attend(1)
                if d:
                    attend(2)
                def scores(j):
                    pe.matmul(psS[j][0:P, 0:L], qT[:, c.parity, j * P:(j + 1) * P], cols(kT, c), start=True, stop=True).then_inc(s_S, 1)

                if c:
                    wait_done(pe, s_qkv, 3, c.n)
                    wait_done(pe, s_res, 1, c.n, 1)
                    scores(0)
                if k:
                    wait_done(pe, s_ln2, J, k.n)
                    if k.reuses(1):
                        pe.wait_ge(place.sem, (k.n - 1) * place.per_turn + 2)
                    for j in range(J):
                        last = pe.transpose(psX[:, j * P:(j + 1) * P], xrow[0:P, k.parity, j * TOP_K * ROW:j * TOP_K * ROW + D], ident[0:P, 0:P])
                    last.then_inc(s_x2T, 1)
                if k:
                    wait_done(pe, s_x2t, 1, k.n)
                    for j in range(J):
                        last = pe.matmul(psL[0:P, j * E:(j + 1) * E], x2t[:, k.parity, j * P:(j + 1) * P], gate_w[:], start=True, stop=True)
                    last.then_inc(s_gate, 1)
                if c:
                    scores(1)
                if c:
                    scores(2)

            attention_iterations(pe, body)

            pe.wait_ge(table.sem, TABLE_COLUMNS)
            pe.matmul(where_row, tab[:, 0:1], ident[:], start=True, stop=True)
            pe.matmul(where_exp, tab[:, 1:2], ident[:], start=True, stop=True).then_inc(s_row, 1)

            for q in range(2):
                pe.wait_ge(s_x2kept[q], 16 * (B // 2))
            setup_dve_done(pe)
            pe.wait_ge(s_late, N_LATE)
            wait_done(pe, table.sem, table.per_turn, 0)

            def tile(x, h, g, y, part, sh, shp):
                if h:
                    q = h.place(RING)
                    wait_done(pe, s_xt, 1, h.n)
                    wait_done(pe, s_clipu, 1, h.n, 2)
                    for two in range(2):
                        last = pe.matmul(psHid[h.parity][0:HID, two * TILE:(two + 1) * TILE], w1_of(wt[:, q, :], two), xt[:, h.parity, :], start=True, stop=True)
                    last.then_inc(s_hid, 1)
                if x:
                    q = x.place(RING)
                    pe.wait_ge(s_xs[q], (x.round(RING) + 1) * 32)
                    wait_done(pe, s_xt, 1, x.n, 2)
                    for k in range(HALVES):
                        last = pe.transpose(psXT[x.parity][:, k * 128:(k + 1) * 128], xs[:, q, k * ROW:k * ROW + D], ident[:])
                    last.then_inc(s_xT, 1)
                if y:
                    q = y.place(RING)
                    wait_done(pe, s_act, 1, y.n)
                    wait_done(pe, s_ys, HALVES, y.n, 2)
                    for k in range(HALVES):
                        last = pe.matmul(psY[y.parity][:, k * D:(k + 1) * D], tt[0:HID + 1, y.parity, k * 128:(k + 1) * 128],
                                         wt[0:HID + 1, q, W2:W2 + D], start=True, stop=True)
                    last.then_inc(s_y, 1)
                if sh and part == 0:
                    wait_done(pe, s_sh_clip, 1, sh.n, 1)
                    wait_done(pe, s_sh_kept, 1, sh.n, 2)
                    pe.matmul(psShG[0:HID, 0:L], w1_of(shared_pack, 0), X2T[:, bass.ds(sh.n * (J * D), L)], start=True, stop=True).then_inc(s_sh_gate, 1)
                if sh and part == 1:
                    wait_done(pe, s_sh_clipu, 1, sh.n, 1)
                    pe.matmul(psShU[0:HID, 0:L], w1_of(shared_pack, 1), X2T[:, bass.ds(sh.n * (J * D), L)], start=True, stop=True).then_inc(s_sh_up, 1)
                if shp and part == 2:
                    wait_done(pe, s_sh_act, 1, shp.n)
                    pe.wait_ge(s_sh_clip, sh.n + 1 if sh else B)
                    for j in range(J):
                        last = pe.matmul(psShZ[0:P, j * D:(j + 1) * D], sh_t[0:HID + 1, j * P:(j + 1) * P],
                                         shared_pack[0:HID + 1, W2:W2 + D], start=True, stop=True)
                    last.then_inc(s_sh_z, 1)

            tile_iterations(pe, tile)

        @block.scalar
        def _(act):
            act.preload_act_table_set("natural_log_exp_and_others")
            for c, name in ((BV, "bv"), (BQ, "bq"), (BK, "bk"), (GAMMA, "gamma"), (BETA, "beta")):
                act.dma_start(vec[:, c:c + 1], a["L0_attn_" + name].rearrange("(d o) -> d o", o=1)).then_inc(s_params, 16)
            act.dma_start(out_bias[:], a["L0_attn_bp"].rearrange("(o d) -> o d", o=1).broadcast_to([128, D])).then_inc(s_params, 16)
            act.dma_start(gate_w[:], a["L0_ffn_gate_w"]).then_inc(s_params, 16)
            act.dma_start(gate_b[:], a["L0_ffn_gate_b"].rearrange("(o e) -> o e", o=1).broadcast_to([128, E])).then_inc(s_params, 16)
            act.wait_ge(s_const, N_CONST)

            def rstd(steps, b, out_ln, out_rstd, var, scale, eps_col):
                steps.begin(act, b.n)
                steps.did(act.activation(out_ln, var, ACT.Ln, scale=scale, bias=eps_col))
                steps.settle()
                steps.did(act.activation(out_rstd, out_ln, ACT.Exp, scale=-0.5))
                steps.end()

            def ln_apply(b, dst, copies, stride, src, nb, rs, done):
                for j in range(J):
                    o = dst[0:P, b.parity, j * copies * stride:(j + 1) * copies * stride].rearrange("p (s c) -> p s c", s=copies)[:, :, 0:D]
                    i = src[0:P, b.parity, j * D:(j + 1) * D].unsqueeze(1).broadcast_to([P, copies, D])
                    act.activation(o, i, ACT.Identity, scale=rs[0:P, b.parity, J + j:J + j + 1], bias=nb[0:P, b.parity, j:j + 1]).then_inc(done, 1)

            def softplus_tail():
                act.wait_ge(setup_dve.sem, SETUP_ABS)
                act.activation(soft[:, 2 * CL:3 * CL], soft[:, CL:2 * CL], ACT.Exp).then_inc(s_soft, 1)
                act.wait_ge(s_soft, 1)
                act.activation(soft[:, 3 * CL:4 * CL], soft[:, 2 * CL:3 * CL], ACT.Ln, bias=1.0).then_inc(s_soft, 1)

            def body(a, b, c, d, k, r):
                if k and k.first == B - 2:
                    softplus_tail()
                if c and c.first == 0:
                    act.wait_ge(setup_dve.sem, SETUP_ATTENTION)
                def copy_probs(j):
                    wait_done(act, s_PT, 1, d.n * J + j)
                    if d.reuses(1):
                        act.wait_ge(s_O, (d.n - 1) * J + (j + 1))
                    act.activation(probsT[0:P, j, :], psPT[j % 2][0:P, 0:L], ACT.Copy).then_inc(s_PTs, 1)

                if d:
                    copy_probs(0)
                if c:
                    wait_done(act, s_v, 1, c.n)
                    act.activation(vs[0:P, c.parity, :], psV[0:P, 0:J * D], ACT.Copy).then_inc(s_qkv, 1)
                if d:
                    copy_probs(1)
                if k:
                    wait_done(act, s_nb2, 1, k.n)
                    if k.reuses(2):
                        act.wait_ge(s_scat[k.parity], k.half * (16 * J * TOP_K))
                    ln_apply(k, xrow, TOP_K, ROW, h1, nb2, rs2, s_ln2)
                if d:
                    copy_probs(2)
                if c:
                    wait_done(act, s_k, 1, c.n)
                    act.activation(cols(kT, c), psK[:, 0:L], ACT.Identity, bias=vec[:, BK:BK + 1]).then_inc(s_qkv, 1)
                if c:
                    wait_done(act, s_q, 1, c.n)
                    act.activation(cols(qT, c), psQ[:, 0:L], ACT.Identity, scale=SCALE, bias=vec[:, BQS:BQS + 1]).then_inc(s_qkv, 1)
                if b:
                    wait_done(act, gn_var.sem, gn_var.per_turn, b.n)
                    g = gco[:, b.parity, :]
                    rstd(gn_rstd, b, g[:, 1:2], g[:, 2:3], g[:, 0:1], -1.0, eps[:, 1:2])
                if a:
                    wait_done(act, ln1_stats.sem, ln1_stats.per_turn, a.n)
                    rs = rs1[0:P, a.parity, :]
                    rstd(ln1_rstd, a, rs[:, 0:J], rs[:, J:2 * J], mv1[0:P, a.parity, :].rearrange("p (j s) -> p s j", s=2)[:, 1, :], 1.0, eps[0:P, 0:1])
                if k:
                    wait_done(act, s_x2T, 1, k.n)
                    if k.reuses(2):
                        act.wait_ge(s_x2kept[k.parity], k.half * 16)
                    act.activation(cols(x2t, k), psX[:, 0:L], ACT.Copy).then_inc(s_x2t, 1)
                if d:
                    wait_done(act, ln2_stats.sem, ln2_stats.per_turn, d.n)
                    rs = rs2[0:P, d.parity, :]
                    rstd(ln2_rstd, d, rs[:, 0:J], rs[:, J:2 * J], mv2[0:P, d.parity, :].rearrange("p (j s) -> p s j", s=2)[:, 1, :], 1.0, eps[0:P, 0:1])
                if b:
                    wait_done(act, gn_coef.sem, gn_coef.per_turn, b.n)
                    act.activation(cols(hT, b), psF[:, 0:L], ACT.Identity, scale=g[:, 3:4], bias=g[:, 5:6]).then_inc(s_hT, 1)
                if a:
                    wait_done(act, s_nb1, 1, a.n)
                    ln_apply(a, ln1, 1, D, h0, nb1, rs1, s_ln1)
                if k:
                    wait_done(act, topk.sem, topk.per_turn, k.n)
                    act.activation(gap[0:P, k.parity, J:2 * J], gap[0:P, k.parity, 0:J], ACT.Exp).then_inc(s_gap, 1)
                if c:
                    for j in range(J):
                        wait_done(act, s_nmax, 1, c.n * J + j)
                        if c.reuses(1):
                            act.wait_ge(s_PT, (c.n - 1) * J + (j + 1))
                        act.activation(probs[0:P, j, :], psS[j][0:P, 0:L], ACT.Exp, bias=nmax[0:P, c.parity, j:j + 1],
                                       accum_out=rsum[0:P, c.parity, j:j + 1]).then_inc(s_exp, 1)

            attention_iterations(act, body)

            write_pads(act, 1)

            act.preload_act_table_set("sigmoid_and_others")

            setup_dve_done(act)

            def tile(x, h, g, y, part, sh, shp):
                if x:
                    wait_done(act, s_xT, 1, x.n)
                    wait_done(act, s_hid, 1, x.n, 2)
                    act.activation(xt[:, x.parity, :], psXT[x.parity][:, 0:TILE], ACT.Copy).then_inc(s_xt, 1)
                if y:
                    q = y.place(RING)
                    wait_done(act, s_y, 1, y.n)
                    if y.reuses(RING):
                        act.wait_ge(s_back[q], y.round(RING) * (16 * HALVES))
                    for k in range(HALVES):
                        act.activation(ys[:, q, k * D:(k + 1) * D], psY[y.parity][:, k * D:(k + 1) * D], ACT.Copy,
                                       scale=xs[:, q, k * ROW + WEIGHT:k * ROW + WEIGHT + 1]).then_inc(s_ys, 1)
                if h:
                    w = wt[:, h.place(RING), :]
                    wait_done(act, s_clip, 1, h.n)
                    wait_done(act, s_gated, 1, h.n, 2)
                    act.activation(sg[0:HID, h.parity, :], hg[0:HID, h.parity, :], ACT.Sigmoid,
                                   scale=w[0:HID, ALPHA:ALPHA + 1], bias=w[0:HID, ALPHA_B:ALPHA_B + 1]).then_inc(s_sig, 1)
                if sh and part == 2:
                    wait_done(act, s_sh_clip, 1, sh.n)
                    wait_done(act, s_sh_gated, 1, sh.n, 1)
                    act.activation(sh_s[0:HID, :], sh_g[0:HID, :], ACT.Sigmoid,
                                   scale=shared_pack[0:HID, ALPHA:ALPHA + 1], bias=shared_pack[0:HID, ALPHA_B:ALPHA_B + 1]).then_inc(s_sh_sig, 1)
                if shp and part == 3:
                    wait_done(act, s_sh_z, 1, shp.n)
                    act.activation(X2T[0:P, bass.ds(shp.n * (J * D), J * D)], psShZ[0:P, 0:J * D], ACT.Copy).then_inc(s_sh_kept, 1)

            tile_iterations(act, tile)

            def store(b):
                wait_done(act, s_fin, 1, b.n)
                act.dma_start(out[bass.ds(b.n, 1)].rearrange("o (p j) d -> p (o j d)", p=P), fin[0:P, b.place(ZRING), :]).then_inc(s_out[b.place(ZRING)], 16)

            batches(act, store)
            for q in range(ZRING):
                act.wait_ge(s_out[q], 16 * (B // ZRING))

        @block.vector
        def _(dve):
            dve.wait_ge(s_const, N_CONST)
            setup = setup_dve
            setup.begin(dve, 0)

            def attention_setup():
                dve.wait_ge(s_params, 16 * N_PARAMS)
                setup.did(dve.tensor_copy(bv_cols[:], vec[:, BV:BV + 1].broadcast_to([128, 128])))
                dve.wait_ge(s_setup_pe, 1)
                setup.did(dve.tensor_copy(wvT[:], bank[0][:, 0:D]))
                dve.wait_ge(s_setup_pe, 2)
                setup.did(dve.tensor_copy(wvp[:], bank[1][:, 0:D]))
                setup.did(dve.tensor_tensor(out_bias[:], bank[1][:, D:2 * D], out_bias[:], ALU.add))
                setup.did(dve.tensor_scalar(vec[:, BQS:BQS + 1], vec[:, BQ:BQ + 1], SCALE, None, ALU.mult))
                setup.settle()
                assert setup.k == SETUP_ATTENTION

            def ln_stats(steps, b, src, st, mv):
                steps.begin(dve, b.n)
                for j in range(J):
                    steps.did(dve.bn_stats(st[0:P, b.parity, j * 6:(j + 1) * 6], src[0:P, b.parity, j * D:(j + 1) * D]))
                steps.settle()
                hold(dve, s_held_dve)
                for j in range(J):
                    steps.did(dve.bn_aggr(mv[0:P, b.parity, j * 2:(j + 1) * 2], st[0:P, b.parity, j * 6:(j + 1) * 6]))
                steps.end()

            def offsets(b, nb, mv, rs, done):
                dve.scalar_tensor_tensor(nb[0:P, b.parity, :], mv[0:P, b.parity, :].rearrange("p (j s) -> p s j", s=2)[:, 0, :], -1.0,
                                         rs[0:P, b.parity, J:2 * J], ALU.mult, ALU.mult).then_inc(done, 1)

            def expert_setup():
                p3 = pack[:].rearrange("p (e c) -> p e c", c=WP)
                dve.wait_ge(s_expw, 16 * N_EXPW)
                acts = act_raw[:].rearrange("p (e f) -> p f e", f=5)
                raw = acts[:, 3:5, :]

                def part(i):
                    return soft[:, i * CL:(i + 1) * CL].rearrange("p (f e) -> p f e", f=2)

                setup.did(dve.tensor_scalar(part(0), raw, -1.0, None, ALU.mult))
                setup.settle()
                setup.did(dve.tensor_tensor(part(1), raw, part(0), ALU.min))
                assert setup.k == SETUP_ABS
                dve.wait_ge(s_setup_pe, 3)
                b_gate = p3[0:HID, :, B_G]
                setup.did(dve.tensor_copy(b_gate, bank[0][0:HID, 0:E + 1]))
                setup.did(dve.tensor_copy(b_up[0:HID, :], bank[0][0:HID, 32:32 + E + 1]))
                dve.wait_ge(s_soft, 2)
                setup.settle()
                setup.did(dve.scalar_tensor_tensor(part(1), raw, 0.0, part(3), ALU.max, ALU.add))
                setup.did(dve.tensor_copy(p3[0:HID, :, ALPHA], acts[0:HID, 0, :]))
                setup.did(dve.tensor_tensor(p3[0:HID, :, ALPHA_B], acts[0:HID, 0, :], b_gate, ALU.mult))
                setup.did(dve.tensor_tensor(p3[0:HID, :, U_ADD], acts[0:HID, 2, :], b_up[0:HID, :], ALU.add))
                w2 = p3[0:HID, :, W2:COLS]
                setup.did(dve.tensor_tensor(w2, w2, acts[0:HID, 1, :].unsqueeze(2).broadcast_to([HID, E + 1, D]), ALU.mult))
                setup.settle()
                for f, bias, lo, hi in ((0, b_gate, G_LO, G_HI), (1, b_up[0:HID, :], U_LO, U_HI)):
                    setup.did(dve.tensor_tensor(p3[0:HID, :, hi], part(1)[0:HID, f, :], bias, ALU.subtract))
                    setup.did(dve.scalar_tensor_tensor(p3[0:HID, :, lo], part(1)[0:HID, f, :], -1.0, bias, ALU.mult, ALU.subtract))
                setup.settle()
                setup.end()

            def body(a, b, c, d, k, r):
                if k and k.first == B - 2:
                    expert_setup()
                if a and a.first == 0:
                    dve.wait_ge(s_wpool, 16)
                if a and a.first == 1:
                    attention_setup()
                def row_max(j):
                    wait_done(dve, s_S, 1, c.n * J + j)
                    dve.tensor_reduce(nmax[0:P, c.parity, j:j + 1], psS[j][0:P, 0:L], AX, ALU.max, negate=True).then_inc(s_nmax, 1)

                if a:
                    dve.wait_ge(s_x[a.parity], (a.half + 1) * 16)
                    wait_done(dve, s_h0, 1, a.n, 2)
                    dve.tensor_tensor(xm[0:P, a.parity, :].rearrange("p (j c) -> p j c", j=J), xin[0:P, a.parity, :].rearrange("p (j c) -> p j c", j=J),
                                      wpool[0:P, :].unsqueeze(1).broadcast_to([P, J, XROW]), ALU.mult).then_inc(s_mul, 1)
                if k:
                    wait_done(dve, ln2_rstd.sem, ln2_rstd.per_turn, k.n)
                    offsets(k, nb2, mv2, rs2, s_nb2)
                if d:
                    wait_done(dve, s_exp, J, d.n)
                    dve.reciprocal(rinv[0:P, d.parity, :], rsum[0:P, d.parity, :]).then_inc(s_rinv, 1)
                if b:
                    g, gm, gc = gst[:, b.parity, :], gsm[:, b.parity, :], gco[:, b.parity, :]
                    wait_done(dve, s_lnT, 1, b.n)
                    gn_stats.begin(dve, b.n)
                    gn_stats.did(dve.bn_stats(g[:, 0:6], psF[:, 0:L]))
                    gn_stats.settle()
                    hold(dve, s_held_dve)
                    gn_stats.did(dve.bn_aggr(g[:, 6:8], g[:, 0:6]))
                    gn_stats.settle()
                    gn_stats.did(dve.scalar_tensor_tensor(g[:, 7:8], g[:, 6:7], g[:, 6:7], g[:, 7:8], ALU.mult, ALU.add))
                    gn_stats.end()
                if d:
                    wait_done(dve, s_hback, 1, d.n)
                    wait_done(dve, s_resid, 1, d.n)
                    dve.tensor_tensor(res[0:P, d.parity, :], psH[0:P, 0:J * D], H1[0:P, bass.ds(d.n * (J * D), J * D)], ALU.add).then_inc(s_res, 1)
                if r:
                    wait_done(dve, s_rank, 1, r.n)
                    place.begin(dve, r.n)
                    hr = hot[0:P, r.parity, :]
                    place.did(dve.tensor_tensor(posall[0:P, :].rearrange("p (j e) -> p j e", e=E), psR[0:P, :].rearrange("p (j e) -> p j e", e=E),
                                                base[0:P, :].unsqueeze(1).broadcast_to([P, J, E]), ALU.add))
                    place.settle()
                    place.did(dve.tensor_tensor(base[:], base[:], psTot, ALU.add))
                    place.did(dve.tensor_tensor(posm[0:P, :].rearrange("p (j s e) -> p j s e", s=TOP_K, e=E), hr.rearrange("p (j s e) -> p j s e", s=TOP_K, e=E),
                                                posall[0:P, :].rearrange("p (j e) -> p j e", e=E).unsqueeze(2).broadcast_to([P, J, TOP_K, E]), ALU.mult))
                    place.settle()
                    place.did(dve.tensor_reduce(posf[0:P, :], posm[0:P, :].rearrange("p (s e) -> p s e", e=E), AX, ALU.add))
                    place.settle()
                    place.did(dve.tensor_copy(pos[0:P, r.parity, :], posf[0:P, :]))
                    place.end()
                if b:
                    wait_done(dve, s_group, 1, b.n)
                    gn_var.begin(dve, b.n)
                    gn_var.did(dve.tensor_copy(gm, psG))
                    gn_var.settle()
                    gn_var.did(dve.scalar_tensor_tensor(gc[:, 0:1], gm[:, 0:1], gm[:, 0:1], gm[:, 1:2], ALU.mult, ALU.subtract))
                    gn_var.end()
                if a:
                    wait_done(dve, s_h0, 1, a.n)
                    ln_stats(ln1_stats, a, h0, st1, mv1)
                if d:
                    wait_done(dve, s_rinv, 1, d.n)
                    if d.reuses(2):
                        dve.wait_ge(s_h1kept[d.parity], d.half * 16)
                    wait_done(dve, s_O, J, d.n)
                    for j in range(J):
                        dve.scalar_tensor_tensor(h1[0:P, d.parity, j * D:(j + 1) * D], psO[0:P, j * D:(j + 1) * D], rinv[0:P, d.parity, j:j + 1],
                                                 res[0:P, d.parity, j * D:(j + 1) * D], ALU.mult, ALU.add).then_inc(s_h1, 1)
                if d:
                    wait_done(dve, s_h1, J, d.n)
                    ln_stats(ln2_stats, d, h1, st2, mv2)
                if b:
                    wait_done(dve, gn_rstd.sem, gn_rstd.per_turn, b.n)
                    gn_coef.begin(dve, b.n)
                    gn_coef.did(dve.tensor_tensor(gc[:, 3:4], gc[:, 2:3], vec[:, GAMMA:GAMMA + 1], ALU.mult))
                    gn_coef.settle()
                    gn_coef.did(dve.tensor_tensor(gc[:, 4:5], gm[:, 0:1], gc[:, 3:4], ALU.mult))
                    gn_coef.settle()
                    gn_coef.did(dve.tensor_tensor(gc[:, 5:6], vec[:, BETA:BETA + 1], gc[:, 4:5], ALU.subtract))
                    gn_coef.end()
                if a:
                    wait_done(dve, ln1_rstd.sem, ln1_rstd.per_turn, a.n)
                    offsets(a, nb1, mv1, rs1, s_nb1)
                if k:
                    wait_done(dve, s_gate, 1, k.n)
                    topk.begin(dve, k.n)
                    topk.did(dve.tensor_tensor(lg[0:P, :].rearrange("p (j e) -> p j e", e=E), psL[0:P, :].rearrange("p (j e) -> p j e", e=E),
                                               gate_b[0:P, :].unsqueeze(1).broadcast_to([P, J, E]), ALU.add))
                if c:
                    row_max(0)
                if k:
                    topk.settle()
                    hold(dve, s_held_dve)
                    for j in range(J):
                        topk.did(dve.max(mx[0:P, j * 8:(j + 1) * 8], lg[0:P, j * E:(j + 1) * E]))
                if c:
                    row_max(1)
                if k:
                    topk.settle()
                    hold(dve, s_held_dve)
                    for j in range(J):
                        topk.did(dve.max_index(ix[0:P, j * 8:(j + 1) * 8], mx[0:P, j * 8:(j + 1) * 8], lg[0:P, j * E:(j + 1) * E]))
                    m3 = mx[0:P, :].rearrange("p (j s) -> p s j", s=8)
                    gp = gap[0:P, k.parity, :]
                    topk.did(dve.tensor_tensor(gp[:, 0:J], m3[:, 1, :], m3[:, 0, :], ALU.subtract))
                    topk.settle()
                    topk.did(dve.tensor_copy(ixf[0:P, :].rearrange("p (j s) -> p j s", s=TOP_K), ix[0:P, :].rearrange("p (j s) -> p j s", s=8)[:, :, 0:TOP_K]))
                    topk.end()
                if c:
                    row_max(2)
                if k:
                    topk.settle()
                    wait_done(dve, s_gap, 1, k.n)
                    topw.begin(dve, k.n)
                    rows = xrow[0:P, k.parity, :].rearrange("p (j s c) -> p s c j", j=J, s=TOP_K)
                    topw.did(dve.tensor_scalar(gp[:, 2 * J:3 * J], gp[:, J:2 * J], 1.0, None, ALU.add))
                    hk = hot[0:P, k.parity, :]
                    topw.did(dve.tensor_tensor(hk.rearrange("p (j s e) -> p (j s) e", s=TOP_K, e=E), iota_e[0:P, :].unsqueeze(1).broadcast_to([P, J * TOP_K, E]),
                                               ixf[0:P, :].unsqueeze(2).broadcast_to([P, J * TOP_K, E]), ALU.is_equal))
                    topw.settle()
                    topw.did(dve.reciprocal(rows[:, 0, WEIGHT, :], gp[:, 2 * J:3 * J]))
                    hs = hk.rearrange("p (j s e) -> p s j e", s=TOP_K, e=E)
                    topw.did(dve.tensor_tensor(mask[0:P, k.parity, :].rearrange("p (j e) -> p j e", e=E), hs[:, 0], hs[:, 1], ALU.add))
                    topw.settle()
                    topw.did(dve.tensor_tensor(rows[:, 1, WEIGHT, :], rows[:, 0, WEIGHT, :], gp[:, J:2 * J], ALU.mult))
                    topw.end()

            attention_iterations(dve, body)

            wait_done(dve, place.sem, place.per_turn, B - 1)
            dve.tensor_copy(ends[0:1, :], base[0:1, :]).then_inc(s_ends, 1)
            table.begin(dve, 0)

            def T(i):
                return tab[:, i * E:(i + 1) * E]

            def step(ins):
                table.did(ins)
                table.settle()

            shift = TILE.bit_length() - 1
            assert 1 << shift == TILE
            step(dve.tensor_tensor(T(1), base[:], base0[:], ALU.subtract))
            step(dve.tensor_scalar(tabi[:, 0:E], T(1), float(TILE - 1), None, ALU.add))
            step(dve.tensor_scalar(tabi[:, E:2 * E], tabi[:, 0:E], shift, None, ALU.arith_shift_right))
            step(dve.tensor_copy(T(2), tabi[:, E:2 * E]))
            src, dst = T(2), T(3)
            for s in (1, 2, 4, 8):
                step(dve.tensor_copy(dst[:, 0:s], src[:, 0:s]))
                step(dve.tensor_tensor(dst[:, s:E], src[:, s:E], src[:, 0:E - s], ALU.add))
                src, dst = dst, (T(4) if dst is not None and s in (1, 4) else T(3))
            upto = src
            one = T(7)
            step(dve.tensor_tensor(T(5), upto, tile_no[:, 0:1].broadcast_to([128, E]), ALU.is_le))
            step(dve.tensor_tensor(T(6), T(5), T(2), ALU.mult))
            step(dve.tensor_reduce(one[:, 0:1], T(5), AX, ALU.add))
            step(dve.tensor_reduce(one[:, 1:2], T(6), AX, ALU.add))
            step(dve.tensor_tensor(one[:, 2:3], tile_no[:], upto[:, E - 1:E], ALU.is_lt))
            step(dve.tensor_tensor(one[:, 3:4], tile_no[:], one[:, 1:2], ALU.subtract))
            step(dve.tensor_scalar(one[:, 4:5], one[:, 3:4], float(TILE), float(-PAD_ROW), ALU.mult, ALU.add))
            step(dve.scalar_tensor_tensor(one[:, 5:6], one[:, 0:1], float(CAP), one[:, 4:5], ALU.mult, ALU.add))
            step(dve.tensor_tensor(one[:, 6:7], one[:, 5:6], one[:, 2:3], ALU.mult))
            step(dve.tensor_scalar(tab[:, 0:1], one[:, 6:7], float(PAD_ROW), None, ALU.add))
            step(dve.tensor_scalar(tab[:, 1:2], one[:, 0:1], float(E - 1), float(WP), ALU.min, ALU.mult))
            assert table.k == TABLE_COLUMNS
            dve.wait_ge(s_row, 1)
            step(dve.tensor_copy(where[0:1, :].rearrange("o (t two) -> o two t", two=2), bank[0][0:1, 0:256].rearrange("o (two t) -> o two t", two=2)))
            table.end()

            for q in range(2):
                dve.wait_ge(s_h1kept[q], 16 * (B // 2))

            def tile(x, h, g, y, part, sh, shp):
                def clip(two, t, lo, hi, done):
                    w = wt[:, h.place(RING), :]
                    wait_done(dve, s_hid, 1, h.n)
                    wait_done(dve, s_act, 1, h.n, 2)
                    dve.tensor_scalar(t[0:HID, h.parity, :], psHid[h.parity][0:HID, two * TILE:(two + 1) * TILE], w[0:HID, lo:lo + 1], w[0:HID, hi:hi + 1],
                                      ALU.max, ALU.min).then_inc(done, 1)

                if h:
                    clip(0, hg, G_LO, G_HI, s_clip)
                if g:
                    w = wt[:, g.place(RING), :]
                    gt, ut = hg[0:HID, g.parity, :], hu[0:HID, g.parity, :]
                    wait_done(dve, s_sig, 1, g.n)
                    dve.scalar_tensor_tensor(gt, gt, w[0:HID, B_G:B_G + 1], sg[0:HID, g.parity, :], ALU.add, ALU.mult).then_inc(s_gated, 1)
                if h:
                    clip(1, hu, U_LO, U_HI, s_clipu)
                if g:
                    wait_done(dve, s_gated, 1, g.n)
                    wait_done(dve, s_y, 1, g.n, 2)
                    dve.scalar_tensor_tensor(tt[0:HID, g.parity, :], ut, w[0:HID, U_ADD:U_ADD + 1], gt, ALU.add, ALU.mult).then_inc(s_act, 1)
                if sh and part == 1:
                    wait_done(dve, s_sh_gate, 1, sh.n)
                    wait_done(dve, s_sh_act, 1, sh.n, 1)
                    dve.tensor_scalar(sh_g[0:HID, :], psShG[0:HID, 0:L], shared_pack[0:HID, G_LO:G_LO + 1], shared_pack[0:HID, G_HI:G_HI + 1],
                                      ALU.max, ALU.min).then_inc(s_sh_clip, 1)
                if sh and part == 2:
                    wait_done(dve, s_sh_up, 1, sh.n)
                    wait_done(dve, s_sh_act, 1, sh.n, 1)
                    dve.tensor_scalar(sh_u[0:HID, :], psShU[0:HID, 0:L], shared_pack[0:HID, U_LO:U_LO + 1], shared_pack[0:HID, U_HI:U_HI + 1],
                                      ALU.max, ALU.min).then_inc(s_sh_clipu, 1)
                if sh and part == 3:
                    wait_done(dve, s_sh_sig, 1, sh.n)
                    dve.scalar_tensor_tensor(sh_g[0:HID, :], sh_g[0:HID, :], shared_pack[0:HID, B_G:B_G + 1], sh_s[0:HID, :], ALU.add, ALU.mult).then_inc(s_sh_gated, 1)
                if shp and part == 0:
                    wait_done(dve, s_sh_gated, 1, shp.n)
                    wait_done(dve, s_sh_clipu, 1, shp.n)
                    wait_done(dve, s_sh_z, 1, shp.n, 1)
                    dve.scalar_tensor_tensor(sh_t[0:HID, :], sh_u[0:HID, :], shared_pack[0:HID, U_ADD:U_ADD + 1], sh_g[0:HID, :], ALU.add, ALU.mult).then_inc(s_sh_act, 1)

            tile_iterations(dve, tile)

            def result(b):
                q = b.place(ZRING)
                if b.reuses(ZRING):
                    dve.wait_ge(s_out[q], b.round(ZRING) * 16)
                if b.first == 0:
                    dve.wait_ge(s_sh_kept, B)
                own = bass.ds(b.n * (J * D), J * D)
                dve.tensor_tensor(fin[0:P, q, :], H1[0:P, own], X2T[0:P, own], ALU.add).then_inc(s_own, 1)
                wait_done(dve, s_own, 1, b.n)
                wait_done(dve, s_zz, 1, b.n)
                dve.tensor_tensor(fin[0:P, q, :], fin[0:P, q, :], z[0:P, q, 0], ALU.add).then_inc(s_fin, 1)

            batches(dve, result)

    return nc


_INS = ['x', 'L0_tok_weight1', 'L0_attn_gamma', 'L0_attn_beta', 'L0_attn_wq', 'L0_attn_bq', 'L0_attn_wk', 'L0_attn_bk', 'L0_attn_wv', 'L0_attn_bv',
        'L0_attn_wp', 'L0_attn_bp', 'L0_ffn_gate_w', 'L0_ffn_gate_b', 'L0_ffn_shared_w1', 'L0_ffn_shared_b1', 'L0_ffn_shared_w2', 'L0_ffn_shared_b2',
        'L0_ffn_shared_act', 'L0_ffn_expert_w1', 'L0_ffn_expert_b1', 'L0_ffn_expert_w2', 'L0_ffn_expert_b2', 'L0_ffn_expert_act']


def kernel(**inputs):
    import numpy as _np
    import concourse.bacc as _bacc
    from concourse import mybir as _mybir
    from concourse.bass_utils import run_bass_kernel_spmd as _run

    nc = _bacc.Bacc("TRN2", target_bir_lowering=False, num_devices=1)
    arrays, args = {}, {}
    for name in _INS:
        v = _np.ascontiguousarray(inputs[name])
        arrays[f"in_{name}"] = v
        args[name] = nc.dram_tensor(f"in_{name}", v.shape, _mybir.dt.from_np(v.dtype), kind="ExternalInput").ap()
    b, rows, d = arrays["in_x"].shape
    out = nc.dram_tensor("out", (b, rows // 2, d), _mybir.dt.float32, kind="ExternalOutput").ap()
    audio_tower(nc, args, out)
    r = _run(nc, [arrays], core_ids=[0])
    return r.results[0]["out"]
```
